# Optimizing a Trainium2 kernel written in Bass

```python
import numpy as np
import jax
import jax.numpy as jnp

def _softmax(x, axis=-1):
    return jax.nn.softmax(x, axis=axis)

def _gelu(x):
    return jax.nn.gelu(x, approximate=True)

def _silu(x):
    return jax.nn.silu(x)

def _sigmoid(x):
    return jax.nn.sigmoid(x)

def _layernorm(x, axis=-1, eps=1e-05):
    m = jnp.mean(x, axis=axis, keepdims=True)
    v = jnp.var(x, axis=axis, keepdims=True)
    return (x - m) / jnp.sqrt(v + eps)

def _scatter_add(tgt, idx, src, axis=0):
    return tgt.at[idx].add(src)

def _segment_sum(src, seg, n):
    return jax.ops.segment_sum(src, seg, n)
kernel_name = 'mk_perceiver_d1_seqx_r4_427319'

def setup_inputs(seed: int=0):
    np.random.seed(seed)
    _w = jnp.asarray

    def _rec_inputs():
        import jax
        import jax.numpy as jnp
        _rk = jax.random.key(seed)
        x = -0.0002928 + 1 * jax.random.normal(jax.random.fold_in(_rk, 1), (16, 64, 256), jnp.float32)
        _lenS = 64 - jax.random.randint(jax.random.fold_in(_rk, 7), (16,), 0, max(1, 64 // 4) + 1, jnp.int32)
        _lenS2 = 1601 - jax.random.randint(jax.random.fold_in(_rk, 8), (16,), 0, max(1, 1601 // 4) + 1, jnp.int32)
        _ctx_1024P = jax.random.normal(jax.random.fold_in(_rk, 11), (16, 16, 256), jnp.float32)
        _ctx_1024c = jax.random.dirichlet(jax.random.fold_in(_rk, 511), 0.3 * jnp.ones((16,), jnp.float32), (16, 1601))
        _ctx_1024t = jnp.einsum('bsk,bkd->bsd', _ctx_1024c, _ctx_1024P)
        _ctx_1024t = _ctx_1024t * jax.lax.rsqrt(jnp.mean(jnp.square(_ctx_1024t)) + 1e-12) * 0.953939
        ctx_1024 = -1.39393e-06 + 0.999914 * (_ctx_1024t + 0.3 * jax.random.normal(jax.random.fold_in(_rk, 611), (16, 1601, 256), jnp.float32))
        return (x, ctx_1024)
    x, ctx_1024 = _rec_inputs()

    def _L0_xattn_setup():
        import jax, jax.numpy as jnp
        import numpy as np
        DIM = 256
        DIM_HEAD = 64
        HEADS = 16
        INNER = DIM_HEAD * HEADS

        def _layernorm(x, g, b, eps=1e-05):
            mu = jnp.mean(x, axis=-1, keepdims=True)
            var = jnp.var(x, axis=-1, keepdims=True)
            return (x - mu) * jax.lax.rsqrt(var + eps) * g + b
        key = jax.random.key(seed)
        ks = jax.random.split(key, 8)
        B, Nq, Nk = (2, 512, 512)
        x = jax.random.normal(ks[0], (B, Nq, DIM), dtype=jnp.float32)
        context = jax.random.normal(ks[1], (B, Nk, DIM), dtype=jnp.float32)
        s = 1.0 / np.sqrt(DIM)
        Wq = jax.random.normal(ks[2], (DIM, INNER), dtype=jnp.float32) * s
        Wkv = jax.random.normal(ks[3], (DIM, 2 * INNER), dtype=jnp.float32) * s
        Wo = jax.random.normal(ks[4], (INNER, DIM), dtype=jnp.float32) * (1.0 / np.sqrt(INNER))
        ln_g = jnp.ones((DIM,), dtype=jnp.float32)
        ln_b = jnp.zeros((DIM,), dtype=jnp.float32)
        return {'x': x, 'context': context, 'Wq': Wq, 'Wkv': Wkv, 'Wo': Wo, 'ln_g': ln_g, 'ln_b': ln_b}
    _L0_xattn_all = _L0_xattn_setup()
    _L0_xattn_in = {k: v for k, v in _L0_xattn_all.items() if k in ('Wq', 'Wkv', 'Wo', 'ln_g', 'ln_b')}
    del _L0_xattn_all

    def _L0_attn_setup():
        import jax, jax.numpy as jnp
        import numpy as np
        D_MODEL = 256
        NUM_HEADS = 16
        DK = D_MODEL // NUM_HEADS
        key = jax.random.key(seed)
        kx, kq, kk, kv, ko = jax.random.split(key, 5)
        B, S = (4, 512)
        bound = float(np.sqrt(6.0 / (D_MODEL + D_MODEL)))
        uni = lambda k: jax.random.uniform(k, (D_MODEL, D_MODEL), jnp.float32, -bound, bound)
        return {'x': jax.random.normal(kx, (B, S, D_MODEL), jnp.float32), 'q_heads': uni(kq), 'k_heads': uni(kk), 'v_heads': uni(kv), 'output_proj': uni(ko)}
    _L0_attn_all = _L0_attn_setup()
    _L0_attn_in = {k: v for k, v in _L0_attn_all.items() if k in ('q_heads', 'k_heads', 'v_heads', 'output_proj')}
    del _L0_attn_all

    def _L0_ffn_setup():
        import jax, jax.numpy as jnp
        import numpy as np
        E, H, F, K = (8, 256, 512, 2)
        B, S = (2, 512)
        key = jax.random.key(seed)
        ks = jax.random.split(key, 8)

        def w(k, shape, fan_in):
            return jax.random.normal(k, shape, jnp.float32) / np.float32(np.sqrt(fan_in))
        return {'x': jax.random.normal(ks[0], (B, S, H), jnp.float32), 'Wgate': w(ks[1], (H, E), H), 'bgate': jnp.zeros((E,), jnp.float32), 'W1': w(ks[2], (E, H, F), H), 'b1': jnp.zeros((E, F), jnp.float32), 'W2': w(ks[3], (E, H, F), H), 'b2': jnp.zeros((E, F), jnp.float32), 'Wg': w(ks[4], (E, F, F), F), 'bg': jnp.zeros((E, F), jnp.float32), 'Wl': w(ks[5], (E, F, F), F), 'bl': jnp.zeros((E, F), jnp.float32), 'W3': w(ks[6], (E, F, H), F), 'b3': jnp.zeros((E, H), jnp.float32)}
    _L0_ffn_all = _L0_ffn_setup()
    _L0_ffn_in = {k: v for k, v in _L0_ffn_all.items() if k in ('Wgate', 'bgate', 'W1', 'b1', 'W2', 'b2', 'Wg', 'bg', 'Wl', 'bl', 'W3', 'b3')}
    del _L0_ffn_all
    return {'x': x, 'ctx_1024': ctx_1024, 'L0_xattn_Wq': _L0_xattn_in['Wq'], 'L0_xattn_Wkv': _L0_xattn_in['Wkv'], 'L0_xattn_Wo': _L0_xattn_in['Wo'], 'L0_xattn_ln_g': _L0_xattn_in['ln_g'], 'L0_xattn_ln_b': _L0_xattn_in['ln_b'], 'L0_attn_q_heads': _L0_attn_in['q_heads'], 'L0_attn_k_heads': _L0_attn_in['k_heads'], 'L0_attn_v_heads': _L0_attn_in['v_heads'], 'L0_attn_output_proj': _L0_attn_in['output_proj'], 'L0_ffn_Wgate': _L0_ffn_in['Wgate'], 'L0_ffn_bgate': _L0_ffn_in['bgate'], 'L0_ffn_W1': _L0_ffn_in['W1'], 'L0_ffn_b1': _L0_ffn_in['b1'], 'L0_ffn_W2': _L0_ffn_in['W2'], 'L0_ffn_b2': _L0_ffn_in['b2'], 'L0_ffn_Wg': _L0_ffn_in['Wg'], 'L0_ffn_bg': _L0_ffn_in['bg'], 'L0_ffn_Wl': _L0_ffn_in['Wl'], 'L0_ffn_bl': _L0_ffn_in['bl'], 'L0_ffn_W3': _L0_ffn_in['W3'], 'L0_ffn_b3': _L0_ffn_in['b3']}

def reference(x, ctx_1024, L0_xattn_Wq, L0_xattn_Wkv, L0_xattn_Wo, L0_xattn_ln_g, L0_xattn_ln_b, L0_attn_q_heads, L0_attn_k_heads, L0_attn_v_heads, L0_attn_output_proj, L0_ffn_Wgate, L0_ffn_bgate, L0_ffn_W1, L0_ffn_b1, L0_ffn_W2, L0_ffn_b2, L0_ffn_Wg, L0_ffn_bg, L0_ffn_Wl, L0_ffn_bl, L0_ffn_W3, L0_ffn_b3):
    import jax
    import jax.numpy as jnp

    def _L0_xattn_ref(x, context, Wq, Wkv, Wo, ln_g, ln_b):
        import jax, jax.numpy as jnp
        import numpy as np
        DIM = 256
        DIM_HEAD = 64
        HEADS = 16
        INNER = DIM_HEAD * HEADS

        def _layernorm(x, g, b, eps=1e-05):
            mu = jnp.mean(x, axis=-1, keepdims=True)
            var = jnp.var(x, axis=-1, keepdims=True)
            return (x - mu) * jax.lax.rsqrt(var + eps) * g + b
        B, Nq, _ = x.shape
        scale = DIM_HEAD ** (-0.5)
        ctx = _layernorm(context, ln_g, ln_b)
        q = x @ Wq
        kv = ctx @ Wkv
        k, v = jnp.split(kv, 2, axis=-1)

        def split_heads(t):
            b, n, _ = t.shape
            return t.reshape(b, n, HEADS, DIM_HEAD).transpose(0, 2, 1, 3)
        q, k, v = map(split_heads, (q, k, v))
        sim = jnp.einsum('bhid,bhjd->bhij', q, k) * scale
        attn = jax.nn.softmax(sim, axis=-1)
        out = jnp.einsum('bhij,bhjd->bhid', attn, v)
        out = out.transpose(0, 2, 1, 3).reshape(B, Nq, INNER)
        return out @ Wo

    def _L0_attn_ref(x, q_heads, k_heads, v_heads, output_proj):
        import jax, jax.numpy as jnp
        import numpy as np
        D_MODEL = 256
        NUM_HEADS = 16
        DK = D_MODEL // NUM_HEADS
        B, S, _ = x.shape

        def proj(W):
            return (x @ W.T).reshape(B, S, NUM_HEADS, DK).transpose(0, 2, 1, 3)
        q, k, v = (proj(q_heads), proj(k_heads), proj(v_heads))
        scale = 1.0 / jnp.sqrt(jnp.asarray(DK, x.dtype))
        scores = jnp.einsum('bhqd,bhkd->bhqk', q, k) * scale
        causal = jnp.triu(jnp.ones((S, S), bool), k=1)
        scores = jnp.where(causal, jnp.asarray(-jnp.inf, scores.dtype), scores)
        attn = jax.nn.softmax(scores, axis=-1)
        out = jnp.einsum('bhqk,bhkd->bhqd', attn, v)
        out = out.transpose(0, 2, 1, 3).reshape(B, S, D_MODEL)
        return out @ output_proj.T

    def _L0_ffn_ref(x, Wgate, bgate, W1, b1, W2, b2, Wg, bg, Wl, bl, W3, b3):
        import jax, jax.numpy as jnp
        import numpy as np
        E, H, F, K = (8, 256, 512, 2)
        B, S = (2, 512)
        gout = x @ Wgate + bgate
        topv, topi = jax.lax.top_k(gout, K)
        topw = jax.nn.softmax(topv, axis=-1)
        combine = jnp.sum(jax.nn.one_hot(topi, E, dtype=x.dtype) * topw[..., None], axis=-2)
        x1 = jnp.einsum('bsh,ehf->bsef', x, W1) + b1
        x2 = jnp.einsum('bsh,ehf->bsef', x, W2) + b2
        z = x1 * x2
        g = jnp.einsum('bsef,efg->bseg', z, Wg) + bg
        o = g * jax.nn.sigmoid(g) * (jnp.einsum('bsef,efg->bseg', z, Wl) + bl)
        y = jnp.einsum('bsef,efh->bseh', o, W3) + b3
        return jnp.einsum('bse,bseh->bsh', combine, y)
    x = x + _L0_xattn_ref(_layernorm(x, axis=-1), ctx_1024, L0_xattn_Wq, L0_xattn_Wkv, L0_xattn_Wo, L0_xattn_ln_g, L0_xattn_ln_b)
    x = x + _L0_attn_ref(_layernorm(x, axis=-1), L0_attn_q_heads, L0_attn_k_heads, L0_attn_v_heads, L0_attn_output_proj)
    x = x + _L0_ffn_ref(_layernorm(x, axis=-1), L0_ffn_Wgate, L0_ffn_bgate, L0_ffn_W1, L0_ffn_b1, L0_ffn_W2, L0_ffn_b2, L0_ffn_Wg, L0_ffn_bg, L0_ffn_Wl, L0_ffn_bl, L0_ffn_W3, L0_ffn_b3)
    return x

_drawn_inputs = setup_inputs


def setup_inputs(seed=0):
    import zlib

    import numpy as np

    out = dict(_drawn_inputs(seed))
    spreads = {'L0_xattn_ln_g': (1.0, 0.2),
     'L0_xattn_ln_b': (0.0, 0.1),
     'L0_ffn_bgate': (0.0, 0.1),
     'L0_ffn_b1': (0.0, 0.1),
     'L0_ffn_b2': (0.0, 0.1),
     'L0_ffn_bg': (0.0, 0.1),
     'L0_ffn_bl': (0.0, 0.1),
     'L0_ffn_b3': (0.0, 0.1)}
    factors = {}
    for name, (base, spread) in spreads.items():
        noise = np.random.default_rng([zlib.crc32(name.encode()), seed]).standard_normal(out[name].shape)
        drawn = base * np.exp(spread * noise) if base else spread * noise
        out[name] = jnp.asarray(drawn.astype(out[name].dtype))
    for name, factor in factors.items():
        out[name] = (out[name] * factor).astype(out[name].dtype)
    return out
```

```python
from contextlib import ExitStack

import concourse.bass as bass
from concourse import mybir

F32 = mybir.dt.float32
F32R = mybir.dt.float32r
U32 = mybir.dt.uint32
I32 = mybir.dt.int32
ALU = mybir.AluOpType
ACT = mybir.ActivationFunctionType
AX_X = mybir.AxisListType.X

P = 128
B, NQ, DIM = 16, 64, 256
NK = 1601
HEADS, DH = 16, 64
TOK = B * NQ
TT = TOK // P
DC = DIM // P
PAIRS = HEADS // 2
HALF = TOK // 2
UH = HEADS // 2
UQ = UH * NQ
UNITS = 2 * B
KT = -(-NK // P)
LAST = NK - (KT - 1) * P
EPS = 1e-5
SCALE = DH ** -0.5


def wait(eng, sem, value):
    if isinstance(value, int) and value <= 0:
        return
    eng.wait_ge(sem, value)


def rows(t):
    return LAST if t == KT - 1 else P


class LayerNorm:

    def __init__(self, nc, sb, ps, sem, tag, x, ident, halfpow, split):
        self.nc, self.x, self.ident, self.halfpow, self.split = nc, x, ident, halfpow, split
        self.st = sb(f"{tag}_st", [P, TT, 6], F32)
        self.mv = sb(f"{tag}_mv", [P, TT, 2], F32)
        self.ve = sb(f"{tag}_ve", [P, TT], F32)
        self.rstd = sb(f"{tag}_rstd", [P, TT], F32)
        self.xn = sb(f"{tag}_xn", [P, TT, DIM], F32)
        self.hT = sb(f"{tag}_hT", [P, DC, TOK], F32)
        if split:
            self.hTh = sb(f"{tag}_hTh", [P, DC, TOK], F32R)
            self.hTl = sb(f"{tag}_hTl", [P, DC, TOK], F32R)
        self.ps = ps
        self.stats = sem(f"{tag}_stats")
        self.aggr = sem(f"{tag}_aggr")
        self.veps = sem(f"{tag}_veps")
        self.root = sem(f"{tag}_root")
        self.norm = sem(f"{tag}_norm")
        self.turned = sem(f"{tag}_turned")
        self.copied = sem(f"{tag}_copied")
        self.high = sem(f"{tag}_high")
        self.low = sem(f"{tag}_low")

    def vector_normalise(self, v):
        for i in range(TT):
            v.bn_stats(self.st[:, i, :], self.x[:, i, :]).then_inc(self.stats, 1)
        for i in range(TT):
            v.wait_ge(self.stats, i + 1)
            v.bn_aggr(self.mv[:, i, :], self.st[:, i, :]).then_inc(self.aggr, 1)
        v.wait_ge(self.aggr, TT)
        v.tensor_scalar(self.ve[:, :], self.mv[:, :, 1], EPS, None, ALU.add).then_inc(self.veps, 1)
        v.wait_ge(self.root, 1)
        for i in range(TT):
            v.tensor_scalar(self.xn[:, i, :], self.x[:, i, :], self.mv[:, i, 0:1], self.rstd[:, i:i + 1],
                            ALU.subtract, ALU.mult).then_inc(self.norm, 1)

    def pool_root(self, pool):
        pool.wait_ge(self.veps, 1)
        pool.tensor_tensor(self.rstd[:, :], self.ve[:, :], self.halfpow[:, 0:TT], ALU.pow).then_inc(self.root, 1)

    def tensor_turn(self, pe):
        for th in range(2):
            for c in range(DC):
                for i in range(4):
                    pe.wait_ge(self.norm, 4 * th + i + 1)
                    m = pe.transpose(self.ps[:, 2 * th + c, i * P:(i + 1) * P],
                                     self.xn[:, 4 * th + i, c * P:(c + 1) * P], self.ident[:, :])
                m.then_inc(self.turned, 1)

    def scalar_copy(self, act):
        for th in range(2):
            for c in range(DC):
                act.wait_ge(self.turned, 2 * th + c + 1)
                act.activation(self.hT[:, c, th * HALF:(th + 1) * HALF], self.ps[:, 2 * th + c, :],
                               ACT.Copy).then_inc(self.copied, 1)

    def vector_split(self, v):
        for th in range(2):
            cols = slice(th * HALF, (th + 1) * HALF)
            v.wait_ge(self.copied, 2 * th + 2)
            v.tensor_copy(self.hTh[:, :, cols], self.hT[:, :, cols]).then_inc(self.high, 1)
            v.wait_ge(self.high, th + 1)
            v.tensor_tensor(self.hTl[:, :, cols], self.hT[:, :, cols], self.hTh[:, :, cols].bitcast(F32),
                            ALU.subtract).then_inc(self.low, 1)


def three_passes(pe, out, wh, wl, mh, ml, first, last, **more):
    pe.matmul(out, wl, mh, start=first, stop=False, **more)
    pe.matmul(out, wh, ml, start=False, stop=False, **more)
    return pe.matmul(out, wh, mh, start=False, stop=last, **more)


def constants(nc, ident, ones, halfpow, res_x, x, zeroed, made, x_in):
    with nc.Block() as block:
        @block.gpsimd
        def _(pool):
            pool.memset(ident[:, :], 0.0).then_inc(zeroed, 1)
            pool.memset(ones[:, :], 1.0).then_inc(made, 1)
            pool.memset(halfpow[:, :], -0.5).then_inc(made, 1)
            pool.wait_ge(zeroed, 1)
            pool.affine_select(out=ident[:, :], in_=ident[:, :], compare_op=ALU.not_equal, fill=1.0, base=0,
                               pattern=[[-1, P]], channel_multiplier=1).then_inc(made, 1)
            pool.wait_ge(made, 3)

        @block.sync
        def _(sp):
            sp.dma_start(res_x[:, :, :], x.rearrange("b q d -> (b q) d").rearrange("(i p) d -> p i d", p=P)
                         ).then_inc(x_in, 16)
            sp.wait_ge(x_in, 16)


def collecting(nc, ctx, kept):
    def sem(name):
        kept.append(ctx.enter_context(nc.semaphore(name)))
        return kept[-1]
    return sem


def clear(pool, spent):
    for s in spent:
        pool.sem_clear(s)


def queries(nc, res_x, ident, halfpow, Wq, WkT, QT, spent):
    with ExitStack() as ctx:
        sb = lambda n, s, d: ctx.enter_context(nc.sbuf_tensor(n, s, d))
        sem = collecting(nc, ctx, spent)
        bank = ctx.enter_context(nc.psum_tensor("q_banks", [P, 8, HALF], F32))
        ln = LayerNorm(nc, sb, bank[:, 0:4, :], sem, "ln1", res_x, ident, halfpow, True)
        wq = sb("wq", [P, DC, HEADS * DH], F32)
        wqh = sb("wqh", [P, DC, HEADS * DH], F32R)
        wql = sb("wql", [P, DC, HEADS * DH], F32R)
        wk = sb("wk", [P, PAIRS, DIM], F32)
        wkh = sb("wkh", [P, PAIRS, 2, DIM], F32R)
        wkl = sb("wkl", [P, PAIRS, 2, DIM], F32R)
        qf = sb("qf", [P, 2, TOK], F32)
        qh = sb("qh", [P, 2, TOK], F32R)
        ql = sb("ql", [P, 2, TOK], F32R)
        stage = sb("stage", [P, 2, 2, DC, B // 2, 2, NQ], F32)

        wq_in, wk_in = sem("wq_in"), sem("wk_in")
        wq_high, wq_low = sem("wq_high"), sem("wq_low")
        wk_zero, wk_high, wk_low = sem("wk_zero"), sem("wk_high"), sem("wk_low")
        q_made, q_copied, q_high, q_low = sem("q_made"), sem("q_copied"), sem("q_high"), sem("q_low")
        k_made, k_act, k_dve = sem("k_made"), sem("k_act"), sem("k_dve")
        stored = [sem("stored0"), sem("stored1")]
        pieces = [(th, hh, c) for th in range(2) for hh in range(2) for c in range(DC)]

        with nc.Block() as block:
            @block.sync
            def _(sp):
                sp.dma_start(wq[:, :, :], Wq.rearrange("(c p) n -> p c n", p=P)).then_inc(wq_in, 16)
                sp.dma_start(wk[:, :, :], WkT.rearrange("(j p) d -> p j d", p=P)).then_inc(wk_in, 16)
                for p in range(PAIRS):
                    hf, k = p // (PAIRS // 2), p % (PAIRS // 2)
                    for th in range(2):
                        sp.wait_ge(k_act, 4 * p + 2 * (th + 1))
                        sp.wait_ge(k_dve, 4 * p + 2 * (th + 1))
                        for c in range(DC):
                            dst = QT[th * B // 2:(th + 1) * B // 2, hf, :, c, 2 * k:2 * k + 2, :]
                            sp.dma_start(dst.rearrange("b p h t -> p b (h t)"),
                                         stage[:, p % 2, th, c].rearrange("p b h t -> p b (h t)")
                                         ).then_inc(stored[p % 2], 16)
                for s in stored:
                    sp.wait_ge(s, 16 * 4 * PAIRS // 2)

            @block.gpsimd
            def _(pool):
                pool.memset(wkh[:, :, :, :].bitcast(F32), 0.0).then_inc(wk_zero, 1)
                pool.memset(wkl[:, :, :, :].bitcast(F32), 0.0).then_inc(wk_zero, 1)
                ln.pool_root(pool)
                pool.wait_ge(wq_high, 1)
                pool.tensor_tensor(wql[:, :, :], wq[:, :, :], wqh[:, :, :].bitcast(F32), ALU.subtract
                                   ).then_inc(wq_low, 1)

            @block.tensor
            def _(pe):
                ln.tensor_turn(pe)

                def project(p):
                    for th in range(2):
                        if p >= 1:
                            pe.wait_ge(q_copied, 2 * (p - 1) + th + 1)
                        for c in range(DC):
                            w = slice(p * P, (p + 1) * P)
                            t = slice(th * HALF, (th + 1) * HALF)
                            m = three_passes(pe, bank[:, 4 + th, :], wqh[:, c, w], wql[:, c, w],
                                             ln.hTh[:, c, t], ln.hTl[:, c, t], c == 0, c == DC - 1)
                        m.then_inc(q_made, 1)

                pe.wait_ge(wq_low, 1)
                pe.wait_ge(ln.low, 2)
                project(0)
                pe.wait_ge(wk_low, 2)
                for p in range(PAIRS):
                    if p + 1 < PAIRS:
                        project(p + 1)
                    pe.wait_ge(q_low, p + 1)
                    for n, (th, hh, c) in enumerate(pieces):
                        g = len(pieces) * p + n
                        if g >= 4:
                            pe.wait_ge(k_act if g % 2 == 0 else k_dve, (g - 4) // 2 + 1)
                        t = slice(th * HALF, (th + 1) * HALF)
                        w = slice(c * P, (c + 1) * P)
                        three_passes(pe, bank[:, g % 4, :], wkh[:, p, hh, w], wkl[:, p, hh, w],
                                     qh[:, p % 2, t], ql[:, p % 2, t], True, True).then_inc(k_made, 1)

            def take(eng, copy, p, parity, mine):
                for n, (th, hh, c) in enumerate(pieces):
                    if n % 2 != parity:
                        continue
                    g = len(pieces) * p + n
                    eng.wait_ge(k_made, g + 1)
                    if p >= 2:
                        eng.wait_ge(stored[p % 2], 64 * (p // 2))
                    copy(stage[:, p % 2, th, c, :, hh, :],
                         bank[:, g % 4, :].rearrange("p (b t) -> p b t", t=NQ)).then_inc(mine, 1)

            @block.scalar
            def _(act):
                ln.scalar_copy(act)

                def copy_q(p):
                    for th in range(2):
                        act.wait_ge(q_made, 2 * p + th + 1)
                        if p >= 2:
                            act.wait_ge(q_low, p - 1)
                        act.activation(qf[:, p % 2, th * HALF:(th + 1) * HALF], bank[:, 4 + th, :],
                                       ACT.Copy).then_inc(q_copied, 1)

                copy_q(0)
                for p in range(PAIRS):
                    if p + 1 < PAIRS:
                        copy_q(p + 1)
                    take(act, lambda o, i: act.activation(o, i, ACT.Copy), p, 0, k_act)

            @block.vector
            def _(v):
                ln.vector_normalise(v)
                v.wait_ge(wq_in, 16)
                v.tensor_copy(wqh[:, :, :], wq[:, :, :]).then_inc(wq_high, 1)
                ln.vector_split(v)
                v.wait_ge(wk_in, 16)
                v.wait_ge(wk_zero, 2)

                def split_q(p):
                    v.wait_ge(q_copied, 2 * p + 2)
                    if p >= 2:
                        v.wait_ge(k_made, len(pieces) * (p - 1))
                    v.tensor_copy(qh[:, p % 2, :], qf[:, p % 2, :]).then_inc(q_high, 1)
                    v.wait_ge(q_high, p + 1)
                    v.tensor_tensor(ql[:, p % 2, :], qf[:, p % 2, :], qh[:, p % 2, :].bitcast(F32),
                                    ALU.subtract).then_inc(q_low, 1)

                for hh in range(2):
                    r = slice(hh * DH, (hh + 1) * DH)
                    v.tensor_copy(wkh[r, :, hh, :], wk[r, :, :]).then_inc(wk_high, 1)
                split_q(0)
                for hh in range(2):
                    r = slice(hh * DH, (hh + 1) * DH)
                    v.wait_ge(wk_high, hh + 1)
                    v.tensor_tensor(wkl[r, :, hh, :], wk[r, :, :], wkh[r, :, hh, :].bitcast(F32),
                                    ALU.subtract).then_inc(wk_low, 1)
                for p in range(PAIRS):
                    if p + 1 < PAIRS:
                        split_q(p + 1)
                    take(v, v.tensor_copy, p, 1, k_dve)


SLOTS = 2 * KT
LAG = KT + 8
RING = 5


def ring(t):
    return RING - 1 if t == KT - 1 else t % (RING - 1)


class Step:

    def __init__(self, r, c):
        self.r, self.c = r, c

    def back(self, n):
        c = self.c - n
        r = self.r + c // SLOTS
        c = c % SLOTS
        if isinstance(r, int) and not 0 <= r < B:
            return None
        return r, c // KT, c % KT

    def unit(self, start):
        c = self.c - start
        if c % KT:
            return None
        r = self.r + c // SLOTS
        if isinstance(r, int) and not 0 <= r < B:
            return None
        return r, c % SLOTS // KT

    def batch(self, at):
        c = self.c - at
        n = self.r + c // SLOTS
        return [n] if c % SLOTS == 0 and (not isinstance(n, int) or 0 <= n < B) else []

    def context(self, at):
        found = []
        for t in range(KT):
            c = self.c - at(t)
            if c % SLOTS == 0:
                n = self.r + c // SLOTS
                if not isinstance(n, int) or 0 <= n < B:
                    found.append((n, t))
        return found


def clock(eng, step):
    for c in range(-2 * SLOTS, 2 * SLOTS):
        step(Step(0, c))
    with eng.Fori(2, B - 2) as r:
        for c in range(SLOTS):
            step(Step(r, c))
    for c in range(4 * SLOTS):
        step(Step(B - 2, c))


def spread(start):
    return lambda t: start + 5 * t // 3


def attend(nc, ident, ones, ctx_in, ln_g, ln_b, QT, OT, earlier, spent):
    with ExitStack() as ctx:
        sb = lambda n, s, d: ctx.enter_context(nc.sbuf_tensor(n, s, d))
        ps = lambda n, s: ctx.enter_context(nc.psum_tensor(n, s, F32))
        sem = collecting(nc, ctx, spent)
        raw = sb("raw", [P, KT, DIM], F32)
        nrm = sb("nrm", [P, KT, DIM], F32)
        ch = sb("ch", [P, KT, DIM], F32R)
        cl = sb("cl", [P, KT, DIM], F32R)
        tf = sb("tf", [P, 3, DC, P], F32)
        th = sb("th", [P, KT, DC, P], F32R)
        tl = sb("tl", [P, KT, DC, P], F32R)
        st = sb("st", [P, KT, 6], F32)
        msum, mdif, vsum = sb("msum", [P, KT], F32), sb("mdif", [P, KT], F32), sb("vsum", [P, KT], F32)
        ve = sb("ve", [P, KT], F32)
        negmu = sb("negmu", [P, KT], F32)
        rstd = sb("rstd", [P, KT], F32)
        shift = sb("shift", [P, KT], F32)
        half13 = sb("half13", [P, KT], F32)
        gain = sb("gain", [P, DC], F32)
        bias = sb("bias", [P, DC], F32)
        qr = sb("qr", [P, DC, UQ], F32)
        qh = sb("qsh", [P, 2, DC, UQ], F32R)
        ql = sb("qsl", [P, 2, DC, UQ], F32R)
        s = sb("s", [P, 2, KT, UQ], F32)
        ph = sb("ph", [P, RING, UQ], F32R)
        pl = sb("pl", [P, RING, UQ], F32R)
        top = sb("top", [P, UQ], F32)
        mcol = sb("mcol", [P, 4], F32)
        most = sb("most", [P, 2, UQ], F32)
        total = sb("total", [P, 2, UQ], F32)
        icol = sb("icol", [P, 4], F32)
        inv = sb("inv", [P, UQ], F32)
        o = sb("o", [P, 2, DC, UQ], F32)
        score = ps("score", [P, 2, UQ])
        acc = ps("acc", [P, 2, DC, UQ])
        turn = ps("turn", [P, DC, P])
        misc = ps("misc", [P, 4, P])

        raw_in = [sem(f"raw_in{t}") for t in range(KT)]
        gb_in, q_in = sem("gb_in"), sem("q_in")
        o_out = [sem("o_out0"), sem("o_out1")]
        c_zero, c_exp = sem("c_zero"), sem("c_exp")
        c_stats, c_mom, c_ve, c_rstd, c_shift = sem("c_stats"), sem("c_mom"), sem("c_ve"), sem("c_rstd"), sem("c_shift")
        c_norm, c_turn, c_gain = sem("c_norm"), sem("c_turn"), sem("c_gain")
        t_high, t_low, r_high, r_low = sem("t_high"), sem("t_low"), sem("r_high"), sem("r_low")
        q_high, q_low = sem("qs_high"), sem("qs_low")
        scored, copied, maxed = sem("scored"), sem("copied"), sem("maxed")
        top_turned, top_col, top_spread, top_row = sem("top_turned"), sem("top_col"), sem("top_spread"), sem("top_row")
        shifted, expd, p_high, p_low, summed = sem("shifted"), sem("expd"), sem("p_high"), sem("p_low"), sem("summed")
        multiplied, sum_col, inverted, inv_spread, inv_row, scaled, biased = (
            sem("multiplied"), sem("sum_col"), sem("inverted"), sem("inv_spread"), sem("inv_row"), sem("scaled"),
            sem("biased"))

        slot = lambda r, u, t: SLOTS * r + KT * u + t
        unit = lambda r, u: 2 * r + u
        tile = lambda n, t: KT * n + t
        at_norm, at_turn, at_split = spread(-12), spread(-11), spread(-10)
        at_raw = lambda t: spread(-11)(t) - SLOTS
        at_stats = lambda t: t - 27
        at_root = -14
        at_rows = spread(LAG - KT + 1)

        with nc.Block() as block:
            @block.sync
            def _(sp):
                sp.dma_start(gain[:, :], ln_g).then_inc(gb_in, 16)
                sp.dma_start(bias[:, :], ln_b).then_inc(gb_in, 16)

                def step(k):
                    for n, t in k.context(at_raw):
                        wait(sp, c_norm, tile(n - 1, t) + 1)
                        sp.dma_start(raw[0:rows(t), t, :], ctx_in[n, t * P:t * P + rows(t), :]
                                     ).then_inc(raw_in[t], 16)
                    if (f := k.unit(-9)):
                        r, u = f
                        wait(sp, q_low, unit(r, u))
                        sp.dma_start(qr[:, :, :], QT[r, u].rearrange("p c h t -> p c (h t)")).then_inc(q_in, 16)
                    if (f := k.unit(KT + LAG + 5)):
                        r, u = f
                        sp.wait_ge(biased, DC * (unit(r, u) + 1))
                        sp.dma_start(OT[r, u].rearrange("p c h t -> p c (h t)"), o[:, u]).then_inc(o_out[u], 16)

                clock(sp, step)
                for u in range(2):
                    sp.wait_ge(o_out[u], 16 * B)

            @block.gpsimd
            def _(pool):
                clear(pool, earlier)
                pool.memset(st[:, :, :], 0.0).then_inc(c_zero, 1)
                pool.memset(half13[:, :], -0.5).then_inc(c_exp, 1)

                def step(k):
                    for n in k.batch(at_root):
                        pool.wait_ge(c_ve, 2 * (n + 1))
                        if isinstance(n, int) and n == 0:
                            pool.wait_ge(c_exp, 1)
                        wait(pool, c_norm, KT * n)
                        pool.tensor_tensor(rstd[:, :], ve[:, :], half13[:, :], ALU.pow).then_inc(c_rstd, 1)
                        pool.wait_ge(c_rstd, n + 1)
                        pool.tensor_tensor(shift[:, :], negmu[:, :], rstd[:, :], ALU.mult).then_inc(c_shift, 1)
                    if (f := k.unit(-5)):
                        r, u = f
                        pool.wait_ge(q_high, unit(r, u) + 1)
                        pool.tensor_tensor(ql[:, u], qr[:, :, :], qh[:, u].bitcast(F32), ALU.subtract
                                           ).then_inc(q_low, 1)
                    for n, t in k.context(at_split):
                        pool.wait_ge(t_high, tile(n, t) + 1)
                        pool.tensor_tensor(tl[:, t, :, 0:rows(t)], tf[:, 2 if t == KT - 1 else t % 2, :, 0:rows(t)],
                                           th[:, t, :, 0:rows(t)].bitcast(F32), ALU.subtract).then_inc(t_low, 1)
                    for n, t in k.context(at_rows):
                        pool.wait_ge(r_high, tile(n, t) + 1)
                        pool.tensor_tensor(cl[0:rows(t), t, :], nrm[0:rows(t), t, :],
                                           ch[0:rows(t), t, :].bitcast(F32), ALU.subtract).then_inc(r_low, 1)
                    if (f := k.back(LAG - 2)):
                        r, u, t = f
                        if t == 1:
                            wait(pool, sum_col, unit(r, u) - 1)
                            pool.wait_ge(expd, slot(r, u, t) + 1)
                            pool.tensor_tensor(total[:, u, :], s[:, u, 0, :], s[:, u, 1, :], ALU.add).then_inc(summed, 1)
                        elif t > 1:
                            pool.wait_ge(expd, slot(r, u, t) + 1)
                            pool.wait_ge(summed, (KT - 1) * unit(r, u) + t - 1)
                            pool.tensor_tensor(total[0:rows(t), u, :], total[0:rows(t), u, :], s[0:rows(t), u, t, :],
                                               ALU.add).then_inc(summed, 1)

                clock(pool, step)

            @block.tensor
            def _(pe):
                def step(k):
                    if (f := k.back(0)):
                        r, u, t = f
                        if t == 0:
                            pe.wait_ge(q_low, unit(r, u) + 1)
                        if u == 0:
                            pe.wait_ge(t_low, tile(r, t) + 1)
                        wait(pe, copied, slot(r, u, t) - 1)
                        for c in range(DC):
                            m = three_passes(pe, score[0:rows(t), slot(0, u, t) % 2, :], th[:, t, c, 0:rows(t)],
                                             tl[:, t, c, 0:rows(t)], qh[:, u, c, :], ql[:, u, c, :],
                                             c == 0, c == DC - 1)
                        m.then_inc(scored, 1)
                    for n, t in k.context(at_turn):
                        pe.wait_ge(c_norm, tile(n, t) + 1)
                        wait(pe, c_gain, DC * tile(n, t))
                        for c in range(DC):
                            m = pe.transpose(turn[:, c, 0:rows(t)], nrm[0:rows(t), t, c * P:(c + 1) * P],
                                             ident[0:rows(t), 0:rows(t)])
                        m.then_inc(c_turn, 1)
                    if (f := k.back(LAG)):
                        r, u, t = f
                        if t == 0:
                            wait(pe, scaled, DC * (unit(r, u) - 1))
                        if u == 0:
                            pe.wait_ge(r_low, tile(r, t) + 1)
                        pe.wait_ge(p_low, slot(r, u, t) + 1)
                        n = rows(t)
                        for c in range(DC):
                            w = slice(c * P, (c + 1) * P)
                            m = three_passes(pe, acc[:, u, c, :], ch[0:n, t, w], cl[0:n, t, w],
                                             ph[0:n, ring(t), :], pl[0:n, ring(t), :], t == 0, t == KT - 1)
                        m.then_inc(multiplied, 1)
                    if (f := k.unit(KT + 1)):
                        r, u = f
                        pe.wait_ge(maxed, (KT - 1) * (unit(r, u) + 1))
                        wait(pe, inv_row, unit(r, u) - 2)
                        for q in range(4):
                            m = pe.transpose(misc[:, q, :], top[:, q * P:(q + 1) * P], ident[:, :])
                        m.then_inc(top_turned, 1)
                    if (f := k.unit(KT + 2)):
                        r, u = f
                        pe.wait_ge(top_col, unit(r, u) + 1)
                        for q in range(4):
                            m = pe.matmul(misc[:, q, :], mcol[:, q:q + 1].broadcast_to([P, P]), ident[:, :],
                                          start=True, stop=True)
                        m.then_inc(top_spread, 1)
                    if (f := k.unit(KT + LAG)):
                        r, u = f
                        pe.wait_ge(summed, (KT - 1) * (unit(r, u) + 1))
                        ahead = unit(r, u) + 2
                        pe.wait_ge(top_row, min(ahead, UNITS) if isinstance(r, int) else ahead)
                        for q in range(4):
                            m = pe.matmul(misc[:, 0, q:q + 1], total[:, u, q * P:(q + 1) * P], ones[:, 0:1],
                                          start=True, stop=True)
                        m.then_inc(sum_col, 1)
                    if (f := k.unit(KT + LAG + 1)):
                        r, u = f
                        pe.wait_ge(inverted, unit(r, u) + 1)
                        for q in range(4):
                            m = pe.matmul(misc[:, q, :], icol[:, q:q + 1].broadcast_to([P, P]), ident[:, :],
                                          start=True, stop=True)
                        m.then_inc(inv_spread, 1)

                clock(pe, step)

            @block.scalar
            def _(act):
                def step(k):
                    if (f := k.unit(KT + 3)):
                        r, u = f
                        act.wait_ge(top_spread, unit(r, u) + 1)
                        wait(act, shifted, KT * (unit(r, u) - 1))
                        act.activation(most[:, u, :], misc[:, :, :], ACT.Copy).then_inc(top_row, 1)
                    if (f := k.back(LAG - 2)):
                        r, u, t = f
                        n = rows(t)
                        act.wait_ge(expd, slot(r, u, t) + 1)
                        wait(act, multiplied, slot(r, u, t) - (RING - 2))
                        act.activation(ph[0:n, ring(t), :], s[0:n, u, t, :], ACT.Copy).then_inc(p_high, 1)
                    if (f := k.back(LAG - 3)):
                        r, u, t = f
                        n = rows(t)
                        act.wait_ge(shifted, slot(r, u, t) + 1)
                        act.activation(s[0:n, u, t, :], s[0:n, u, t, :], ACT.Exp, scale=SCALE).then_inc(expd, 1)
                    for n, t in k.context(at_norm):
                        act.wait_ge(c_shift, n + 1)
                        wait(act, r_low, tile(n - 1, t) + 1)
                        wait(act, c_turn, tile(n - 1, t) + 1)
                        m = rows(t)
                        act.activation(nrm[0:m, t, :], raw[0:m, t, :], ACT.Identity, bias=shift[0:m, t:t + 1],
                                       scale=rstd[0:m, t:t + 1]).then_inc(c_norm, 1)
                    if (f := k.back(0)):
                        r, u, t = f
                        n = rows(t)
                        act.wait_ge(scored, slot(r, u, t) + 1)
                        wait(act, p_low, slot(r - 1, u, t) + 1)
                        if t:
                            wait(act, summed, (KT - 1) * unit(r - 1, u) + t)
                        else:
                            wait(act, summed, (KT - 1) * unit(r - 1, u) + 1)
                        act.activation(s[0:n, u, t, :], score[0:n, slot(0, u, t) % 2, :], ACT.Copy
                                       ).then_inc(copied, 1)
                    for n, t in k.context(at_turn):
                        act.wait_ge(c_turn, tile(n, t) + 1)
                        if isinstance(n, int) and n == 0:
                            act.wait_ge(gb_in, 32)
                        wait(act, t_low, tile(n, t) - 1)
                        m = rows(t)
                        for c in range(DC):
                            act.activation(tf[:, 2 if t == KT - 1 else t % 2, c, 0:m], turn[:, c, 0:m], ACT.Identity,
                                           bias=bias[:, c:c + 1], scale=gain[:, c:c + 1]).then_inc(c_gain, 1)
                    if (f := k.unit(KT + LAG + 2)):
                        r, u = f
                        act.wait_ge(inv_spread, unit(r, u) + 1)
                        wait(act, scaled, DC * unit(r, u))
                        act.activation(inv[:, :], misc[:, :, :], ACT.Copy).then_inc(inv_row, 1)
                    if (f := k.unit(KT + LAG + 4)):
                        r, u = f
                        for c in range(DC):
                            act.wait_ge(scaled, DC * unit(r, u) + c + 1)
                            act.activation(o[:, u, c, :], o[:, u, c, :], ACT.Identity, bias=bias[:, c:c + 1],
                                           scale=gain[:, c:c + 1]).then_inc(biased, 1)

                clock(act, step)

            @block.vector
            def _(v):
                def step(k):
                    if (f := k.unit(KT + 2)):
                        r, u = f
                        v.wait_ge(top_turned, unit(r, u) + 1)
                        wait(v, top_spread, unit(r, u))
                        v.tensor_reduce(mcol[:, :], misc[:, :, :], AX_X, ALU.max).then_inc(top_col, 1)
                    if (f := k.back(LAG - 4)):
                        r, u, t = f
                        n = rows(t)
                        if t == 0:
                            v.wait_ge(top_row, unit(r, u) + 1)
                        v.tensor_tensor(s[0:n, u, t, :], s[0:n, u, t, :], most[0:n, u, :], ALU.subtract
                                        ).then_inc(shifted, 1)
                    if (f := k.back(LAG - 1)):
                        r, u, t = f
                        n = rows(t)
                        v.wait_ge(p_high, slot(r, u, t) + 1)
                        v.tensor_tensor(pl[0:n, ring(t), :], s[0:n, u, t, :], ph[0:n, ring(t), :].bitcast(F32),
                                        ALU.subtract).then_inc(p_low, 1)
                    if (f := k.back(1)):
                        r, u, t = f
                        n = rows(t)
                        if t == 1:
                            wait(v, top_turned, unit(r, u))
                            v.wait_ge(copied, slot(r, u, t) + 1)
                            v.tensor_tensor(top[:, :], s[:, u, 0, :], s[:, u, 1, :], ALU.max).then_inc(maxed, 1)
                        elif t > 1:
                            v.wait_ge(copied, slot(r, u, t) + 1)
                            v.wait_ge(maxed, (KT - 1) * unit(r, u) + t - 1)
                            v.tensor_tensor(top[0:n, :], top[0:n, :], s[0:n, u, t, :], ALU.max).then_inc(maxed, 1)
                    if (f := k.unit(-5)):
                        r, u = f
                        v.wait_ge(q_in, 16 * (unit(r, u) + 1))
                        wait(v, scored, KT * (unit(r, u) - 1))
                        v.tensor_copy(qh[:, u], qr[:, :, :]).then_inc(q_high, 1)
                    for n, t in k.context(at_stats):
                        m = rows(t)
                        v.wait_ge(raw_in[t], 16 * (n + 1))
                        if isinstance(n, int) and n == 0 and t == 0:
                            v.wait_ge(c_zero, 1)
                        wait(v, c_ve, 2 * n)
                        v.bn_stats(st[0:m, t, :], raw[0:m, t, :]).then_inc(c_stats, 1)
                    for n in k.batch(at_root):
                        v.wait_ge(c_stats, KT * (n + 1))
                        v.tensor_tensor(msum[:, :], st[:, :, 1], st[:, :, 4], ALU.add).then_inc(c_mom, 1)
                        v.tensor_tensor(mdif[:, :], st[:, :, 1], st[:, :, 4], ALU.subtract).then_inc(c_mom, 1)
                        v.tensor_tensor(vsum[:, :], st[:, :, 2], st[:, :, 5], ALU.add).then_inc(c_mom, 1)
                        v.wait_ge(c_mom, 5 * n + 3)
                        v.tensor_scalar(negmu[:, :], msum[:, :], -0.5, None, ALU.mult).then_inc(c_ve, 1)
                        v.tensor_tensor(mdif[:, :], mdif[:, :], mdif[:, :], ALU.mult).then_inc(c_mom, 1)
                        v.tensor_scalar(vsum[:, :], vsum[:, :], 1.0 / DIM, EPS, ALU.mult, ALU.add).then_inc(c_mom, 1)
                        v.wait_ge(c_mom, 5 * n + 5)
                        v.scalar_tensor_tensor(out=ve[:, :], in0=mdif[:, :], scalar=0.25, in1=vsum[:, :],
                                               op0=ALU.mult, op1=ALU.add).then_inc(c_ve, 1)
                    for n, t in k.context(at_split):
                        m = rows(t)
                        v.wait_ge(c_gain, DC * (tile(n, t) + 1))
                        wait(v, scored, slot(n - 1, 1, t) + 1)
                        v.tensor_copy(th[:, t, :, 0:m], tf[:, 2 if t == KT - 1 else t % 2, :, 0:m]).then_inc(t_high, 1)
                    for n, t in k.context(at_rows):
                        m = rows(t)
                        v.wait_ge(c_norm, tile(n, t) + 1)
                        wait(v, multiplied, slot(n - 1, 1, t) + 1)
                        v.tensor_copy(ch[0:m, t, :], nrm[0:m, t, :]).then_inc(r_high, 1)
                    if (f := k.unit(KT + LAG + 1)):
                        r, u = f
                        v.wait_ge(sum_col, unit(r, u) + 1)
                        wait(v, inv_spread, unit(r, u))
                        v.reciprocal(icol[:, :], misc[:, 0, 0:4]).then_inc(inverted, 1)
                    if (f := k.unit(KT + LAG + 3)):
                        r, u = f
                        v.wait_ge(inv_row, unit(r, u) + 1)
                        v.wait_ge(multiplied, KT * (unit(r, u) + 1))
                        wait(v, o_out[u], 16 * r)
                        for c in range(DC):
                            v.tensor_tensor(o[:, u, c, :], acc[:, u, c, :], inv[:, :], ALU.mult).then_inc(scaled, 1)

                clock(v, step)


def project_out(nc, res_x, Wv, Wo, OT, earlier):
    with ExitStack() as ctx:
        sb = lambda n, s, d: ctx.enter_context(nc.sbuf_tensor(n, s, d))
        ps = lambda n, s: ctx.enter_context(nc.psum_tensor(n, s, F32))
        sem = lambda n: ctx.enter_context(nc.semaphore(n))
        wv = sb("wv", [P, DC, HEADS, DH], F32)
        wvh = sb("wvh", [P, DC, HEADS, P], F32R)
        wvl = sb("wvl", [P, DC, HEADS, P], F32R)
        wo = sb("wo", [P, PAIRS, DIM], F32)
        woh = sb("woh", [P, PAIRS, DIM], F32R)
        wol = sb("wol", [P, PAIRS, DIM], F32R)
        at = sb("at", [P, 2, 2, DC, B // 2, 2 * NQ], F32)
        ath = sb("ath", [P, 2, 2, DC, B // 2, 2 * NQ], F32R)
        atl = sb("atl", [P, 2, 2, DC, B // 2, 2 * NQ], F32R)
        vf = sb("vf", [P, 2, TOK], F32)
        vh = sb("vh", [P, 2, TOK], F32R)
        vl = sb("vl", [P, 2, TOK], F32R)
        pv = ps("pv", [P, 2, HALF])
        po = ps("po", [P, TT, DIM])
        w_in, w_zero, wv_high, wv_low, wo_high, wo_low = (sem("w_in"), sem("w_zero"), sem("wv_high"), sem("wv_low"),
                                                          sem("wo_high"), sem("wo_low"))
        at_in = [[sem(f"at_in{a}{b}") for b in range(2)] for a in range(2)]
        at_high, at_low = sem("at_high"), sem("at_low")
        v_made, v_copied, v_high, v_low, out_made, added = (sem("v_made"), sem("v_copied"), sem("v_high"),
                                                            sem("v_low"), sem("out_made"), sem("added"))
        out_used = sem("out_used")

        with nc.Block() as block:
            @block.sync
            def _(sp):
                sp.dma_start(wv[:, :, :, :], Wv.rearrange("(c p) (h d) -> p c h d", p=P, d=DH)).then_inc(w_in, 16)
                for p in range(PAIRS):
                    hf, k = p // (PAIRS // 2), p % (PAIRS // 2)
                    for t in range(2):
                        if p >= 2:
                            sp.wait_ge(at_low, 2 * (p - 2) + t + 1)
                        for c in range(DC):
                            src = OT[t * B // 2:(t + 1) * B // 2, hf, :, c, 2 * k:2 * k + 2, :]
                            sp.dma_start(at[:, p % 2, t, c], src.rearrange("b p h t -> p b (h t)")
                                         ).then_inc(at_in[p % 2][t], 16)
                    if p == 0:
                        sp.dma_start(wo[:, :, :], Wo.rearrange("(j p) d -> p j d", p=P)).then_inc(wo_high, 16)

            @block.gpsimd
            def _(pool):
                pool.memset(wvh[:, :, :, :].bitcast(F32), 0.0).then_inc(w_zero, 1)
                pool.memset(wvl[:, :, :, :].bitcast(F32), 0.0).then_inc(w_zero, 1)
                clear(pool, earlier)
            @block.tensor
            def _(pe):
                def values(p):
                    for t in range(2):
                        if p >= 1:
                            pe.wait_ge(v_copied, 2 * (p - 1) + t + 1)
                        pe.wait_ge(at_low, 2 * p + t + 1)
                        for hh in range(2):
                            for c in range(DC):
                                m = three_passes(pe, pv[:, t, :], wvh[:, c, 2 * p + hh, :], wvl[:, c, 2 * p + hh, :],
                                                 ath[:, p % 2, t, c, :, hh * NQ:(hh + 1) * NQ],
                                                 atl[:, p % 2, t, c, :, hh * NQ:(hh + 1) * NQ],
                                                 hh == 0 and c == 0, hh == 1 and c == DC - 1)
                        m.then_inc(v_made, 1)

                pe.wait_ge(wv_low, 2)
                values(0)
                pe.wait_ge(wo_low, 1)
                for p in range(PAIRS):
                    if p + 1 < PAIRS:
                        values(p + 1)
                    pe.wait_ge(v_low, p + 1)
                    for i in range(TT):
                        w = slice(i * P, (i + 1) * P)
                        m = three_passes(pe, po[:, i, :], vh[:, p % 2, w], vl[:, p % 2, w], woh[:, p, :], wol[:, p, :],
                                         p == 0 and i % 2 == 0, p == PAIRS - 1, skip_group_check=True)
                        if p == PAIRS - 1:
                            m.then_inc(out_made, 1)
                        elif i == TT - 1:
                            m.then_inc(out_used, 1)

            @block.scalar
            def _(act):
                for p in range(PAIRS):
                    for t in range(2):
                        act.wait_ge(v_made, 2 * p + t + 1)
                        if p >= 2:
                            act.wait_ge(v_low, p - 1)
                        act.activation(vf[:, p % 2, t * HALF:(t + 1) * HALF], pv[:, t, :], ACT.Copy
                                       ).then_inc(v_copied, 1)

            @block.vector
            def _(v):
                def split_at(p):
                    for t in range(2):
                        v.wait_ge(at_in[p % 2][t], 32 * (p // 2 + 1))
                        if p >= 2:
                            v.wait_ge(v_made, 2 * (p - 2) + t + 1)
                        v.tensor_copy(ath[:, p % 2, t], at[:, p % 2, t]).then_inc(at_high, 1)
                        v.wait_ge(at_high, 2 * p + t + 1)
                        v.tensor_tensor(atl[:, p % 2, t], at[:, p % 2, t], ath[:, p % 2, t].bitcast(F32),
                                        ALU.subtract).then_inc(at_low, 1)

                v.wait_ge(w_in, 16)
                v.wait_ge(w_zero, 2)
                for hh in range(2):
                    mine = wvh[:, :, hh::2, hh * DH:(hh + 1) * DH]
                    v.tensor_copy(mine, wv[:, :, hh::2, :]).then_inc(wv_high, 1)
                    v.wait_ge(wv_high, hh + 1)
                    v.tensor_tensor(wvl[:, :, hh::2, hh * DH:(hh + 1) * DH], wv[:, :, hh::2, :], mine.bitcast(F32),
                                    ALU.subtract).then_inc(wv_low, 1)
                split_at(0)
                v.wait_ge(wo_high, 16)
                v.tensor_copy(woh[:, :, :], wo[:, :, :]).then_inc(wo_high, 1)
                v.wait_ge(wo_high, 17)
                v.tensor_tensor(wol[:, :, :], wo[:, :, :], woh[:, :, :].bitcast(F32), ALU.subtract).then_inc(wo_low, 1)
                for p in range(PAIRS):
                    if p + 1 < PAIRS:
                        split_at(p + 1)
                    v.wait_ge(v_copied, 2 * p + 2)
                    if p >= 2:
                        v.wait_ge(out_used, p - 1)
                    v.tensor_copy(vh[:, p % 2, :], vf[:, p % 2, :]).then_inc(v_high, 1)
                    v.wait_ge(v_high, p + 1)
                    v.tensor_tensor(vl[:, p % 2, :], vf[:, p % 2, :], vh[:, p % 2, :].bitcast(F32), ALU.subtract
                                    ).then_inc(v_low, 1)
                for i in range(TT):
                    v.wait_ge(out_made, (i | 1) + 1)
                    v.tensor_tensor(res_x[:, i, :], res_x[:, i, :], po[:, i, :], ALU.add).then_inc(added, 1)
                v.wait_ge(added, TT)


SH, SD = 16, 16
SPAIRS = SH // 2


def self_attention(nc, res_x, ident, halfpow, Wqkv, WoT, XG):
    with ExitStack() as ctx:
        sb = lambda n, s, d: ctx.enter_context(nc.sbuf_tensor(n, s, d))
        sem = lambda n: ctx.enter_context(nc.semaphore(n))
        bank = ctx.enter_context(nc.psum_tensor("s_banks", [P, 8, HALF], F32))
        ln = LayerNorm(nc, sb, bank[:, 0:4, :], sem, "ln2", res_x, ident, halfpow, False)
        w = sb("w_qkv", [P, 3, DC, DIM], F32)
        wo = sb("w_so", [P, DC, DIM], F32)
        qT = sb("s_qT", [P, DC, TOK], F32)
        kT = sb("s_kT", [P, DC, TOK], F32)
        vb = sb("s_vb", [P, B, SPAIRS, 2 * SD], F32)
        mine = sb("s_mine", [P, 8], F32)
        above = sb("s_above", [P, NQ], F32)
        above2 = sb("s_above2", [P, NQ], F32)
        kb = sb("s_kb", [P, 4, 8, NQ], F32)
        s = sb("s_s", [P, 2, SH, NQ], F32)
        top = sb("s_top", [P, 2, SH], F32)
        tot = sb("s_tot", [P, 2, SH], F32)
        inv = sb("s_inv", [P, 2, SH], F32)
        aT = sb("s_aT", [P, 2, SPAIRS, P], F32)
        oT = sb("s_oT", [P, 2, DC, P], F32)

        nil = sb("s_nil", [P, ROWS // P * DIM // 4], F32)
        w_in, wo_in, nil_set, cleared = sem("s_w_in"), sem("s_wo_in"), sem("s_nil_set"), sem("s_cleared")
        g1, g2, v_zero = sem("s_g1"), sem("s_g2"), sem("s_v_zero")
        qk_made, qk_copied, v_made, v_laid = sem("s_qk_made"), sem("s_qk_copied"), sem("s_v_made"), sem("s_v_laid")
        k_laid, scored, masked = sem("s_k_laid"), sem("s_scored"), sem("s_masked")
        topped, shifted, expd, summed, inverted, normed = (sem("s_topped"), sem("s_shifted"), sem("s_expd"),
                                                           sem("s_summed"), sem("s_inverted"), sem("s_normed"))
        turned, a_copied, o_made, o_copied, y_made, added = (sem("s_turned"), sem("s_a_copied"), sem("s_o_made"),
                                                             sem("s_o_copied"), sem("s_y_made"), sem("s_added"))

        with nc.Block() as block:
            @block.sync
            def _(sp):
                sp.dma_start(w[:, :, :, :], Wqkv.rearrange("n (c p) d -> p n c d", p=P)).then_inc(w_in, 16)
                sp.dma_start(wo[:, :, :], WoT.rearrange("(c p) d -> p c d", p=P)).then_inc(wo_in, 16)
                sp.wait_ge(nil_set, 1)
                flat = XG.rearrange("(p n) d -> p (n d)", p=P)
                w4 = ROWS // P * DIM // 4
                for n in range(4):
                    sp.dma_start(flat[:, n * w4:(n + 1) * w4], nil[:, :]).then_inc(cleared, 16)
                sp.wait_ge(cleared, 64)

            @block.gpsimd
            def _(pool):
                pool.memset(nil[:, :], 0.0).then_inc(nil_set, 1)
                pool.memset(mine[:, :], 1.0).then_inc(g1, 1)
                pool.memset(above[:, :], 0.0).then_inc(g1, 1)
                pool.memset(above2[:, :], 0.0).then_inc(g1, 1)
                pool.memset(vb[:, :, :, :], 0.0).then_inc(v_zero, 1)
                pool.wait_ge(g1, 3)
                pool.affine_select(out=mine[:, :], in_=mine[:, :], compare_op=ALU.is_ge, fill=0.0, base=0,
                                   pattern=[[-SD, 8]], channel_multiplier=1).then_inc(g2, 1)
                pool.affine_select(out=above[:, :], in_=above[:, :], compare_op=ALU.is_ge, fill=-1e30, base=0,
                                   pattern=[[-1, NQ]], channel_multiplier=1).then_inc(g2, 1)
                pool.affine_select(out=above2[:, :], in_=above2[:, :], compare_op=ALU.is_ge, fill=-1e30, base=-NQ,
                                   pattern=[[-1, NQ]], channel_multiplier=1).then_inc(g2, 1)
                pool.wait_ge(g2, 3)
                pool.affine_select(out=mine[:, :], in_=mine[:, :], compare_op=ALU.is_ge, fill=0.0, base=SD - 1,
                                   pattern=[[SD, 8]], channel_multiplier=-1).then_inc(g2, 1)
                ln.pool_root(pool)
                pool.wait_ge(g2, 4)
                pool.wait_ge(qk_copied, 8)

                def lay_keys(i):
                    for n in range(4):
                        g = 4 * i + n
                        b, m = 2 * i + n // 2, n % 2
                        if g >= 4:
                            pool.wait_ge(scored, g - 3)
                        keys = kT[:, m, b * NQ:(b + 1) * NQ].unsqueeze(1).broadcast_to([P, 8, NQ])
                        pool.tensor_tensor(kb[:, n, :, :], keys, mine[:, :].unsqueeze(2).broadcast_to([P, 8, NQ]),
                                           ALU.mult).then_inc(k_laid, 1)

                lay_keys(0)
                for i in range(TT):
                    if i + 1 < TT:
                        lay_keys(i + 1)
                    pool.wait_ge(inverted, i + 1)
                    pool.tensor_tensor(s[:, i % 2], s[:, i % 2], inv[:, i % 2, :].unsqueeze(2).broadcast_to([P, SH, NQ]),
                                       ALU.mult).then_inc(normed, 1)

            @block.tensor
            def _(pe):
                ln.tensor_turn(pe)
                pe.wait_ge(w_in, 16)
                for n in range(8):
                    t, kind, m = n // 4, n // 2 % 2, n % 2
                    pe.wait_ge(ln.copied, 2 * t + 2)
                    bk = 4 + n % 4
                    if n >= 4:
                        pe.wait_ge(qk_copied, n - 3)
                    for c in range(DC):
                        mm = pe.matmul(bank[:, bk, :], w[:, kind, c, m * P:(m + 1) * P],
                                       ln.hT[:, c, t * HALF:(t + 1) * HALF], start=c == 0, stop=c == DC - 1)
                    mm.then_inc(qk_made, 1)
                for b in range(B):
                    if b >= 4:
                        pe.wait_ge(v_laid, 2 * (b - 3))
                    else:
                        pe.wait_ge(ln.copied, 4)
                    for hh in range(2):
                        for c in range(DC):
                            heads = w[:, 2, c, :].rearrange("p (j e d) -> p j e d", e=2, d=SD)[:, :, hh, :]
                            mm = pe.matmul(bank[hh * NQ:(hh + 1) * NQ, b % 4, 0:P], ln.hT[:, c, b * NQ:(b + 1) * NQ],
                                           heads, start=c == 0, stop=c == DC - 1)
                    mm.then_inc(v_made, 1)
                pe.wait_ge(v_laid, 2 * B)
                pe.wait_ge(wo_in, 16)

                def scores(i):
                    for n in range(4):
                        b2, m = n // 2, n % 2
                        pe.wait_ge(k_laid, 4 * i + n + 1)
                        if i >= 2 and n == 0:
                            pe.wait_ge(masked, 2 * (i - 1))
                        b = 2 * i + b2
                        pe.matmul(bank[b2 * NQ:(b2 + 1) * NQ, 2 * (i % 2) + m, :], qT[:, m, b * NQ:(b + 1) * NQ],
                                  kb[:, n, :, :], start=True, stop=True).then_inc(scored, 1)

                scores(0)
                for i in range(TT):
                    if i + 1 < TT:
                        scores(i + 1)
                    pe.wait_ge(normed, i + 1)
                    if i >= 1:
                        pe.wait_ge(a_copied, 2 * i)
                    for g in range(2):
                        for n in range(4):
                            pr = 4 * g + n
                            mm = pe.transpose(bank[:, 4 + g, n * P:(n + 1) * P],
                                              s[:, i % 2, 2 * pr:2 * pr + 2, :].rearrange("p h k -> p (h k)"), ident[:, :])
                        mm.then_inc(turned, 1)
                    pe.wait_ge(a_copied, 2 * i + 2)
                    if i >= 1:
                        pe.wait_ge(o_copied, i)
                    for pr in range(SPAIRS):
                        m, r = pr // 4, 32 * (pr % 4)
                        for b2 in range(2):
                            mm = pe.matmul(bank[r:r + 32, 6, m * P + b2 * NQ:m * P + (b2 + 1) * NQ],
                                           vb[:, 2 * i + b2, pr, :], aT[:, i % 2, pr, b2 * NQ:(b2 + 1) * NQ],
                                           start=True, stop=True)
                    mm.then_inc(o_made, 1)
                    pe.wait_ge(o_copied, i + 1)
                    if i >= 1:
                        pe.wait_ge(added, i)
                    for c in range(DC):
                        mm = pe.matmul(bank[:, 7, 0:DIM], oT[:, i % 2, c, :], wo[:, c, :], start=c == 0,
                                       stop=c == DC - 1)
                    mm.then_inc(y_made, 1)

            @block.scalar
            def _(act):
                ln.scalar_copy(act)
                for n in range(8):
                    t, kind, m = n // 4, n // 2 % 2, n % 2
                    act.wait_ge(qk_made, n + 1)
                    act.activation((kT if kind else qT)[:, m, t * HALF:(t + 1) * HALF], bank[:, 4 + n % 4, :],
                                   ACT.Copy).then_inc(qk_copied, 1)
                act.wait_ge(v_zero, 1)
                for b in range(B):
                    act.wait_ge(v_made, b + 1)
                    for hh in range(2):
                        r = slice(hh * NQ, (hh + 1) * NQ)
                        src = bank[r, b % 4, 0:P].rearrange("p (j d) -> p j d", d=SD)
                        act.activation(vb[r, b, :, hh * SD:(hh + 1) * SD], src, ACT.Copy).then_inc(v_laid, 1)

                def exp(i):
                    act.wait_ge(shifted, i + 1)
                    act.activation(s[:, i % 2], s[:, i % 2], ACT.Exp, scale=SD ** -0.5).then_inc(expd, 1)

                exp(0)
                for i in range(TT):
                    if i + 1 < TT:
                        exp(i + 1)
                    for g in range(2):
                        act.wait_ge(turned, 2 * i + g + 1)
                        if i >= 2:
                            act.wait_ge(o_made, i - 1)
                        act.activation(aT[:, i % 2, 4 * g:4 * g + 4, :], bank[:, 4 + g, :], ACT.Copy
                                       ).then_inc(a_copied, 1)
                    act.wait_ge(o_made, i + 1)
                    if i >= 2:
                        act.wait_ge(y_made, i - 1)
                    act.activation(oT[:, i % 2], bank[:, 6, 0:DC * P], ACT.Copy).then_inc(o_copied, 1)

            @block.vector
            def _(v):
                ln.vector_normalise(v)
                v.wait_ge(g2, 4)
                v.tensor_copy(above[NQ:P, :], above2[NQ:P, :]).then_inc(g1, 1)
                v.wait_ge(g1, 4)

                def softmax(i):
                    for m in range(2):
                        v.wait_ge(scored, 4 * i + 3 + m)
                        if i >= 2:
                            v.wait_ge(turned, 2 * (i - 1))
                        v.tensor_tensor(s[:, i % 2, 8 * m:8 * m + 8, :], bank[:, 2 * (i % 2) + m, :],
                                        above[:, :].unsqueeze(1).broadcast_to([P, 8, NQ]), ALU.add).then_inc(masked, 1)
                    v.wait_ge(masked, 2 * i + 2)
                    v.tensor_reduce(top[:, i % 2], s[:, i % 2], AX_X, ALU.max).then_inc(topped, 1)
                    v.wait_ge(topped, i + 1)
                    v.tensor_tensor(s[:, i % 2], s[:, i % 2], top[:, i % 2].unsqueeze(2).broadcast_to([P, SH, NQ]),
                                    ALU.subtract).then_inc(shifted, 1)
                    v.wait_ge(expd, i + 1)
                    if i >= 2:
                        v.wait_ge(normed, i - 1)
                    v.tensor_reduce(tot[:, i % 2], s[:, i % 2], AX_X, ALU.add).then_inc(summed, 1)
                    v.wait_ge(summed, i + 1)
                    v.reciprocal(inv[:, i % 2], tot[:, i % 2]).then_inc(inverted, 1)

                softmax(0)
                for i in range(TT):
                    if i + 1 < TT:
                        softmax(i + 1)
                    v.wait_ge(y_made, i + 1)
                    v.tensor_tensor(res_x[:, i, :], res_x[:, i, :], bank[:, 7, 0:DIM], ALU.add).then_inc(added, 1)
                v.wait_ge(added, TT)


E, F = 8, 512
FC = F // P
TOP = 2
MT = 256
TILES = (TOP * TOK + E * (MT - 1)) // MT
ROWS = TILES * MT
BIASES = 4 * FC


def route(nc, res_x, ident, ones, halfpow, Wgate, bgate, b3, XG, share, place, owner):
    with ExitStack() as ctx:
        sb = lambda n, s, d: ctx.enter_context(nc.sbuf_tensor(n, s, d))
        ps = lambda n, s: ctx.enter_context(nc.psum_tensor(n, s, F32))
        sem = lambda n: ctx.enter_context(nc.semaphore(n))
        bank = ps("r_banks", [P, 4, HALF])
        ln = LayerNorm(nc, sb, bank, sem, "ln3", res_x, ident, halfpow, False)
        wg = sb("r_wg", [P, DC, E], F32)
        bg = sb("r_bg", [1, E], F32)
        b3s = sb("r_b3", [E, DIM], F32)
        before = sb("r_before", [P, P], F32)
        iota_e = sb("r_iota_e", [P, E], F32)
        iota_t = sb("r_iota_t", [P, TILES], F32)
        logits = sb("r_logits", [P, TT, E], F32)
        best = sb("r_best", [P, TT, 8], F32)
        which = sb("r_which", [P, TT, 8], U32)
        whichf = sb("r_whichf", [P, TT, TOP], F32)
        gap = sb("r_gap", [P, TT], F32)
        egap = sb("r_egap", [P, TT], F32)
        den = sb("r_den", [P, TT], F32)
        hot = sb("r_hot", [P, TOP, TT, E], F32)
        both = sb("r_both", [P, TT, E], F32)
        mixed = sb("r_mixed", [P, TOP, TT, E], F32)
        comb = sb("r_comb", [P, TT, E], F32)
        combT = sb("r_combT", [E, TT, P], F32)
        rank = sb("r_rank", [P, TT + 1, E], F32)
        over = sb("r_over", [P, 4, E], F32)
        ends = sb("r_ends", [P, 4, E], F32)
        base = sb("r_base", [P, E], F32)
        spot = sb("r_spot", [P, TT, E], F32)
        picked = sb("r_picked", [P, TOP, TT, E], F32)
        placef = sb("r_placef", [P, TOP, TT], F32)
        past = sb("r_past", [P, TILES, E], F32)
        ownerf = sb("r_ownerf", [P, TILES], F32)
        pg = ps("r_pg", [P, TT, E])
        pr = ps("r_pr", [P, TT + 1, E])
        pc = ps("r_pc", [P, 2, P])
        pb = ps("r_pb", [P, DIM])

        w_in, g1, g2 = sem("r_w_in"), sem("r_g1"), sem("r_g2")
        gated, g_copied, d = sem("r_gated"), sem("r_g_copied"), sem("r_d")
        ranked, r_copied, edone = sem("r_ranked"), sem("r_r_copied"), sem("r_edone")
        c_turned, c_copied, b_made, b_added, sent = (sem("r_c_turned"), sem("r_c_copied"), sem("r_b_made"),
                                                     sem("r_b_added"), sem("r_sent"))
        steps = ["max", "index", "indexf", "gap", "den", "share0", "share1", "hot", "both", "mixed", "comb",
                 "over", "tiles1", "tiles", "end1", "end2", "ends", "base", "spot", "picked", "placef", "place",
                 "past", "ownerf", "ownermin", "owner"]
        counts = {"max": TT, "index": TT, "hot": TOP, "mixed": TOP, "picked": TOP, "over": 4, "end1": 2, "end2": 2,
                  "ends": 2}
        at, n = {}, 0
        for name in steps:
            n += counts.get(name, 1)
            at[name] = n

        with nc.Block() as block:
            @block.sync
            def _(sp):
                sp.dma_start(wg[:, :, :], Wgate.rearrange("(c p) e -> p c e", p=P)).then_inc(w_in, 16)
                sp.dma_start(bg[:, :], bgate.rearrange("(a e) -> a e", a=1)).then_inc(w_in, 16)
                sp.dma_start(b3s[:, :], b3).then_inc(w_in, 16)

            @block.gpsimd
            def _(pool):
                pool.memset(before[:, :], 1.0).then_inc(g1, 1)
                pool.iota(iota_e[:, :], [[1, E]], base=0, channel_multiplier=0,
                          allow_small_or_imprecise_dtypes=True).then_inc(g2, 1)
                pool.iota(iota_t[:, :], [[1, TILES]], base=0, channel_multiplier=0,
                          allow_small_or_imprecise_dtypes=True).then_inc(g2, 1)
                pool.wait_ge(g1, 1)
                pool.affine_select(out=before[:, :], in_=before[:, :], compare_op=ALU.is_gt, fill=0.0, base=0,
                                   pattern=[[1, P]], channel_multiplier=-1).then_inc(g2, 1)
                ln.pool_root(pool)
                pool.wait_ge(d, at["place"])
                pool.wait_ge(ln.norm, TT)
                for i in range(TT):
                    for k in range(TOP):
                        pool.indirect_dma_start(XG, bass.IndirectOffsetOnAxis(ap=place[:, k, i:i + 1], axis=0),
                                                ln.xn[:, i, :], None).then_inc(sent, 16)
                pool.wait_ge(sent, 16 * TT * TOP)

            @block.tensor
            def _(pe):
                ln.tensor_turn(pe)
                pe.wait_ge(ln.copied, 4)
                pe.wait_ge(w_in, 48)
                for i in range(TT):
                    for c in range(DC):
                        pe.matmul(pg[:, i, :], ln.hT[:, c, i * P:(i + 1) * P], wg[:, c, :], start=c == 0, stop=False)
                    m = pe.matmul(pg[:, i, :], ones[0:1, :], bg[:, :], start=False, stop=True)
                m.then_inc(gated, 1)
                pe.wait_ge(d, at["both"])
                pe.wait_ge(g2, 3)
                for i in range(TT + 1):
                    for j in range(i):
                        m = pe.matmul(pr[:, i, :], ones[:, :], both[:, j, :], start=j == 0,
                                      stop=i == TT and j == TT - 1)
                    if i < TT:
                        m = pe.matmul(pr[:, i, :], before[:, :], both[:, i, :], start=i == 0, stop=True)
                m.then_inc(ranked, 1)
                pe.wait_ge(d, at["comb"])
                for i in range(TT):
                    if i >= 2:
                        pe.wait_ge(c_copied, i - 1)
                    pe.transpose(pc[0:E, i % 2, :], comb[:, i, :], ident[:, :]).then_inc(c_turned, 1)
                    pe.wait_ge(c_copied, i + 1)
                    if i:
                        pe.wait_ge(b_added, i)
                    pe.matmul(pb[:, :], combT[:, i, :], b3s[:, :], start=True, stop=True).then_inc(b_made, 1)

            @block.scalar
            def _(act):
                ln.scalar_copy(act)
                act.wait_ge(gated, 1)
                act.activation(logits[:, :, :], pg[:, :, :], ACT.Copy).then_inc(g_copied, 1)
                act.wait_ge(d, at["gap"])
                act.activation(egap[:, :], gap[:, :], ACT.Exp).then_inc(edone, 1)
                act.wait_ge(ranked, 1)
                act.activation(rank[:, :, :], pr[:, :, :], ACT.Copy).then_inc(r_copied, 1)
                for i in range(TT):
                    act.wait_ge(c_turned, i + 1)
                    act.activation(combT[:, i, :], pc[0:E, i % 2, :], ACT.Copy).then_inc(c_copied, 1)

            @block.vector
            def _(v):
                done = [0]

                def after(name):
                    v.wait_ge(d, at[name])

                def inc(op):
                    done[0] += 1
                    op.then_inc(d, 1)

                ln.vector_normalise(v)
                v.wait_ge(g_copied, 1)
                for i in range(TT):
                    inc(v.max(best[:, i, :], logits[:, i, :]))
                for i in range(TT):
                    v.wait_ge(d, i + 1)
                    inc(v.max_index(which[:, i, :], best[:, i, :], logits[:, i, :]))
                after("index")
                inc(v.tensor_copy(whichf[:, :, :], which[:, :, 0:TOP]))
                inc(v.tensor_tensor(gap[:, :], best[:, :, 1], best[:, :, 0], ALU.subtract))
                v.wait_ge(edone, 1)
                inc(v.tensor_scalar(den[:, :], egap[:, :], 1.0, None, ALU.add))
                after("den")
                inc(v.reciprocal(share[:, 0, :], den[:, :]))
                after("share0")
                inc(v.tensor_tensor(share[:, 1, :], egap[:, :], share[:, 0, :], ALU.mult))
                v.wait_ge(g2, 3)
                for k in range(TOP):
                    inc(v.tensor_tensor(hot[:, k], whichf[:, :, k].unsqueeze(2).broadcast_to([P, TT, E]),
                                        iota_e[:, :].unsqueeze(1).broadcast_to([P, TT, E]), ALU.is_equal))
                after("hot")
                inc(v.tensor_tensor(both[:, :, :], hot[:, 0], hot[:, 1], ALU.add))
                for k in range(TOP):
                    inc(v.tensor_tensor(mixed[:, k], hot[:, k], share[:, k, :].unsqueeze(2).broadcast_to([P, TT, E]),
                                        ALU.mult))
                after("mixed")
                inc(v.tensor_tensor(comb[:, :, :], mixed[:, 0], mixed[:, 1], ALU.add))
                v.wait_ge(r_copied, 1)
                for n in range(4):
                    inc(v.tensor_scalar(over[:, n, :], rank[:, TT, :], float(n * MT), None, ALU.is_gt))
                after("over")
                inc(v.tensor_tensor(over[:, 0:2, :], over[:, 0:2, :], over[:, 2:4, :], ALU.add))
                after("tiles1")
                inc(v.tensor_tensor(ends[:, 0, :], over[:, 0, :], over[:, 1, :], ALU.add))
                for n, name in enumerate(("tiles", "end1", "end2")):
                    after(name)
                    z = 1 << n
                    inc(v.tensor_tensor(ends[:, n + 1, z:], ends[:, n, z:], ends[:, n, 0:E - z], ALU.add))
                    inc(v.tensor_copy(ends[:, n + 1, 0:z], ends[:, n, 0:z]))
                after("ends")
                inc(v.tensor_tensor(base[:, :], ends[:, 3, :], ends[:, 0, :], ALU.subtract))
                after("base")
                inc(v.scalar_tensor_tensor(out=spot[:, :, :], in0=base[:, :].unsqueeze(1).broadcast_to([P, TT, E]),
                                           scalar=float(MT), in1=rank[:, 0:TT, :], op0=ALU.mult, op1=ALU.add))
                after("spot")
                for k in range(TOP):
                    inc(v.tensor_tensor(picked[:, k], hot[:, k], spot[:, :, :], ALU.mult))
                after("picked")
                inc(v.tensor_reduce(placef[:, :, :], picked[:, :, :, :], AX_X, ALU.add))
                after("placef")
                inc(v.tensor_copy(place[:, :, :], placef[:, :, :]))
                inc(v.tensor_tensor(past[:, :, :], ends[:, 3, :].unsqueeze(1).broadcast_to([P, TILES, E]),
                                    iota_t[:, :].unsqueeze(2).broadcast_to([P, TILES, E]), ALU.is_le))
                after("past")
                inc(v.tensor_reduce(ownerf[:, :], past[:, :, :], AX_X, ALU.add))
                after("ownerf")
                inc(v.tensor_scalar(ownerf[:, :], ownerf[:, :], float(E - 1), None, ALU.min))
                after("ownermin")
                inc(v.tensor_copy(owner[:, :], ownerf[:, :]))
                assert done[0] == at["owner"]
                after("owner")
                for i in range(TT):
                    v.wait_ge(b_made, i + 1)
                    v.tensor_tensor(res_x[:, i, :], res_x[:, i, :], pb[:, :], ALU.add).then_inc(b_added, 1)
                v.wait_ge(b_added, TT)


def experts(nc, res_x, ident, W1, W2, Wg, Wl, W3, Bias, XG, YG, share, place, owner, out):
    with ExitStack() as ctx:
        sb = lambda n, s, d: ctx.enter_context(nc.sbuf_tensor(n, s, d))
        ps = lambda n, s: ctx.enter_context(nc.psum_tensor(n, s, F32))
        sem = lambda n: ctx.enter_context(nc.semaphore(n))
        A = 2 * DC * F
        G = 2 * FC * F
        Y = FC * DIM
        wr = sb("wr", [P, A + G + Y], F32)
        wh = sb("wh", [P, 2, A + G + Y], F32R)
        wl = sb("wl", [P, 2, A + G + Y], F32R)
        bias = sb("e_bias", [P, 2, BIASES], F32)
        halfg = sb("e_halfg", [P, 2, FC], F32)
        xg = sb("e_xg", [P, 2, MT // P, DIM], F32)
        xf = sb("e_xf", [P, DC, MT], F32)
        xh = sb("e_xh", [P, DC, MT], F32R)
        xl = sb("e_xl", [P, DC, MT], F32R)
        x1 = sb("e_x1", [P, 2, MT], F32)
        z = sb("e_z", [P, FC, MT], F32)
        zh = sb("e_zh", [P, 2, FC, MT], F32R)
        zl = sb("e_zl", [P, 2, FC, MT], F32R)
        tanh = sb("e_tanh", [P, 2, MT], F32)
        g = sb("e_g", [P, 2, MT], F32)
        u = sb("e_u", [P, 2, MT], F32)
        o = sb("e_o", [P, FC, MT], F32)
        oh = sb("e_oh", [P, FC, MT], F32R)
        ol = sb("e_ol", [P, FC, MT], F32R)
        y = sb("e_y", [P, MT // P, DIM], F32)
        pp = ps("pp", [P, FC, 2, MT])
        pt = ps("pt", [P, DC, MT])
        py = ps("py", [P, MT // P, DIM])

        w_in = [sem(f"e_w_in{n}") for n in range(4)]
        x_in, bx_in, bg_in = ([sem(f"e_{n}{b}") for b in range(2)] for n in ("x_in", "bx_in", "bg_in"))
        y_out = sem("e_y_out")
        w_high, w_low = [sem(f"e_w_high{n}") for n in range(4)], [sem(f"e_w_low{n}") for n in range(4)]
        b_half = sem("e_b_half")
        turned, x_copied, x_high, x_low = sem("e_turned"), sem("e_x_copied"), sem("e_x_high"), sem("e_x_low")
        x_made, x1_done, z_done, z_high, z_low = (sem("e_x_made"), sem("e_x1_done"), sem("e_z_done"),
                                                  sem("e_z_high"), sem("e_z_low"))
        g_made, g_done, u_done, o_done, o_high, o_low = (sem("e_g_made"), sem("e_g_done"), sem("e_u_done"),
                                                         sem("e_o_done"), sem("e_o_high"), sem("e_o_low"))
        tanh_done = sem("e_tanh_done")
        y_made, y_copied = sem("e_y_made"), sem("e_y_copied")
        parts = [slice(0, A), slice(A, A + G // 2), slice(A + G // 2, A + G), slice(A + G, A + G + Y)]

        def w1(w, b, k, c, f):
            return w[:, b, (k * DC + c) * F + f * P:(k * DC + c) * F + (f + 1) * P]

        def wgl(w, b, k, c, f):
            return w[:, b, A + (k * FC + c) * F + f * P:A + (k * FC + c) * F + (f + 1) * P]

        def w3(w, b, c):
            return w[:, b, A + G + c * DIM:A + G + (c + 1) * DIM]

        def tiles(eng, step):
            step(-1, 1, -1)
            step(0, 0, 0)
            step(1, 1, 0)
            step(2, 0, 1)
            with eng.Fori(1, (TILES - 3) // 2) as r:
                step(2 * r + 1, 1, r)
                step(2 * r + 2, 0, r + 1)
            step(TILES - 2, 1, TILES // 2 - 1)
            step(TILES - 1, 0, TILES // 2)
            step(TILES, 1, TILES // 2)

        def on(i):
            return not isinstance(i, int) or 0 <= i < TILES

        with nc.Block() as block:
            @block.sync
            def _(sp):
                def expert(i):
                    return sp.value_load(owner[0:1, bass.ds(i, 1)], min_val=0, max_val=E - 1)

                def rows_and_biases(i, b, e):
                    wait(sp, turned, i - 1)
                    sp.dma_start(xg[:, b], XG[bass.ds(i * MT, MT), :].rearrange("(t p) d -> p t d", p=P)
                                 ).then_inc(x_in[b], 16)
                    wait(sp, z_done, FC * (i - 1))
                    sp.dma_start(bias[:, b, 0:2 * FC], Bias[bass.ds(e, 1), :, 0:2 * FC].rearrange("a p n -> (a p) n")
                                 ).then_inc(bx_in[b], 16)

                def gate_biases(i, b, e):
                    wait(sp, o_done, FC * (i - 1))
                    sp.dma_start(bias[:, b, 2 * FC:], Bias[bass.ds(e, 1), :, 2 * FC:].rearrange("a p n -> (a p) n")
                                 ).then_inc(bg_in[b], 16)

                def weights(i, n, e):
                    wait(sp, w_low[n], i)
                    ws, rows_, width = [((W1, W2), DC, F), ((Wg,), FC, F), ((Wl,), FC, F), ((W3,), FC, DIM)][n]
                    at = parts[n].start
                    for k, w in enumerate(ws):
                        to = wr[:, at + k * rows_ * width:at + (k + 1) * rows_ * width]
                        sp.dma_start(to.rearrange("p (c f) -> p c f", c=rows_),
                                     w[bass.ds(e, 1)].rearrange("a (c p) f -> p (a c) f", p=P)).then_inc(w_in[n], 16)

                def step(i, b, h):
                    if on(i + 1):
                        gate_biases(i + 1, 1 - b, expert(i + 1))
                    if on(i + 2):
                        e = expert(i + 2)
                        rows_and_biases(i + 2, b, e)
                        weights(i + 2, 0, e)
                        weights(i + 2, 1, e)
                    if on(i - 1):
                        sp.wait_ge(y_copied, i)
                        sp.dma_start(YG[bass.ds((i - 1) * MT, MT), :].rearrange("(t p) d -> p t d", p=P), y[:, :, :]
                                     ).then_inc(y_out, 16)
                    if on(i + 2):
                        weights(i + 2, 2, e)
                        weights(i + 2, 3, e)

                e0 = expert(0)
                rows_and_biases(0, 0, e0)
                for n in range(4):
                    weights(0, n, e0)
                tiles(sp, step)
                sp.wait_ge(y_out, 16 * TILES)

            @block.gpsimd
            def _(pool):
                def step(i, b, h):
                    if on(i + 1):
                        for n in (1, 2, 3):
                            pool.wait_ge(w_high[n], i + 2)
                            pool.tensor_tensor(wl[:, 1 - b, parts[n]], wr[:, parts[n]],
                                               wh[:, 1 - b, parts[n]].bitcast(F32), ALU.subtract).then_inc(w_low[n], 1)

                tiles(pool, step)

            @block.tensor
            def _(pe):
                def first(i, b, h):
                    if not on(i):
                        return
                    pe.wait_ge(x_in[b], 16 * (h + 1))
                    wait(pe, x_copied, i)
                    for t in range(MT // P):
                        for c in range(DC):
                            m = pe.transpose(pt[:, c, t * P:(t + 1) * P], xg[:, b, t, c * P:(c + 1) * P], ident[:, :])
                    m.then_inc(turned, 1)

                def products(i, b):
                    if not on(i):
                        return
                    pe.wait_ge(x_low, i + 1)
                    pe.wait_ge(w_low[0], i + 1)
                    for f in range(FC):
                        wait(pe, o_done, FC * (i - 2) + f + 1)
                        if isinstance(i, int) and i == 1:
                            pe.wait_ge(z_done, f + 1)
                        for k in range(2):
                            for c in range(DC):
                                m = three_passes(pe, pp[:, f, k, :], w1(wh, b, k, c, f), w1(wl, b, k, c, f),
                                                 xh[:, c, :], xl[:, c, :], c == 0, c == DC - 1)
                        m.then_inc(x_made, 1)

                def outputs(i, b):
                    if not on(i):
                        return
                    pe.wait_ge(o_low, 2 * (i + 1))
                    pe.wait_ge(w_low[3], i + 1)
                    wait(pe, y_copied, i)
                    for t in range(MT // P):
                        for c in range(FC):
                            m = three_passes(pe, py[:, t, :], oh[:, c, t * P:(t + 1) * P], ol[:, c, t * P:(t + 1) * P],
                                             w3(wh, b, c), w3(wl, b, c), c == 0, c == FC - 1)
                    m.then_inc(y_made, 1)

                def gate(i, b):
                    if not on(i):
                        return
                    pe.wait_ge(w_low[1], i + 1)
                    pe.wait_ge(w_low[2], i + 1)
                    pe.wait_ge(z_low, 2 * (i + 1))
                    for f in range(FC):
                        if not isinstance(i, int) or i + 1 < TILES:
                            pe.wait_ge(z_done, FC * (i + 1) + f + 1)
                        else:
                            wait(pe, o_done, FC * (i - 1) + f + 1)
                        for k in range(2):
                            for c in range(FC):
                                m = three_passes(pe, pp[:, f, k, :], wgl(wh, b, k, c, f), wgl(wl, b, k, c, f),
                                                 zh[:, b, c, :], zl[:, b, c, :], c == 0, c == FC - 1)
                        m.then_inc(g_made, 1)

                def step(i, b, h):
                    products(i + 1, 1 - b)
                    outputs(i - 1, 1 - b)
                    first(i + 2, b, h + 1)
                    gate(i, b)

                first(0, 0, 0)
                tiles(pe, step)

            @block.scalar
            def _(act):
                def first(i, b):
                    if not on(i):
                        return
                    act.wait_ge(turned, i + 1)
                    wait(act, x_low, i)
                    act.activation(xf[:, :, :], pt[:, :, :], ACT.Copy).then_inc(x_copied, 1)

                def high(i, b, n):
                    if not on(i):
                        return
                    act.wait_ge(w_in[n], (32 if n == 0 else 16) * (i + 1))
                    used, each = [(x_made, FC), (g_made, FC), (g_made, FC), (y_made, 1)][n]
                    wait(act, used, each * (i - 1))
                    act.activation(wh[:, b, parts[n]], wr[:, parts[n]], ACT.Copy).then_inc(w_high[n], 1)

                def step(i, b, h):
                    if on(i + 1):
                        for f in range(FC):
                            act.wait_ge(x_made, FC * (i + 1) + f + 1)
                            if f == 0:
                                act.wait_ge(bx_in[1 - b], 16 * (h + 1 if b == 0 else h + 2))
                            wait(act, z_done, FC * (i + 1) + f - 1)
                            act.activation(x1[:, f % 2, :], pp[:, f, 0, :], ACT.Identity,
                                           bias=bias[:, 1 - b, f:f + 1]).then_inc(x1_done, 1)
                    high(i + 1, 1 - b, 1)
                    first(i + 2, b)
                    high(i + 1, 1 - b, 2)
                    high(i + 2, b, 0)
                    if on(i - 1):
                        act.wait_ge(y_made, i)
                        wait(act, y_out, 16 * (i - 1))
                        act.activation(y[:, :, :], py[:, :, :], ACT.Copy).then_inc(y_copied, 1)
                    high(i + 1, 1 - b, 3)
                    if on(i):
                        for f in range(FC):
                            act.wait_ge(g_made, FC * i + f + 1)
                            if f == 0:
                                act.wait_ge(b_half, i + 1)
                            wait(act, u_done, FC * i + f - 1)
                            act.activation(tanh[:, f % 2, :], pp[:, f, 0, :], ACT.Tanh, scale=0.5,
                                           bias=halfg[:, b, f:f + 1]).then_inc(tanh_done, 1)
                            act.activation(g[:, f % 2, :], pp[:, f, 0, :], ACT.Identity,
                                           bias=bias[:, b, 2 * FC + f:2 * FC + f + 1]).then_inc(g_done, 1)

                first(0, 0)
                high(0, 0, 0)
                tiles(act, step)

            @block.vector
            def _(v):
                def first(i, b):
                    if not on(i):
                        return
                    v.wait_ge(x_copied, i + 1)
                    wait(v, x_made, FC * i)
                    v.tensor_copy(xh[:, :, :], xf[:, :, :]).then_inc(x_high, 1)
                    v.wait_ge(x_high, i + 1)
                    v.tensor_tensor(xl[:, :, :], xf[:, :, :], xh[:, :, :].bitcast(F32), ALU.subtract
                                    ).then_inc(x_low, 1)

                def low(i, b):
                    if not on(i):
                        return
                    v.wait_ge(w_high[0], i + 1)
                    v.tensor_tensor(wl[:, b, parts[0]], wr[:, parts[0]], wh[:, b, parts[0]].bitcast(F32), ALU.subtract
                                    ).then_inc(w_low[0], 1)

                def halves(i, b, h):
                    if not on(i):
                        return
                    v.wait_ge(bg_in[b], 16 * (h + 1))
                    wait(v, tanh_done, FC * (i - 1))
                    v.tensor_scalar(halfg[:, b], bias[:, b, 2 * FC:3 * FC], 0.5, None, ALU.mult).then_inc(b_half, 1)

                def step(i, b, h):
                    if on(i + 1):
                        for f in range(FC):
                            v.wait_ge(x1_done, FC * (i + 1) + f + 1)
                            wait(v, z_low, 2 * (i + 1) + f // 2 - 1)
                            v.scalar_tensor_tensor(out=z[:, f, :], in0=pp[:, f, 1, :],
                                                   scalar=bias[:, 1 - b, FC + f:FC + f + 1], in1=x1[:, f % 2, :],
                                                   op0=ALU.add, op1=ALU.mult).then_inc(z_done, 1)
                            if f % 2:
                                pair = f // 2
                                w = slice(f - 1, f + 1)
                                v.wait_ge(z_done, FC * (i + 1) + f + 1)
                                wait(v, g_made, FC * i)
                                v.tensor_copy(zh[:, 1 - b, w, :], z[:, w, :]).then_inc(z_high, 1)
                                v.wait_ge(z_high, 2 * (i + 1) + pair + 1)
                                v.tensor_tensor(zl[:, 1 - b, w, :], z[:, w, :], zh[:, 1 - b, w, :].bitcast(F32),
                                                ALU.subtract).then_inc(z_low, 1)
                    halves(i + 1, 1 - b, h if b == 0 else h + 1)
                    first(i + 2, b)
                    low(i + 2, b)
                    if on(i):
                        for f in range(FC):
                            v.wait_ge(g_done, FC * i + f + 1)
                            wait(v, o_done, FC * i + f - 1)
                            v.scalar_tensor_tensor(out=u[:, f % 2, :], in0=tanh[:, f % 2, :], scalar=1.0,
                                                   in1=g[:, f % 2, :], op0=ALU.add, op1=ALU.mult).then_inc(u_done, 1)
                            v.wait_ge(u_done, FC * i + f + 1)
                            wait(v, o_low, 2 * i + f // 2 - 1)
                            v.scalar_tensor_tensor(out=o[:, f, :], in0=pp[:, f, 1, :],
                                                   scalar=bias[:, b, 3 * FC + f:3 * FC + f + 1], in1=u[:, f % 2, :],
                                                   op0=ALU.add, op1=ALU.mult).then_inc(o_done, 1)
                            if f % 2:
                                pair = f // 2
                                w = slice(f - 1, f + 1)
                                v.wait_ge(o_done, FC * i + f + 1)
                                wait(v, y_made, i)
                                v.tensor_copy(oh[:, w, :], o[:, w, :]).then_inc(o_high, 1)
                                v.wait_ge(o_high, 2 * i + pair + 1)
                                v.tensor_tensor(ol[:, w, :], o[:, w, :], oh[:, w, :].bitcast(F32), ALU.subtract
                                                ).then_inc(o_low, 1)

                first(0, 0)
                low(0, 0)
                tiles(v, step)

    with ExitStack() as ctx:
        sem = lambda n: ctx.enter_context(nc.semaphore(n))
        got = ctx.enter_context(nc.sbuf_tensor("f_got", [P, TT, TOP, DIM], F32))
        half = ctx.enter_context(nc.sbuf_tensor("f_half", [P, TOP, TT], F32))
        fetched = [sem(f"f_fetched{i}") for i in range(TT)]
        halved, mixed, stored = sem("f_halved"), sem("f_mixed"), sem("f_stored")

        with nc.Block() as block:
            @block.gpsimd
            def _(pool):
                for i in range(TT):
                    for k in range(TOP):
                        pool.indirect_dma_start(got[:, i, k, :], None, YG,
                                                bass.IndirectOffsetOnAxis(ap=place[:, k, i:i + 1], axis=0)
                                                ).then_inc(fetched[i], 16)

            @block.vector
            def _(v):
                v.tensor_scalar(half[:, :, :], share[:, :, :], 0.5, None, ALU.mult).then_inc(halved, 1)
                v.wait_ge(halved, 1)
                for i in range(TT):
                    v.wait_ge(fetched[i], 16 * TOP)
                    for k in range(TOP):
                        if k:
                            v.wait_ge(mixed, TOP * i + k)
                        v.scalar_tensor_tensor(out=res_x[:, i, :], in0=got[:, i, k, :], scalar=half[:, k, i:i + 1],
                                               in1=res_x[:, i, :], op0=ALU.mult, op1=ALU.add).then_inc(mixed, 1)

            @block.sync
            def _(sp):
                to = out.rearrange("b q d -> (b q) d").rearrange("(i p) d -> p i d", p=P)
                for i in range(TT):
                    sp.wait_ge(mixed, TOP * (i + 1))
                    sp.dma_start(to[:, i, :], res_x[:, i, :]).then_inc(stored, 16)
                sp.wait_ge(stored, 16 * TT)


def layer(nc, x, ctx_in, Wq, WkT, Wv, Wo, ln_g, ln_b, Wqkv, WoT, Wgate, bgate, W1, W2, Wg, Wl, W3, Bias, b3, out):
    scratch = lambda n, s: nc.dram_tensor(n, s, F32, kind="Internal").ap()
    QT = scratch("queries_scratch", (B, 2, P, DC, UH, NQ))
    OT = scratch("outputs_scratch", (B, 2, P, DC, UH, NQ))
    XG = scratch("routed_scratch", (ROWS, DIM))
    YG = scratch("expert_scratch", (ROWS, DIM))
    with ExitStack() as ctx:
        sb = lambda n, s, d: ctx.enter_context(nc.sbuf_tensor(n, s, d))
        sem = lambda n: ctx.enter_context(nc.semaphore(n))
        ident, ones, halfpow = sb("ident", [P, P], F32), sb("ones", [P, P], F32), sb("halfpow", [P, 16], F32)
        res_x = sb("res_x", [P, TT, DIM], F32)
        share = sb("share", [P, TOP, TT], F32)
        place = sb("place", [P, TOP, TT], U32)
        owner = sb("owner", [P, TILES], I32)
        constants(nc, ident, ones, halfpow, res_x, x, sem("zeroed"), sem("made"), sem("x_loaded"))
        spent, spent2 = [], []
        queries(nc, res_x, ident, halfpow, Wq, WkT, QT, spent)
        attend(nc, ident, ones, ctx_in, ln_g, ln_b, QT, OT, spent, spent2)
        project_out(nc, res_x, Wv, Wo, OT, spent2)
        self_attention(nc, res_x, ident, halfpow, Wqkv, WoT, XG)
        route(nc, res_x, ident, ones, halfpow, Wgate, bgate, b3, XG, share, place, owner)
        experts(nc, res_x, ident, W1, W2, Wg, Wl, W3, Bias, XG, YG, share, place, owner, out)


def kernel(x, ctx_1024, L0_xattn_Wq, L0_xattn_Wkv, L0_xattn_Wo, L0_xattn_ln_g, L0_xattn_ln_b, L0_attn_q_heads,
           L0_attn_k_heads, L0_attn_v_heads, L0_attn_output_proj, L0_ffn_Wgate, L0_ffn_bgate, L0_ffn_W1, L0_ffn_b1,
           L0_ffn_W2, L0_ffn_b2, L0_ffn_Wg, L0_ffn_bg, L0_ffn_Wl, L0_ffn_bl, L0_ffn_W3, L0_ffn_b3):
    import numpy as np
    import concourse.bacc as bacc
    from concourse.bass_utils import run_bass_kernel_spmd

    inner = HEADS * DH
    by_column = lambda a: np.ascontiguousarray(a.reshape(-1, P).T)
    arrays = {
        "x": x, "ctx_in": ctx_1024, "Wq": L0_xattn_Wq,
        "WkT": L0_xattn_Wkv[:, :inner].T, "Wv": L0_xattn_Wkv[:, inner:], "Wo": L0_xattn_Wo,
        "ln_g": by_column(L0_xattn_ln_g), "ln_b": by_column(L0_xattn_ln_b),
        "Wqkv": np.stack([L0_attn_q_heads.T, L0_attn_k_heads.T, L0_attn_v_heads.T]),
        "WoT": L0_attn_output_proj.T, "Wgate": L0_ffn_Wgate, "bgate": L0_ffn_bgate,
        "W1": L0_ffn_W1, "W2": L0_ffn_W2, "Wg": L0_ffn_Wg, "Wl": L0_ffn_Wl, "W3": L0_ffn_W3,
        "Bias": np.concatenate([b.reshape(E, FC, P).transpose(0, 2, 1)
                                for b in (L0_ffn_b1, L0_ffn_b2, L0_ffn_bg, L0_ffn_bl)], axis=2),
        "b3": L0_ffn_b3,
    }
    nc = bacc.Bacc("TRN2", target_bir_lowering=False, num_devices=1)
    feed, args = {}, []
    for name, a in arrays.items():
        a = np.ascontiguousarray(a)
        feed[f"in_{name}"] = a
        args.append(nc.dram_tensor(f"in_{name}", a.shape, mybir.dt.from_np(a.dtype), kind="ExternalInput").ap())
    args.append(nc.dram_tensor("out_x", (B, NQ, DIM), F32, kind="ExternalOutput").ap())
    layer(nc, *args)
    r = run_bass_kernel_spmd(nc, [feed], core_ids=[0])
    return r.results[0]["out_x"]
```

```python
from contextlib import ExitStack

import concourse.bass as bass
from concourse import mybir

F32 = mybir.dt.float32
F32R = mybir.dt.float32r
U32 = mybir.dt.uint32
I32 = mybir.dt.int32
ALU = mybir.AluOpType
ACT = mybir.ActivationFunctionType
AX_X = mybir.AxisListType.X

P = 128
B, NQ, DIM = 16, 64, 256
NK = 1601
HEADS, DH = 16, 64
TOK = B * NQ
TT = TOK // P
DC = DIM // P
PAIRS = HEADS // 2
HALF = TOK // 2
UH = HEADS // 2
UQ = UH * NQ
UNITS = 2 * B
KT = -(-NK // P)
LAST = NK - (KT - 1) * P
EPS = 1e-5
SCALE = DH ** -0.5


def wait(eng, sem, value):
    if isinstance(value, int) and value <= 0:
        return
    eng.wait_ge(sem, value)


def rows(t):
    return LAST if t == KT - 1 else P


class LayerNorm:

    def __init__(self, nc, sb, ps, sem, tag, x, ident, halfpow, split, xn=None):
        self.nc, self.x, self.ident, self.halfpow, self.split = nc, x, ident, halfpow, split
        self.st = sb(f"{tag}_st", [P, TT, 6], F32)
        self.mv = sb(f"{tag}_mv", [P, TT, 2], F32)
        self.ve = sb(f"{tag}_ve", [P, TT], F32)
        self.rstd = sb(f"{tag}_rstd", [P, TT], F32)
        self.xn = sb(f"{tag}_xn", [P, TT, DIM], F32) if xn is None else xn
        self.hT = sb(f"{tag}_hT", [P, DC, TOK], F32)
        if split:
            self.hTh = sb(f"{tag}_hTh", [P, DC, TOK], F32R)
            self.hTl = sb(f"{tag}_hTl", [P, DC, TOK], F32R)
        self.ps = ps
        self.stats = sem(f"{tag}_stats")
        self.aggr = sem(f"{tag}_aggr")
        self.veps = sem(f"{tag}_veps")
        self.root = sem(f"{tag}_root")
        self.norm = sem(f"{tag}_norm")
        self.turned = sem(f"{tag}_turned")
        self.copied = sem(f"{tag}_copied")
        self.high = sem(f"{tag}_high")
        self.low = sem(f"{tag}_low")

    def vector_normalise(self, v):
        for i in range(TT):
            v.bn_stats(self.st[:, i, :], self.x[:, i, :]).then_inc(self.stats, 1)
        for i in range(TT):
            v.wait_ge(self.stats, i + 1)
            v.bn_aggr(self.mv[:, i, :], self.st[:, i, :]).then_inc(self.aggr, 1)
        v.wait_ge(self.aggr, TT)
        v.tensor_scalar(self.ve[:, :], self.mv[:, :, 1], EPS, None, ALU.add).then_inc(self.veps, 1)
        v.wait_ge(self.root, 1)
        for i in range(TT):
            v.tensor_scalar(self.xn[:, i, :], self.x[:, i, :], self.mv[:, i, 0:1], self.rstd[:, i:i + 1],
                            ALU.subtract, ALU.mult).then_inc(self.norm, 1)

    def pool_root(self, pool):
        pool.wait_ge(self.veps, 1)
        pool.tensor_tensor(self.rstd[:, :], self.ve[:, :], self.halfpow[:, 0:TT], ALU.pow).then_inc(self.root, 1)

    def tensor_turn(self, pe):
        for th in range(2):
            for c in range(DC):
                for i in range(4):
                    pe.wait_ge(self.norm, 4 * th + i + 1)
                    m = pe.transpose(self.ps[:, 2 * th + c, i * P:(i + 1) * P],
                                     self.xn[:, 4 * th + i, c * P:(c + 1) * P], self.ident[:, :])
                m.then_inc(self.turned, 1)

    def scalar_copy(self, act):
        for th in range(2):
            for c in range(DC):
                act.wait_ge(self.turned, 2 * th + c + 1)
                act.activation(self.hT[:, c, th * HALF:(th + 1) * HALF], self.ps[:, 2 * th + c, :],
                               ACT.Copy).then_inc(self.copied, 1)

    def vector_split(self, v):
        for th in range(2):
            cols = slice(th * HALF, (th + 1) * HALF)
            v.wait_ge(self.copied, 2 * th + 2)
            v.tensor_copy(self.hTh[:, :, cols], self.hT[:, :, cols]).then_inc(self.high, 1)
            v.wait_ge(self.high, th + 1)
            v.tensor_tensor(self.hTl[:, :, cols], self.hT[:, :, cols], self.hTh[:, :, cols].bitcast(F32),
                            ALU.subtract).then_inc(self.low, 1)


def three_passes(pe, out, wh, wl, mh, ml, first, last, **more):
    pe.matmul(out, wl, mh, start=first, stop=False, **more)
    pe.matmul(out, wh, ml, start=False, stop=False, **more)
    return pe.matmul(out, wh, mh, start=False, stop=last, **more)


def constants(nc, ident, ones, halfpow, res_x, x, zeroed, made, x_in):
    with nc.Block() as block:
        @block.gpsimd
        def _(pool):
            pool.memset(ident[:, :], 0.0).then_inc(zeroed, 1)
            pool.memset(ones[:, :], 1.0).then_inc(made, 1)
            pool.memset(halfpow[:, :], -0.5).then_inc(made, 1)
            pool.wait_ge(zeroed, 1)
            pool.affine_select(out=ident[:, :], in_=ident[:, :], compare_op=ALU.not_equal, fill=1.0, base=0,
                               pattern=[[-1, P]], channel_multiplier=1).then_inc(made, 1)
            pool.wait_ge(made, 3)

        @block.sync
        def _(sp):
            sp.dma_start(res_x[:, :, :], x.rearrange("b q d -> (b q) d").rearrange("(i p) d -> p i d", p=P)
                         ).then_inc(x_in, 16)
            sp.wait_ge(x_in, 16)


def collecting(nc, ctx, kept):
    def sem(name):
        kept.append(ctx.enter_context(nc.semaphore(name)))
        return kept[-1]
    return sem


def clear(pool, spent):
    for s in spent:
        pool.sem_clear(s)


def queries(nc, res_x, ident, halfpow, Wq, WkT, QT, spent):
    with ExitStack() as ctx:
        sb = lambda n, s, d: ctx.enter_context(nc.sbuf_tensor(n, s, d))
        sem = collecting(nc, ctx, spent)
        bank = ctx.enter_context(nc.psum_tensor("q_banks", [P, 8, HALF], F32))
        ln = LayerNorm(nc, sb, bank[:, 0:4, :], sem, "ln1", res_x, ident, halfpow, True)
        wq = sb("wq", [P, DC, HEADS * DH], F32)
        wqh = sb("wqh", [P, DC, HEADS * DH], F32R)
        wql = sb("wql", [P, DC, HEADS * DH], F32R)
        wk = sb("wk", [P, PAIRS, DIM], F32)
        wkh = sb("wkh", [P, PAIRS, 2, DIM], F32R)
        wkl = sb("wkl", [P, PAIRS, 2, DIM], F32R)
        qf = sb("qf", [P, 2, TOK], F32)
        qh = sb("qh", [P, 2, TOK], F32R)
        ql = sb("ql", [P, 2, TOK], F32R)
        stage = sb("stage", [P, 2, 2, DC, B // 2, 2, NQ], F32)

        wq_in, wk_in = sem("wq_in"), sem("wk_in")
        wq_high, wq_low = sem("wq_high"), sem("wq_low")
        wk_zero, wk_high, wk_low = sem("wk_zero"), sem("wk_high"), sem("wk_low")
        q_made, q_copied, q_high, q_low = sem("q_made"), sem("q_copied"), sem("q_high"), sem("q_low")
        k_made, k_act, k_dve = sem("k_made"), sem("k_act"), sem("k_dve")
        stored = [sem("stored0"), sem("stored1")]
        pieces = [(th, hh, c) for th in range(2) for hh in range(2) for c in range(DC)]

        with nc.Block() as block:
            @block.sync
            def _(sp):
                sp.dma_start(wq[:, :, :], Wq.rearrange("(c p) n -> p c n", p=P)).then_inc(wq_in, 16)
                sp.dma_start(wk[:, :, :], WkT.rearrange("(j p) d -> p j d", p=P)).then_inc(wk_in, 16)
                for p in range(PAIRS):
                    hf, k = p // (PAIRS // 2), p % (PAIRS // 2)
                    for th in range(2):
                        sp.wait_ge(k_act, 4 * p + 2 * (th + 1))
                        sp.wait_ge(k_dve, 4 * p + 2 * (th + 1))
                        for c in range(DC):
                            dst = QT[th * B // 2:(th + 1) * B // 2, hf, :, c, 2 * k:2 * k + 2, :]
                            sp.dma_start(dst.rearrange("b p h t -> p b (h t)"),
                                         stage[:, p % 2, th, c].rearrange("p b h t -> p b (h t)")
                                         ).then_inc(stored[p % 2], 16)
                for s in stored:
                    sp.wait_ge(s, 16 * 4 * PAIRS // 2)

            @block.gpsimd
            def _(pool):
                pool.memset(wkh[:, :, :, :].bitcast(F32), 0.0).then_inc(wk_zero, 1)
                pool.memset(wkl[:, :, :, :].bitcast(F32), 0.0).then_inc(wk_zero, 1)
                ln.pool_root(pool)
                pool.wait_ge(wq_high, 1)
                pool.tensor_tensor(wql[:, :, :], wq[:, :, :], wqh[:, :, :].bitcast(F32), ALU.subtract
                                   ).then_inc(wq_low, 1)

            @block.tensor
            def _(pe):
                ln.tensor_turn(pe)

                def project(p):
                    for th in range(2):
                        if p >= 1:
                            pe.wait_ge(q_copied, 2 * (p - 1) + th + 1)
                        for c in range(DC):
                            w = slice(p * P, (p + 1) * P)
                            t = slice(th * HALF, (th + 1) * HALF)
                            m = three_passes(pe, bank[:, 4 + th, :], wqh[:, c, w], wql[:, c, w],
                                             ln.hTh[:, c, t], ln.hTl[:, c, t], c == 0, c == DC - 1)
                        m.then_inc(q_made, 1)

                pe.wait_ge(wq_low, 1)
                pe.wait_ge(ln.low, 2)
                project(0)
                pe.wait_ge(wk_low, 2)
                for p in range(PAIRS):
                    if p + 1 < PAIRS:
                        project(p + 1)
                    pe.wait_ge(q_low, p + 1)
                    for n, (th, hh, c) in enumerate(pieces):
                        g = len(pieces) * p + n
                        if g >= 4:
                            pe.wait_ge(k_act if g % 2 == 0 else k_dve, (g - 4) // 2 + 1)
                        t = slice(th * HALF, (th + 1) * HALF)
                        w = slice(c * P, (c + 1) * P)
                        three_passes(pe, bank[:, g % 4, :], wkh[:, p, hh, w], wkl[:, p, hh, w],
                                     qh[:, p % 2, t], ql[:, p % 2, t], True, True).then_inc(k_made, 1)

            def take(eng, copy, p, parity, mine):
                for n, (th, hh, c) in enumerate(pieces):
                    if n % 2 != parity:
                        continue
                    g = len(pieces) * p + n
                    eng.wait_ge(k_made, g + 1)
                    if p >= 2:
                        eng.wait_ge(stored[p % 2], 64 * (p // 2))
                    copy(stage[:, p % 2, th, c, :, hh, :],
                         bank[:, g % 4, :].rearrange("p (b t) -> p b t", t=NQ)).then_inc(mine, 1)

            @block.scalar
            def _(act):
                ln.scalar_copy(act)

                def copy_q(p):
                    for th in range(2):
                        act.wait_ge(q_made, 2 * p + th + 1)
                        if p >= 2:
                            act.wait_ge(q_low, p - 1)
                        act.activation(qf[:, p % 2, th * HALF:(th + 1) * HALF], bank[:, 4 + th, :],
                                       ACT.Copy).then_inc(q_copied, 1)

                copy_q(0)
                for p in range(PAIRS):
                    if p + 1 < PAIRS:
                        copy_q(p + 1)
                    take(act, lambda o, i: act.activation(o, i, ACT.Copy), p, 0, k_act)

            @block.vector
            def _(v):
                ln.vector_normalise(v)
                v.wait_ge(wq_in, 16)
                v.tensor_copy(wqh[:, :, :], wq[:, :, :]).then_inc(wq_high, 1)
                ln.vector_split(v)
                v.wait_ge(wk_in, 16)
                v.wait_ge(wk_zero, 2)

                def split_q(p):
                    v.wait_ge(q_copied, 2 * p + 2)
                    if p >= 2:
                        v.wait_ge(k_made, len(pieces) * (p - 1))
                    v.tensor_copy(qh[:, p % 2, :], qf[:, p % 2, :]).then_inc(q_high, 1)
                    v.wait_ge(q_high, p + 1)
                    v.tensor_tensor(ql[:, p % 2, :], qf[:, p % 2, :], qh[:, p % 2, :].bitcast(F32),
                                    ALU.subtract).then_inc(q_low, 1)

                for hh in range(2):
                    r = slice(hh * DH, (hh + 1) * DH)
                    v.tensor_copy(wkh[r, :, hh, :], wk[r, :, :]).then_inc(wk_high, 1)
                split_q(0)
                for hh in range(2):
                    r = slice(hh * DH, (hh + 1) * DH)
                    v.wait_ge(wk_high, hh + 1)
                    v.tensor_tensor(wkl[r, :, hh, :], wk[r, :, :], wkh[r, :, hh, :].bitcast(F32),
                                    ALU.subtract).then_inc(wk_low, 1)
                for p in range(PAIRS):
                    if p + 1 < PAIRS:
                        split_q(p + 1)
                    take(v, v.tensor_copy, p, 1, k_dve)


SLOTS = 2 * KT
LAG = KT + 8
RING = 5


def ring(t):
    return RING - 1 if t == KT - 1 else t % (RING - 1)


class Step:

    def __init__(self, r, c):
        self.r, self.c = r, c

    def back(self, n):
        c = self.c - n
        r = self.r + c // SLOTS
        c = c % SLOTS
        if isinstance(r, int) and not 0 <= r < B:
            return None
        return r, c // KT, c % KT

    def unit(self, start):
        c = self.c - start
        if c % KT:
            return None
        r = self.r + c // SLOTS
        if isinstance(r, int) and not 0 <= r < B:
            return None
        return r, c % SLOTS // KT

    def batch(self, at):
        c = self.c - at
        n = self.r + c // SLOTS
        return [n] if c % SLOTS == 0 and (not isinstance(n, int) or 0 <= n < B) else []

    def context(self, at):
        found = []
        for t in range(KT):
            c = self.c - at(t)
            if c % SLOTS == 0:
                n = self.r + c // SLOTS
                if not isinstance(n, int) or 0 <= n < B:
                    found.append((n, t))
        return found


def clock(eng, step):
    for c in range(-2 * SLOTS, 2 * SLOTS):
        step(Step(0, c))
    with eng.Fori(2, B - 2) as r:
        for c in range(SLOTS):
            step(Step(r, c))
    for c in range(4 * SLOTS):
        step(Step(B - 2, c))


def spread(start):
    return lambda t: start + 5 * t // 3


def attend(nc, ident, ones, ctx_in, ln_g, ln_b, QT, OT, earlier, spent):
    with ExitStack() as ctx:
        sb = lambda n, s, d: ctx.enter_context(nc.sbuf_tensor(n, s, d))
        ps = lambda n, s: ctx.enter_context(nc.psum_tensor(n, s, F32))
        sem = collecting(nc, ctx, spent)
        raw = sb("raw", [P, KT, DIM], F32)
        nrm = sb("nrm", [P, KT, DIM], F32)
        ch = sb("ch", [P, KT, DIM], F32R)
        cl = sb("cl", [P, KT, DIM], F32R)
        tf = sb("tf", [P, 3, DC, P], F32)
        th = sb("th", [P, KT, DC, P], F32R)
        tl = sb("tl", [P, KT, DC, P], F32R)
        st = sb("st", [P, KT, 6], F32)
        msum, mdif, vsum = sb("msum", [P, KT], F32), sb("mdif", [P, KT], F32), sb("vsum", [P, KT], F32)
        ve = sb("ve", [P, KT], F32)
        negmu = sb("negmu", [P, KT], F32)
        rstd = sb("rstd", [P, KT], F32)
        shift = sb("shift", [P, KT], F32)
        half13 = sb("half13", [P, KT], F32)
        gain = sb("gain", [P, DC], F32)
        bias = sb("bias", [P, DC], F32)
        qr = sb("qr", [P, DC, UQ], F32)
        qh = sb("qsh", [P, 2, DC, UQ], F32R)
        ql = sb("qsl", [P, 2, DC, UQ], F32R)
        s = sb("s", [P, 2, KT, UQ], F32)
        ph = sb("ph", [P, RING, UQ], F32R)
        pl = sb("pl", [P, RING, UQ], F32R)
        top = sb("top", [P, UQ], F32)
        mcol = sb("mcol", [P, 4], F32)
        most = sb("most", [P, 2, UQ], F32)
        total = sb("total", [P, 2, UQ], F32)
        icol = sb("icol", [P, 4], F32)
        inv = sb("inv", [P, UQ], F32)
        o = sb("o", [P, 2, DC, UQ], F32)
        score = ps("score", [P, 2, UQ])
        acc = ps("acc", [P, 2, DC, UQ])
        turn = ps("turn", [P, DC, P])
        misc = ps("misc", [P, 4, P])

        raw_in = [sem(f"raw_in{t}") for t in range(KT)]
        gb_in, q_in = sem("gb_in"), sem("q_in")
        o_out = [sem("o_out0"), sem("o_out1")]
        c_zero, c_exp = sem("c_zero"), sem("c_exp")
        c_stats, c_mom, c_ve, c_rstd, c_shift = sem("c_stats"), sem("c_mom"), sem("c_ve"), sem("c_rstd"), sem("c_shift")
        c_norm, c_turn, c_gain = sem("c_norm"), sem("c_turn"), sem("c_gain")
        t_high, t_low, r_high, r_low = sem("t_high"), sem("t_low"), sem("r_high"), sem("r_low")
        q_high, q_low = sem("qs_high"), sem("qs_low")
        scored, copied, maxed = sem("scored"), sem("copied"), sem("maxed")
        top_turned, top_col, top_spread, top_row = sem("top_turned"), sem("top_col"), sem("top_spread"), sem("top_row")
        shifted, expd, p_high, p_low, summed = sem("shifted"), sem("expd"), sem("p_high"), sem("p_low"), sem("summed")
        multiplied, sum_col, inverted, inv_spread, inv_row, scaled, biased = (
            sem("multiplied"), sem("sum_col"), sem("inverted"), sem("inv_spread"), sem("inv_row"), sem("scaled"),
            sem("biased"))

        slot = lambda r, u, t: SLOTS * r + KT * u + t
        unit = lambda r, u: 2 * r + u
        tile = lambda n, t: KT * n + t
        at_norm, at_turn, at_split = spread(-12), spread(-11), spread(-10)
        at_raw = lambda t: spread(-11)(t) - SLOTS
        at_stats = lambda t: t - 27
        at_root = -14
        at_rows = spread(LAG - KT + 1)

        with nc.Block() as block:
            @block.sync
            def _(sp):
                sp.dma_start(gain[:, :], ln_g).then_inc(gb_in, 16)
                sp.dma_start(bias[:, :], ln_b).then_inc(gb_in, 16)

                def step(k):
                    for n, t in k.context(at_raw):
                        wait(sp, c_norm, tile(n - 1, t) + 1)
                        sp.dma_start(raw[0:rows(t), t, :], ctx_in[n, t * P:t * P + rows(t), :]
                                     ).then_inc(raw_in[t], 16)
                    if (f := k.unit(-9)):
                        r, u = f
                        wait(sp, q_low, unit(r, u))
                        sp.dma_start(qr[:, :, :], QT[r, u].rearrange("p c h t -> p c (h t)")).then_inc(q_in, 16)
                    if (f := k.unit(KT + LAG + 5)):
                        r, u = f
                        sp.wait_ge(biased, DC * (unit(r, u) + 1))
                        sp.dma_start(OT[r, u].rearrange("p c h t -> p c (h t)"), o[:, u]).then_inc(o_out[u], 16)

                clock(sp, step)
                for u in range(2):
                    sp.wait_ge(o_out[u], 16 * B)

            @block.gpsimd
            def _(pool):
                clear(pool, earlier)
                pool.memset(st[:, :, :], 0.0).then_inc(c_zero, 1)
                pool.memset(half13[:, :], -0.5).then_inc(c_exp, 1)

                def step(k):
                    for n in k.batch(at_root):
                        pool.wait_ge(c_ve, 2 * (n + 1))
                        if isinstance(n, int) and n == 0:
                            pool.wait_ge(c_exp, 1)
                        wait(pool, c_norm, KT * n)
                        pool.tensor_tensor(rstd[:, :], ve[:, :], half13[:, :], ALU.pow).then_inc(c_rstd, 1)
                        pool.wait_ge(c_rstd, n + 1)
                        pool.tensor_tensor(shift[:, :], negmu[:, :], rstd[:, :], ALU.mult).then_inc(c_shift, 1)
                    if (f := k.unit(-5)):
                        r, u = f
                        pool.wait_ge(q_high, unit(r, u) + 1)
                        pool.tensor_tensor(ql[:, u], qr[:, :, :], qh[:, u].bitcast(F32), ALU.subtract
                                           ).then_inc(q_low, 1)
                    for n, t in k.context(at_split):
                        pool.wait_ge(t_high, tile(n, t) + 1)
                        pool.tensor_tensor(tl[:, t, :, 0:rows(t)], tf[:, 2 if t == KT - 1 else t % 2, :, 0:rows(t)],
                                           th[:, t, :, 0:rows(t)].bitcast(F32), ALU.subtract).then_inc(t_low, 1)
                    for n, t in k.context(at_rows):
                        pool.wait_ge(r_high, tile(n, t) + 1)
                        pool.tensor_tensor(cl[0:rows(t), t, :], nrm[0:rows(t), t, :],
                                           ch[0:rows(t), t, :].bitcast(F32), ALU.subtract).then_inc(r_low, 1)
                    if (f := k.back(LAG - 2)):
                        r, u, t = f
                        if t == 1:
                            wait(pool, sum_col, unit(r, u) - 1)
                            pool.wait_ge(expd, slot(r, u, t) + 1)
                            pool.tensor_tensor(total[:, u, :], s[:, u, 0, :], s[:, u, 1, :], ALU.add).then_inc(summed, 1)
                        elif t > 1:
                            pool.wait_ge(expd, slot(r, u, t) + 1)
                            pool.wait_ge(summed, (KT - 1) * unit(r, u) + t - 1)
                            pool.tensor_tensor(total[0:rows(t), u, :], total[0:rows(t), u, :], s[0:rows(t), u, t, :],
                                               ALU.add).then_inc(summed, 1)

                clock(pool, step)

            @block.tensor
            def _(pe):
                def step(k):
                    if (f := k.back(0)):
                        r, u, t = f
                        if t == 0:
                            pe.wait_ge(q_low, unit(r, u) + 1)
                        if u == 0:
                            pe.wait_ge(t_low, tile(r, t) + 1)
                        wait(pe, copied, slot(r, u, t) - 1)
                        for c in range(DC):
                            m = three_passes(pe, score[0:rows(t), slot(0, u, t) % 2, :], th[:, t, c, 0:rows(t)],
                                             tl[:, t, c, 0:rows(t)], qh[:, u, c, :], ql[:, u, c, :],
                                             c == 0, c == DC - 1)
                        m.then_inc(scored, 1)
                    for n, t in k.context(at_turn):
                        pe.wait_ge(c_norm, tile(n, t) + 1)
                        wait(pe, c_gain, DC * tile(n, t))
                        for c in range(DC):
                            m = pe.transpose(turn[:, c, 0:rows(t)], nrm[0:rows(t), t, c * P:(c + 1) * P],
                                             ident[0:rows(t), 0:rows(t)])
                        m.then_inc(c_turn, 1)
                    if (f := k.back(LAG)):
                        r, u, t = f
                        if t == 0:
                            wait(pe, scaled, DC * (unit(r, u) - 1))
                        if u == 0:
                            pe.wait_ge(r_low, tile(r, t) + 1)
                        pe.wait_ge(p_low, slot(r, u, t) + 1)
                        n = rows(t)
                        for c in range(DC):
                            w = slice(c * P, (c + 1) * P)
                            m = three_passes(pe, acc[:, u, c, :], ch[0:n, t, w], cl[0:n, t, w],
                                             ph[0:n, ring(t), :], pl[0:n, ring(t), :], t == 0, t == KT - 1)
                        m.then_inc(multiplied, 1)
                    if (f := k.unit(KT + 1)):
                        r, u = f
                        pe.wait_ge(maxed, (KT - 1) * (unit(r, u) + 1))
                        wait(pe, inv_row, unit(r, u) - 2)
                        for q in range(4):
                            m = pe.transpose(misc[:, q, :], top[:, q * P:(q + 1) * P], ident[:, :])
                        m.then_inc(top_turned, 1)
                    if (f := k.unit(KT + 2)):
                        r, u = f
                        pe.wait_ge(top_col, unit(r, u) + 1)
                        for q in range(4):
                            m = pe.matmul(misc[:, q, :], mcol[:, q:q + 1].broadcast_to([P, P]), ident[:, :],
                                          start=True, stop=True)
                        m.then_inc(top_spread, 1)
                    if (f := k.unit(KT + LAG)):
                        r, u = f
                        pe.wait_ge(summed, (KT - 1) * (unit(r, u) + 1))
                        ahead = unit(r, u) + 2
                        pe.wait_ge(top_row, min(ahead, UNITS) if isinstance(r, int) else ahead)
                        for q in range(4):
                            m = pe.matmul(misc[:, 0, q:q + 1], total[:, u, q * P:(q + 1) * P], ones[:, 0:1],
                                          start=True, stop=True)
                        m.then_inc(sum_col, 1)
                    if (f := k.unit(KT + LAG + 1)):
                        r, u = f
                        pe.wait_ge(inverted, unit(r, u) + 1)
                        for q in range(4):
                            m = pe.matmul(misc[:, q, :], icol[:, q:q + 1].broadcast_to([P, P]), ident[:, :],
                                          start=True, stop=True)
                        m.then_inc(inv_spread, 1)

                clock(pe, step)

            @block.scalar
            def _(act):
                def step(k):
                    if (f := k.unit(KT + 3)):
                        r, u = f
                        act.wait_ge(top_spread, unit(r, u) + 1)
                        wait(act, shifted, KT * (unit(r, u) - 1))
                        act.activation(most[:, u, :], misc[:, :, :], ACT.Copy).then_inc(top_row, 1)
                    if (f := k.back(LAG - 2)):
                        r, u, t = f
                        n = rows(t)
                        act.wait_ge(expd, slot(r, u, t) + 1)
                        wait(act, multiplied, slot(r, u, t) - (RING - 2))
                        act.activation(ph[0:n, ring(t), :], s[0:n, u, t, :], ACT.Copy).then_inc(p_high, 1)
                    if (f := k.back(LAG - 3)):
                        r, u, t = f
                        n = rows(t)
                        act.wait_ge(shifted, slot(r, u, t) + 1)
                        act.activation(s[0:n, u, t, :], s[0:n, u, t, :], ACT.Exp, scale=SCALE).then_inc(expd, 1)
                    for n, t in k.context(at_norm):
                        act.wait_ge(c_shift, n + 1)
                        wait(act, r_low, tile(n - 1, t) + 1)
                        wait(act, c_turn, tile(n - 1, t) + 1)
                        m = rows(t)
                        act.activation(nrm[0:m, t, :], raw[0:m, t, :], ACT.Identity, bias=shift[0:m, t:t + 1],
                                       scale=rstd[0:m, t:t + 1]).then_inc(c_norm, 1)
                    if (f := k.back(0)):
                        r, u, t = f
                        n = rows(t)
                        act.wait_ge(scored, slot(r, u, t) + 1)
                        wait(act, p_low, slot(r - 1, u, t) + 1)
                        if t:
                            wait(act, summed, (KT - 1) * unit(r - 1, u) + t)
                        else:
                            wait(act, summed, (KT - 1) * unit(r - 1, u) + 1)
                        act.activation(s[0:n, u, t, :], score[0:n, slot(0, u, t) % 2, :], ACT.Copy
                                       ).then_inc(copied, 1)
                    for n, t in k.context(at_turn):
                        act.wait_ge(c_turn, tile(n, t) + 1)
                        if isinstance(n, int) and n == 0:
                            act.wait_ge(gb_in, 32)
                        wait(act, t_low, tile(n, t) - 1)
                        m = rows(t)
                        for c in range(DC):
                            act.activation(tf[:, 2 if t == KT - 1 else t % 2, c, 0:m], turn[:, c, 0:m], ACT.Identity,
                                           bias=bias[:, c:c + 1], scale=gain[:, c:c + 1]).then_inc(c_gain, 1)
                    if (f := k.unit(KT + LAG + 2)):
                        r, u = f
                        act.wait_ge(inv_spread, unit(r, u) + 1)
                        wait(act, scaled, DC * unit(r, u))
                        act.activation(inv[:, :], misc[:, :, :], ACT.Copy).then_inc(inv_row, 1)
                    if (f := k.unit(KT + LAG + 4)):
                        r, u = f
                        for c in range(DC):
                            act.wait_ge(scaled, DC * unit(r, u) + c + 1)
                            act.activation(o[:, u, c, :], o[:, u, c, :], ACT.Identity, bias=bias[:, c:c + 1],
                                           scale=gain[:, c:c + 1]).then_inc(biased, 1)

                clock(act, step)

            @block.vector
            def _(v):
                def step(k):
                    if (f := k.unit(KT + 2)):
                        r, u = f
                        v.wait_ge(top_turned, unit(r, u) + 1)
                        wait(v, top_spread, unit(r, u))
                        v.tensor_reduce(mcol[:, :], misc[:, :, :], AX_X, ALU.max).then_inc(top_col, 1)
                    if (f := k.back(LAG - 4)):
                        r, u, t = f
                        n = rows(t)
                        if t == 0:
                            v.wait_ge(top_row, unit(r, u) + 1)
                        v.tensor_tensor(s[0:n, u, t, :], s[0:n, u, t, :], most[0:n, u, :], ALU.subtract
                                        ).then_inc(shifted, 1)
                    if (f := k.back(LAG - 1)):
                        r, u, t = f
                        n = rows(t)
                        v.wait_ge(p_high, slot(r, u, t) + 1)
                        v.tensor_tensor(pl[0:n, ring(t), :], s[0:n, u, t, :], ph[0:n, ring(t), :].bitcast(F32),
                                        ALU.subtract).then_inc(p_low, 1)
                    if (f := k.back(1)):
                        r, u, t = f
                        n = rows(t)
                        if t == 1:
                            wait(v, top_turned, unit(r, u))
                            v.wait_ge(copied, slot(r, u, t) + 1)
                            v.tensor_tensor(top[:, :], s[:, u, 0, :], s[:, u, 1, :], ALU.max).then_inc(maxed, 1)
                        elif t > 1:
                            v.wait_ge(copied, slot(r, u, t) + 1)
                            v.wait_ge(maxed, (KT - 1) * unit(r, u) + t - 1)
                            v.tensor_tensor(top[0:n, :], top[0:n, :], s[0:n, u, t, :], ALU.max).then_inc(maxed, 1)
                    if (f := k.unit(-5)):
                        r, u = f
                        v.wait_ge(q_in, 16 * (unit(r, u) + 1))
                        wait(v, scored, KT * (unit(r, u) - 1))
                        v.tensor_copy(qh[:, u], qr[:, :, :]).then_inc(q_high, 1)
                    for n, t in k.context(at_stats):
                        m = rows(t)
                        v.wait_ge(raw_in[t], 16 * (n + 1))
                        if isinstance(n, int) and n == 0 and t == 0:
                            v.wait_ge(c_zero, 1)
                        wait(v, c_ve, 2 * n)
                        v.bn_stats(st[0:m, t, :], raw[0:m, t, :]).then_inc(c_stats, 1)
                    for n in k.batch(at_root):
                        v.wait_ge(c_stats, KT * (n + 1))
                        v.tensor_tensor(msum[:, :], st[:, :, 1], st[:, :, 4], ALU.add).then_inc(c_mom, 1)
                        v.tensor_tensor(mdif[:, :], st[:, :, 1], st[:, :, 4], ALU.subtract).then_inc(c_mom, 1)
                        v.tensor_tensor(vsum[:, :], st[:, :, 2], st[:, :, 5], ALU.add).then_inc(c_mom, 1)
                        v.wait_ge(c_mom, 5 * n + 3)
                        v.tensor_scalar(negmu[:, :], msum[:, :], -0.5, None, ALU.mult).then_inc(c_ve, 1)
                        v.tensor_tensor(mdif[:, :], mdif[:, :], mdif[:, :], ALU.mult).then_inc(c_mom, 1)
                        v.tensor_scalar(vsum[:, :], vsum[:, :], 1.0 / DIM, EPS, ALU.mult, ALU.add).then_inc(c_mom, 1)
                        v.wait_ge(c_mom, 5 * n + 5)
                        v.scalar_tensor_tensor(out=ve[:, :], in0=mdif[:, :], scalar=0.25, in1=vsum[:, :],
                                               op0=ALU.mult, op1=ALU.add).then_inc(c_ve, 1)
                    for n, t in k.context(at_split):
                        m = rows(t)
                        v.wait_ge(c_gain, DC * (tile(n, t) + 1))
                        wait(v, scored, slot(n - 1, 1, t) + 1)
                        v.tensor_copy(th[:, t, :, 0:m], tf[:, 2 if t == KT - 1 else t % 2, :, 0:m]).then_inc(t_high, 1)
                    for n, t in k.context(at_rows):
                        m = rows(t)
                        v.wait_ge(c_norm, tile(n, t) + 1)
                        wait(v, multiplied, slot(n - 1, 1, t) + 1)
                        v.tensor_copy(ch[0:m, t, :], nrm[0:m, t, :]).then_inc(r_high, 1)
                    if (f := k.unit(KT + LAG + 1)):
                        r, u = f
                        v.wait_ge(sum_col, unit(r, u) + 1)
                        wait(v, inv_spread, unit(r, u))
                        v.reciprocal(icol[:, :], misc[:, 0, 0:4]).then_inc(inverted, 1)
                    if (f := k.unit(KT + LAG + 3)):
                        r, u = f
                        v.wait_ge(inv_row, unit(r, u) + 1)
                        v.wait_ge(multiplied, KT * (unit(r, u) + 1))
                        wait(v, o_out[u], 16 * r)
                        for c in range(DC):
                            v.tensor_tensor(o[:, u, c, :], acc[:, u, c, :], inv[:, :], ALU.mult).then_inc(scaled, 1)

                clock(v, step)


def project_out(nc, res_x, Wv, Wo, OT, earlier):
    with ExitStack() as ctx:
        sb = lambda n, s, d: ctx.enter_context(nc.sbuf_tensor(n, s, d))
        ps = lambda n, s: ctx.enter_context(nc.psum_tensor(n, s, F32))
        sem = lambda n: ctx.enter_context(nc.semaphore(n))
        wv = sb("wv", [P, DC, HEADS, DH], F32)
        wvh = sb("wvh", [P, DC, HEADS, P], F32R)
        wvl = sb("wvl", [P, DC, HEADS, P], F32R)
        wo = sb("wo", [P, PAIRS, DIM], F32)
        woh = sb("woh", [P, PAIRS, DIM], F32R)
        wol = sb("wol", [P, PAIRS, DIM], F32R)
        at = sb("at", [P, 2, 2, DC, B // 2, 2 * NQ], F32)
        ath = sb("ath", [P, 2, 2, DC, B // 2, 2 * NQ], F32R)
        atl = sb("atl", [P, 2, 2, DC, B // 2, 2 * NQ], F32R)
        vh = sb("vh", [P, 2, TOK], F32R)
        vl = sb("vl", [P, 2, TOK], F32R)
        pv = ps("pv", [P, 2, HALF])
        po = ps("po", [P, TT, DIM])
        wv_in, wo_in = [sem("wv_in0"), sem("wv_in1")], sem("wo_in")
        h_zero, l_zero, wv_high, wv_low, wo_high, wo_low = (sem("h_zero"), sem("l_zero"), sem("wv_high"),
                                                            sem("wv_low"), sem("wo_high"), sem("wo_low"))
        at_in = [[sem(f"at_in{a}{b}") for b in range(2)] for a in range(2)]
        at_high, at_low = sem("at_high"), sem("at_low")
        v_made, v_high, v_low, out_made, added = (sem("v_made"), sem("v_high"), sem("v_low"), sem("out_made"),
                                                  sem("added"))
        out_used = sem("out_used")

        def group(g):
            return slice(g * HEADS // 2, (g + 1) * HEADS // 2)

        def side(w, g, hh):
            return w[:, :, group(g).start + hh:group(g).stop:2, hh * DH:(hh + 1) * DH]

        def plain(g, hh):
            return wv[:, :, group(g).start + hh:group(g).stop:2, :]

        with nc.Block() as block:
            @block.sync
            def _(sp):
                def load_values_weights(g):
                    sp.dma_start(wv[:, :, group(g), :],
                                 Wv.rearrange("(c p) (h d) -> p c h d", p=P, d=DH)[:, :, group(g), :]
                                 ).then_inc(wv_in[g], 16)

                load_values_weights(0)
                for p in range(PAIRS):
                    hf, k = p // (PAIRS // 2), p % (PAIRS // 2)
                    for t in range(2):
                        if p >= 2:
                            sp.wait_ge(at_low, 2 * (p - 2) + t + 1)
                        for c in range(DC):
                            src = OT[t * B // 2:(t + 1) * B // 2, hf, :, c, 2 * k:2 * k + 2, :]
                            sp.dma_start(at[:, p % 2, t, c], src.rearrange("b p h t -> p b (h t)")
                                         ).then_inc(at_in[p % 2][t], 16)
                        if p == 1 and t == 0:
                            sp.dma_start(wo[:, :, :], Wo.rearrange("(j p) d -> p j d", p=P)).then_inc(wo_in, 16)
                    if p == 1:
                        load_values_weights(1)

            @block.gpsimd
            def _(pool):
                for g in range(2):
                    pool.memset(wvh[:, :, group(g), :].bitcast(F32), 0.0).then_inc(h_zero, 1)
                clear(pool, earlier)
                pool.wait_ge(wo_high, 1)
                pool.tensor_tensor(wol[:, :, :], wo[:, :, :], woh[:, :, :].bitcast(F32), ALU.subtract
                                   ).then_inc(wo_low, 1)

            @block.tensor
            def _(pe):
                def values(p):
                    if p % (PAIRS // 2) == 0:
                        pe.wait_ge(wv_low, 2 * (p // (PAIRS // 2) + 1))
                    for t in range(2):
                        if p >= 1:
                            pe.wait_ge(v_low, 2 * (p - 1) + t + 1)
                        pe.wait_ge(at_low, 2 * p + t + 1)
                        for hh in range(2):
                            for c in range(DC):
                                m = three_passes(pe, pv[:, t, :], wvh[:, c, 2 * p + hh, :], wvl[:, c, 2 * p + hh, :],
                                                 ath[:, p % 2, t, c, :, hh * NQ:(hh + 1) * NQ],
                                                 atl[:, p % 2, t, c, :, hh * NQ:(hh + 1) * NQ],
                                                 hh == 0 and c == 0, hh == 1 and c == DC - 1)
                        m.then_inc(v_made, 1)

                values(0)
                for p in range(PAIRS):
                    if p + 1 < PAIRS:
                        values(p + 1)
                    if p == 0:
                        pe.wait_ge(wo_low, 1)
                    pe.wait_ge(v_low, 2 * p + 2)
                    for i in range(TT):
                        w = slice(i * P, (i + 1) * P)
                        m = three_passes(pe, po[:, i, :], vh[:, p % 2, w], vl[:, p % 2, w], woh[:, p, :], wol[:, p, :],
                                         p == 0 and i % 2 == 0, p == PAIRS - 1, skip_group_check=True)
                        if p == PAIRS - 1:
                            m.then_inc(out_made, 1)
                        elif i == TT - 1:
                            m.then_inc(out_used, 1)

            @block.scalar
            def _(act):
                def high_at(p, t):
                    act.wait_ge(at_in[p % 2][t], 32 * (p // 2 + 1))
                    if p >= 2:
                        act.wait_ge(v_made, 2 * (p - 2) + t + 1)
                    act.activation(ath[:, p % 2, t], at[:, p % 2, t], ACT.Copy).then_inc(at_high, 1)

                def high_weights(g):
                    act.wait_ge(wv_in[g], 16)
                    act.wait_ge(h_zero, g + 1)
                    for hh in range(2):
                        act.activation(side(wvh, g, hh), plain(g, hh), ACT.Copy).then_inc(wv_high, 1)

                high_weights(0)
                for t in range(2):
                    high_at(0, t)
                high_at(1, 0)
                for p in range(PAIRS):
                    for t in range(2):
                        act.wait_ge(v_made, 2 * p + t + 1)
                        if p >= 2:
                            act.wait_ge(out_used, p - 1)
                        act.activation(vh[:, p % 2, t * HALF:(t + 1) * HALF], pv[:, t, :], ACT.Copy
                                       ).then_inc(v_high, 1)
                        if p == 0 and t == 0:
                            high_at(1, 1)
                            act.wait_ge(wo_in, 16)
                            act.activation(woh[:, :, :], wo[:, :, :], ACT.Copy).then_inc(wo_high, 1)
                        if p + 2 < PAIRS:
                            high_at(p + 2, t)
                    if p == 1:
                        high_weights(1)

            @block.vector
            def _(v):
                def low_at(p, t):
                    v.wait_ge(at_high, 2 * p + t + 1)
                    v.tensor_tensor(atl[:, p % 2, t], at[:, p % 2, t], ath[:, p % 2, t].bitcast(F32),
                                    ALU.subtract).then_inc(at_low, 1)

                def low_weights(g):
                    v.wait_ge(l_zero, g + 1)
                    for hh in range(2):
                        v.wait_ge(wv_high, 2 * g + hh + 1)
                        v.tensor_tensor(side(wvl, g, hh), plain(g, hh), side(wvh, g, hh).bitcast(F32), ALU.subtract
                                        ).then_inc(wv_low, 1)

                for g in range(2):
                    v.memset(wvl[:, :, group(g), :].bitcast(F32), 0.0).then_inc(l_zero, 1)
                low_weights(0)
                for t in range(2):
                    low_at(0, t)
                low_at(1, 0)
                for p in range(PAIRS):
                    for t in range(2):
                        cols = slice(t * HALF, (t + 1) * HALF)
                        v.wait_ge(v_high, 2 * p + t + 1)
                        v.tensor_tensor(vl[:, p % 2, cols], pv[:, t, :], vh[:, p % 2, cols].bitcast(F32),
                                        ALU.subtract).then_inc(v_low, 1)
                        if p == 0 and t == 0:
                            low_at(1, 1)
                        if p + 2 < PAIRS:
                            low_at(p + 2, t)
                    if p == 1:
                        low_weights(1)
                for i in range(TT):
                    v.wait_ge(out_made, (i | 1) + 1)
                    v.tensor_tensor(res_x[:, i, :], res_x[:, i, :], po[:, i, :], ALU.add).then_inc(added, 1)
                v.wait_ge(added, TT)


SH, SD = 16, 16
SPAIRS = SH // 2


def self_attention(nc, res_x, ident, halfpow, Wqkv, WoT, XG):
    with ExitStack() as ctx:
        sb = lambda n, s, d: ctx.enter_context(nc.sbuf_tensor(n, s, d))
        sem = lambda n: ctx.enter_context(nc.semaphore(n))
        bank = ctx.enter_context(nc.psum_tensor("s_banks", [P, 8, HALF], F32))
        ln = LayerNorm(nc, sb, bank[:, 0:4, :], sem, "ln2", res_x, ident, halfpow, False)
        w = sb("w_qkv", [P, 3, DC, DIM], F32)
        wo = sb("w_so", [P, DC, DIM], F32)
        qT = sb("s_qT", [P, DC, TOK], F32)
        kT = sb("s_kT", [P, DC, TOK], F32)
        vb = sb("s_vb", [P, B, SPAIRS, 2 * SD], F32)
        mine = sb("s_mine", [P, 8], F32)
        above = sb("s_above", [P, NQ], F32)
        above2 = sb("s_above2", [P, NQ], F32)
        kb = sb("s_kb", [P, 16, 8, NQ], F32)
        s = sb("s_s", [P, 4, SH, NQ], F32)
        top = sb("s_top", [P, 2, SH], F32)
        tot = sb("s_tot", [P, 2, SH], F32)
        inv = sb("s_inv", [P, 2, SH], F32)
        aT = sb("s_aT", [P, 2, SPAIRS, P], F32)
        oT = sb("s_oT", [P, 2, DC, P], F32)

        nil = sb("s_nil", [P, ROWS // P * DIM // 4], F32)
        w_in, wo_in, nil_set, cleared = sem("s_w_in"), sem("s_wo_in"), sem("s_nil_set"), sem("s_cleared")
        g1, g2, v_zero = sem("s_g1"), sem("s_g2"), sem("s_v_zero")
        qk_made, qk_copied, v_made = sem("s_qk_made"), sem("s_qk_copied"), sem("s_v_made")
        v_laid = sem("s_v_laid")
        k_laid0, k_laid, scored, masked = sem("s_k_laid0"), sem("s_k_laid"), sem("s_scored"), sem("s_masked")
        topped, shifted, expd, summed, inverted, normed = (sem("s_topped"), sem("s_shifted"), sem("s_expd"),
                                                           sem("s_summed"), sem("s_inverted"), sem("s_normed"))
        turned, a_copied, o_made, o_copied, y_made, added = (sem("s_turned"), sem("s_a_copied"), sem("s_o_made"),
                                                             sem("s_o_copied"), sem("s_y_made"), sem("s_added"))

        with nc.Block() as block:
            @block.sync
            def _(sp):
                sp.dma_start(w[:, :, :, :], Wqkv.rearrange("n (c p) d -> p n c d", p=P)).then_inc(w_in, 16)
                sp.dma_start(wo[:, :, :], WoT.rearrange("(c p) d -> p c d", p=P)).then_inc(wo_in, 16)
                sp.wait_ge(nil_set, 1)
                flat = XG.rearrange("(p n) d -> p (n d)", p=P)
                w4 = ROWS // P * DIM // 4
                for n in range(4):
                    sp.dma_start(flat[:, n * w4:(n + 1) * w4], nil[:, :]).then_inc(cleared, 16)
                sp.wait_ge(cleared, 64)

            @block.gpsimd
            def _(pool):
                pool.memset(nil[:, :], 0.0).then_inc(nil_set, 1)
                pool.memset(mine[:, :], 1.0).then_inc(g1, 1)
                pool.memset(above[:, :], 0.0).then_inc(g1, 1)
                pool.memset(above2[:, :], 0.0).then_inc(g1, 1)
                pool.memset(vb[:, :, :, :], 0.0).then_inc(v_zero, 1)
                pool.wait_ge(g1, 3)
                pool.affine_select(out=mine[:, :], in_=mine[:, :], compare_op=ALU.is_ge, fill=0.0, base=0,
                                   pattern=[[-SD, 8]], channel_multiplier=1).then_inc(g2, 1)
                pool.affine_select(out=above[:, :], in_=above[:, :], compare_op=ALU.is_ge, fill=-1e30, base=0,
                                   pattern=[[-1, NQ]], channel_multiplier=1).then_inc(g2, 1)
                pool.affine_select(out=above2[:, :], in_=above2[:, :], compare_op=ALU.is_ge, fill=-1e30, base=-NQ,
                                   pattern=[[-1, NQ]], channel_multiplier=1).then_inc(g2, 1)
                pool.wait_ge(g2, 3)
                pool.affine_select(out=mine[:, :], in_=mine[:, :], compare_op=ALU.is_ge, fill=0.0, base=SD - 1,
                                   pattern=[[SD, 8]], channel_multiplier=-1).then_inc(g2, 1)
                ln.pool_root(pool)
                pool.wait_ge(g2, 4)

                def lay_keys(i):
                    pool.wait_ge(qk_copied, 4 if i < TT // 2 else 8)
                    for n in range(1, 4):
                        g = 4 * i + n
                        b, m = 2 * i + n // 2, n % 2
                        if g >= 16:
                            pool.wait_ge(scored, g - 15)
                        keys = kT[:, m, b * NQ:(b + 1) * NQ].unsqueeze(1).broadcast_to([P, 8, NQ])
                        pool.tensor_tensor(kb[:, g % 16, :, :], keys, mine[:, :].unsqueeze(2).broadcast_to([P, 8, NQ]),
                                           ALU.mult).then_inc(k_laid, 1)

                def normalise(i):
                    pool.wait_ge(inverted, i + 1)
                    pool.tensor_tensor(s[:, i % 4], s[:, i % 4], inv[:, i % 2, :].unsqueeze(2).broadcast_to([P, SH, NQ]),
                                       ALU.mult).then_inc(normed, 1)

                for i in range(3):
                    lay_keys(i)
                for i in range(TT):
                    normalise(i)
                    if i + 3 < TT:
                        lay_keys(i + 3)

            @block.tensor
            def _(pe):
                ln.tensor_turn(pe)
                pe.wait_ge(w_in, 16)
                for n in range(8):
                    t, kind, m = n // 4, n // 2 % 2, n % 2
                    pe.wait_ge(ln.copied, 2 * t + 2)
                    bk = 4 + n % 4
                    if n >= 4:
                        pe.wait_ge(qk_copied, n - 3)
                    for c in range(DC):
                        mm = pe.matmul(bank[:, bk, :], w[:, kind, c, m * P:(m + 1) * P],
                                       ln.hT[:, c, t * HALF:(t + 1) * HALF], start=c == 0, stop=c == DC - 1)
                    mm.then_inc(qk_made, 1)

                def values(b):
                    if b >= 4:
                        pe.wait_ge(v_laid, 2 * (b - 3))
                    else:
                        pe.wait_ge(qk_copied, b + 5)
                    for hh in range(2):
                        for c in range(DC):
                            heads = w[:, 2, c, :].rearrange("p (j e d) -> p j e d", e=2, d=SD)[:, :, hh, :]
                            mm = pe.matmul(bank[hh * NQ:(hh + 1) * NQ, 4 + b % 4, 0:P], ln.hT[:, c, b * NQ:(b + 1) * NQ],
                                           heads, start=c == 0, stop=c == DC - 1)
                    mm.then_inc(v_made, 1)

                def scores(i):
                    for n in range(4):
                        b2, m = n // 2, n % 2
                        if n == 0:
                            pe.wait_ge(k_laid0, i + 1)
                        else:
                            pe.wait_ge(k_laid, 3 * i + n)
                        if i >= 2 and n == 0:
                            pe.wait_ge(masked, 2 * (i - 1))
                        b = 2 * i + b2
                        pe.matmul(bank[b2 * NQ:(b2 + 1) * NQ, 2 * (i % 2) + m, :], qT[:, m, b * NQ:(b + 1) * NQ],
                                  kb[:, (4 * i + n) % 16, :, :], start=True, stop=True).then_inc(scored, 1)

                def turn(i):
                    pe.wait_ge(normed, i + 1)
                    if i >= 1:
                        pe.wait_ge(a_copied, 2 * i)
                    for g in range(2):
                        for n in range(4):
                            pr = 4 * g + n
                            mm = pe.transpose(bank[:, 4 + g, n * P:(n + 1) * P],
                                              s[:, i % 4, 2 * pr:2 * pr + 2, :].rearrange("p h k -> p (h k)"), ident[:, :])
                        mm.then_inc(turned, 1)

                def outputs(i):
                    pe.wait_ge(a_copied, 2 * i + 2)
                    if i >= 1:
                        pe.wait_ge(o_copied, i)
                    for pr in range(SPAIRS):
                        m, r = pr // 4, 32 * (pr % 4)
                        for b2 in range(2):
                            mm = pe.matmul(bank[r:r + 32, 6, m * P + b2 * NQ:m * P + (b2 + 1) * NQ],
                                           vb[:, 2 * i + b2, pr, :], aT[:, i % 2, pr, b2 * NQ:(b2 + 1) * NQ],
                                           start=True, stop=True)
                    mm.then_inc(o_made, 1)

                def project(i):
                    pe.wait_ge(o_copied, i + 1)
                    if i >= 1:
                        pe.wait_ge(added, i)
                    for c in range(DC):
                        mm = pe.matmul(bank[:, 7, 0:DIM], oT[:, i % 2, c, :], wo[:, c, :], start=c == 0,
                                       stop=c == DC - 1)
                    mm.then_inc(y_made, 1)

                for i in range(3):
                    for b in (range(4), range(4, 10), range(10, B))[i]:
                        values(b)
                    scores(i)
                pe.wait_ge(v_laid, 2 * B)
                pe.wait_ge(wo_in, 16)
                for i in range(TT):
                    turn(i)
                    if i >= 1:
                        project(i - 1)
                    if i + 3 < TT:
                        scores(i + 3)
                    outputs(i)
                project(TT - 1)

            @block.scalar
            def _(act):
                ln.scalar_copy(act)
                for n in range(8):
                    t, kind, m = n // 4, n // 2 % 2, n % 2
                    act.wait_ge(qk_made, n + 1)
                    act.activation((kT if kind else qT)[:, m, t * HALF:(t + 1) * HALF], bank[:, 4 + n % 4, :],
                                   ACT.Copy).then_inc(qk_copied, 1)
                act.wait_ge(v_zero, 1)
                for b in range(B):
                    act.wait_ge(v_made, b + 1)
                    for hh in range(2):
                        r = slice(hh * NQ, (hh + 1) * NQ)
                        src = bank[r, 4 + b % 4, 0:P].rearrange("p (j d) -> p j d", d=SD)
                        act.activation(vb[r, b, :, hh * SD:(hh + 1) * SD], src, ACT.Copy).then_inc(v_laid, 1)

                def exp(i):
                    act.wait_ge(shifted, i + 1)
                    act.activation(s[:, i % 4], s[:, i % 4], ACT.Exp, scale=SD ** -0.5).then_inc(expd, 1)

                exp(0)
                exp(1)
                for i in range(TT):
                    for g in range(2):
                        act.wait_ge(turned, 2 * i + g + 1)
                        if i >= 2:
                            act.wait_ge(o_made, i - 1)
                        act.activation(aT[:, i % 2, 4 * g:4 * g + 4, :], bank[:, 4 + g, :], ACT.Copy
                                       ).then_inc(a_copied, 1)
                    act.wait_ge(o_made, i + 1)
                    if i >= 2:
                        act.wait_ge(y_made, i - 1)
                    act.activation(oT[:, i % 2], bank[:, 6, 0:DC * P], ACT.Copy).then_inc(o_copied, 1)
                    if i + 2 < TT:
                        exp(i + 2)

            @block.vector
            def _(v):
                ln.vector_normalise(v)
                v.wait_ge(g2, 4)
                v.tensor_copy(above[NQ:P, :], above2[NQ:P, :]).then_inc(g1, 1)
                v.wait_ge(g1, 4)

                def lay_keys(i):
                    v.wait_ge(qk_copied, 4 if i < TT // 2 else 8)
                    g, b = 4 * i, 2 * i
                    if g >= 16:
                        v.wait_ge(scored, g - 15)
                    keys = kT[:, 0, b * NQ:(b + 1) * NQ].unsqueeze(1).broadcast_to([P, 8, NQ])
                    v.tensor_tensor(kb[:, g % 16, :, :], keys, mine[:, :].unsqueeze(2).broadcast_to([P, 8, NQ]),
                                    ALU.mult).then_inc(k_laid0, 1)

                def shift(i):
                    for m in range(2):
                        v.wait_ge(scored, 4 * i + 3 + m)
                        if i >= 4:
                            v.wait_ge(turned, 2 * (i - 3))
                        v.tensor_tensor(s[:, i % 4, 8 * m:8 * m + 8, :], bank[:, 2 * (i % 2) + m, :],
                                        above[:, :].unsqueeze(1).broadcast_to([P, 8, NQ]), ALU.add).then_inc(masked, 1)
                    v.wait_ge(masked, 2 * i + 2)
                    if i >= 2:
                        v.wait_ge(shifted, i - 1)
                    v.tensor_reduce(top[:, i % 2], s[:, i % 4], AX_X, ALU.max).then_inc(topped, 1)
                    v.wait_ge(topped, i + 1)
                    v.tensor_tensor(s[:, i % 4], s[:, i % 4], top[:, i % 2].unsqueeze(2).broadcast_to([P, SH, NQ]),
                                    ALU.subtract).then_inc(shifted, 1)

                def invert(i):
                    v.wait_ge(expd, i + 1)
                    if i >= 2:
                        v.wait_ge(inverted, i - 1)
                        v.wait_ge(normed, i - 1)
                    v.tensor_reduce(tot[:, i % 2], s[:, i % 4], AX_X, ALU.add).then_inc(summed, 1)
                    v.wait_ge(summed, i + 1)
                    v.reciprocal(inv[:, i % 2], tot[:, i % 2]).then_inc(inverted, 1)

                for i in range(4):
                    lay_keys(i)
                shift(0)
                shift(1)
                for i in range(-1, TT):
                    if 0 <= i < TT - 4:
                        lay_keys(i + 4)
                    if i + 1 < TT:
                        invert(i + 1)
                    if i >= 1:
                        v.wait_ge(y_made, i)
                        v.tensor_tensor(res_x[:, i - 1, :], res_x[:, i - 1, :], bank[:, 7, 0:DIM], ALU.add
                                        ).then_inc(added, 1)
                    if i + 3 < TT:
                        shift(i + 3)
                v.wait_ge(y_made, TT)
                v.tensor_tensor(res_x[:, TT - 1, :], res_x[:, TT - 1, :], bank[:, 7, 0:DIM], ALU.add
                                ).then_inc(added, 1)
                v.wait_ge(added, TT)


E, F = 8, 512
FC = F // P
TOP = 2
MT = 256
TILES = (TOP * TOK + E * (MT - 1)) // MT
ROWS = TILES * MT
BIASES = 4 * FC


def route(nc, res_x, ident, ones, halfpow, Wgate, bgate, xn, share, comb, place, owner):
    with ExitStack() as ctx:
        sb = lambda n, s, d: ctx.enter_context(nc.sbuf_tensor(n, s, d))
        ps = lambda n, s: ctx.enter_context(nc.psum_tensor(n, s, F32))
        sem = lambda n: ctx.enter_context(nc.semaphore(n))
        bank = ps("r_banks", [P, 4, HALF])
        ln = LayerNorm(nc, sb, bank, sem, "ln3", res_x, ident, halfpow, False, xn)
        wg = sb("r_wg", [P, DC, E], F32)
        bg = sb("r_bg", [E, 1], F32)
        logitsT = sb("r_logitsT", [E, TOK], F32)
        before = sb("r_before", [P, P], F32)
        iota_e = sb("r_iota_e", [P, E], F32)
        iota_t = sb("r_iota_t", [P, TILES], F32)
        logits = sb("r_logits", [P, TT, E], F32)
        best = sb("r_best", [P, TT, 8], F32)
        which = sb("r_which", [P, TT, 8], U32)
        whichf = sb("r_whichf", [P, TT, TOP], F32)
        gap = sb("r_gap", [P, TT], F32)
        egap = sb("r_egap", [P, TT], F32)
        den = sb("r_den", [P, TT], F32)
        hot = sb("r_hot", [P, TOP, TT, E], F32)
        both = sb("r_both", [P, TT, E], F32)
        mixed = sb("r_mixed", [P, TOP, TT, E], F32)
        sofar = sb("r_sofar", [P, TT + 1, E], F32)
        rank = sb("r_rank", [P, TT + 1, E], F32)
        over = sb("r_over", [P, 4, E], F32)
        ends = sb("r_ends", [P, 4, E], F32)
        base = sb("r_base", [P, E], F32)
        spot = sb("r_spot", [P, TT, E], F32)
        picked = sb("r_picked", [P, TOP, TT, E], F32)
        placef = sb("r_placef", [P, TOP, TT], F32)
        past = sb("r_past", [P, TILES, E], F32)
        ownerf = sb("r_ownerf", [P, TILES], F32)
        pg = ps("r_pg", [P, TT, E])
        pr = ps("r_pr", [P, TT + 1, E])

        w_in, g1, g2 = sem("r_w_in"), sem("r_g1"), sem("r_g2")
        gatedT, gT_copied = sem("r_gatedT"), sem("r_gT_copied")
        gated, g_copied, d = sem("r_gated"), sem("r_g_copied"), sem("r_d")
        ranked, r_copied, edone = sem("r_ranked"), sem("r_r_copied"), sem("r_edone")
        steps = ["max", "index", "indexf", "gap", "den", "share0", "share1", "hot", "both", "sofar", "mixed", "comb",
                 "over", "tiles1", "tiles", "end1", "end2", "ends", "base", "spot", "picked", "placef", "place",
                 "past", "ownerf", "ownermin", "owner"]
        counts = {"max": TT, "index": TT, "hot": TOP, "sofar": TT, "mixed": TOP, "picked": TOP, "over": 4, "end1": 2, "end2": 2,
                  "ends": 2}
        at, n = {}, 0
        for name in steps:
            n += counts.get(name, 1)
            at[name] = n

        with nc.Block() as block:
            @block.sync
            def _(sp):
                sp.dma_start(wg[:, :, :], Wgate.rearrange("(c p) e -> p c e", p=P)).then_inc(w_in, 16)
                sp.dma_start(bg[:, :], bgate.rearrange("(e a) -> e a", a=1)).then_inc(w_in, 16)

            @block.gpsimd
            def _(pool):
                pool.memset(before[:, :], 1.0).then_inc(g1, 1)
                pool.memset(sofar[:, 0, :], 0.0).then_inc(g2, 1)
                pool.iota(iota_e[:, :], [[1, E]], base=0, channel_multiplier=0,
                          allow_small_or_imprecise_dtypes=True).then_inc(g2, 1)
                pool.iota(iota_t[:, :], [[1, TILES]], base=0, channel_multiplier=0,
                          allow_small_or_imprecise_dtypes=True).then_inc(g2, 1)
                pool.wait_ge(g1, 1)
                pool.affine_select(out=before[:, :], in_=before[:, :], compare_op=ALU.is_gt, fill=0.0, base=0,
                                   pattern=[[1, P]], channel_multiplier=-1).then_inc(g2, 1)
                ln.pool_root(pool)

            @block.tensor
            def _(pe):
                ln.tensor_turn(pe)
                pe.wait_ge(w_in, 32)
                for t in range(2):
                    pe.wait_ge(ln.copied, 2 * t + 2)
                    for c in range(DC):
                        m = pe.matmul(bank[0:E, 2 * t, :], wg[:, c, :], ln.hT[:, c, t * HALF:(t + 1) * HALF],
                                      start=c == 0, stop=c == DC - 1)
                    m.then_inc(gatedT, 1)
                for i in range(TT):
                    pe.wait_ge(gT_copied, i // 4 + 1)
                    m = pe.transpose(pg[:, i, :], logitsT[:, i * P:(i + 1) * P], ident[0:E, 0:E])
                m.then_inc(gated, 1)
                pe.wait_ge(d, at["sofar"])
                pe.wait_ge(g2, 4)
                pe.matmul(pr[:, 0:TT, :], ones[:, :], sofar[:, 0:TT, :], start=True, stop=False)
                pe.matmul(pr[:, 0:TT, :], before[:, :], both[:, :, :], start=False, stop=True)
                pe.matmul(pr[:, TT, :], ones[:, :], sofar[:, TT, :], start=True, stop=True).then_inc(ranked, 1)
            @block.scalar
            def _(act):
                ln.scalar_copy(act)
                act.wait_ge(w_in, 32)
                for t in range(2):
                    act.wait_ge(gatedT, t + 1)
                    act.activation(logitsT[:, t * HALF:(t + 1) * HALF], bank[0:E, 2 * t, :], ACT.Identity,
                                   bias=bg[:, 0:1]).then_inc(gT_copied, 1)
                act.wait_ge(gated, 1)
                act.activation(logits[:, :, :], pg[:, :, :], ACT.Copy).then_inc(g_copied, 1)
                act.wait_ge(d, at["gap"])
                act.activation(egap[:, :], gap[:, :], ACT.Exp).then_inc(edone, 1)
                act.wait_ge(ranked, 1)
                act.activation(rank[:, :, :], pr[:, :, :], ACT.Copy).then_inc(r_copied, 1)

            @block.vector
            def _(v):
                done = [0]

                def after(name):
                    v.wait_ge(d, at[name])

                def inc(op):
                    done[0] += 1
                    op.then_inc(d, 1)

                ln.vector_normalise(v)
                v.wait_ge(g_copied, 1)
                for i in range(TT):
                    inc(v.max(best[:, i, :], logits[:, i, :]))
                for i in range(TT):
                    v.wait_ge(d, i + 1)
                    inc(v.max_index(which[:, i, :], best[:, i, :], logits[:, i, :]))
                after("index")
                inc(v.tensor_copy(whichf[:, :, :], which[:, :, 0:TOP]))
                inc(v.tensor_tensor(gap[:, :], best[:, :, 1], best[:, :, 0], ALU.subtract))
                v.wait_ge(edone, 1)
                inc(v.tensor_scalar(den[:, :], egap[:, :], 1.0, None, ALU.add))
                after("den")
                inc(v.reciprocal(share[:, 0, :], den[:, :]))
                after("share0")
                inc(v.tensor_tensor(share[:, 1, :], egap[:, :], share[:, 0, :], ALU.mult))
                v.wait_ge(g2, 4)
                for k in range(TOP):
                    inc(v.tensor_tensor(hot[:, k], whichf[:, :, k].unsqueeze(2).broadcast_to([P, TT, E]),
                                        iota_e[:, :].unsqueeze(1).broadcast_to([P, TT, E]), ALU.is_equal))
                after("hot")
                inc(v.tensor_tensor(both[:, :, :], hot[:, 0], hot[:, 1], ALU.add))
                for i in range(TT):
                    v.wait_ge(d, at["both"] + i)
                    inc(v.tensor_tensor(sofar[:, i + 1, :], sofar[:, i, :], both[:, i, :], ALU.add))
                for k in range(TOP):
                    inc(v.tensor_tensor(mixed[:, k], hot[:, k], share[:, k, :].unsqueeze(2).broadcast_to([P, TT, E]),
                                        ALU.mult))
                after("mixed")
                inc(v.tensor_tensor(comb[:, :, :], mixed[:, 0], mixed[:, 1], ALU.add))
                v.wait_ge(r_copied, 1)
                for n in range(4):
                    inc(v.tensor_scalar(over[:, n, :], rank[:, TT, :], float(n * MT), None, ALU.is_gt))
                after("over")
                inc(v.tensor_tensor(over[:, 0:2, :], over[:, 0:2, :], over[:, 2:4, :], ALU.add))
                after("tiles1")
                inc(v.tensor_tensor(ends[:, 0, :], over[:, 0, :], over[:, 1, :], ALU.add))
                for n, name in enumerate(("tiles", "end1", "end2")):
                    after(name)
                    z = 1 << n
                    inc(v.tensor_tensor(ends[:, n + 1, z:], ends[:, n, z:], ends[:, n, 0:E - z], ALU.add))
                    inc(v.tensor_copy(ends[:, n + 1, 0:z], ends[:, n, 0:z]))
                after("ends")
                inc(v.tensor_tensor(base[:, :], ends[:, 3, :], ends[:, 0, :], ALU.subtract))
                after("base")
                inc(v.scalar_tensor_tensor(out=spot[:, :, :], in0=base[:, :].unsqueeze(1).broadcast_to([P, TT, E]),
                                           scalar=float(MT), in1=rank[:, 0:TT, :], op0=ALU.mult, op1=ALU.add))
                after("spot")
                for k in range(TOP):
                    inc(v.tensor_tensor(picked[:, k], hot[:, k], spot[:, :, :], ALU.mult))
                after("picked")
                inc(v.tensor_reduce(placef[:, :, :], picked[:, :, :, :], AX_X, ALU.add))
                after("placef")
                inc(v.tensor_copy(place[:, :, :], placef[:, :, :]))
                inc(v.tensor_tensor(past[:, :, :], ends[:, 3, :].unsqueeze(1).broadcast_to([P, TILES, E]),
                                    iota_t[:, :].unsqueeze(2).broadcast_to([P, TILES, E]), ALU.is_le))
                after("past")
                inc(v.tensor_reduce(ownerf[:, :], past[:, :, :], AX_X, ALU.add))
                after("ownerf")
                inc(v.tensor_scalar(ownerf[:, :], ownerf[:, :], float(E - 1), None, ALU.min))
                after("ownermin")
                inc(v.tensor_copy(owner[:, :], ownerf[:, :]))
                assert done[0] == at["owner"]
                after("owner")


def experts(nc, res_x, ident, W1, W2, Wg, Wl, W3, Bias, b3, XG, YG, xn, share, comb, place, owner, out):
    with ExitStack() as ctx:
        sb = lambda n, s, d: ctx.enter_context(nc.sbuf_tensor(n, s, d))
        ps = lambda n, s: ctx.enter_context(nc.psum_tensor(n, s, F32))
        sem = lambda n: ctx.enter_context(nc.semaphore(n))
        A = 2 * DC * F
        G = 2 * FC * F
        Y = FC * DIM
        wr = sb("wr", [P, A + G + Y], F32)
        wh = sb("wh", [P, 2, A + G + Y], F32R)
        wl = sb("wl", [P, 2, A + G + Y], F32R)
        bias = sb("e_bias", [P, 2, BIASES], F32)
        halfg = sb("e_halfg", [P, 2, FC], F32)
        xg = sb("e_xg", [P, 2, MT // P, DIM], F32)
        xf = sb("e_xf", [P, DC, MT], F32)
        xh = sb("e_xh", [P, DC, MT], F32R)
        xl = sb("e_xl", [P, DC, MT], F32R)
        x1 = sb("e_x1", [P, 2, MT], F32)
        assert MT == DIM and 2 * FC == TT
        z, o = xn[:, 0:FC, :], xn[:, FC:2 * FC, :]
        zh = sb("e_zh", [P, 2, FC, MT], F32R)
        zl = sb("e_zl", [P, 2, FC, MT], F32R)
        tanh = sb("e_tanh", [P, 2, MT], F32)
        g = sb("e_g", [P, 2, MT], F32)
        u = sb("e_u", [P, 2, MT], F32)
        oh = sb("e_oh", [P, FC, MT], F32R)
        ol = sb("e_ol", [P, FC, MT], F32R)
        y = sb("e_y", [P, MT // P, DIM], F32)
        pp = ps("pp", [P, FC, 2, MT])
        pt = ps("pt", [P, DC, MT])
        py = ps("py", [P, MT // P, DIM])

        sent = sem("e_sent")
        w_in = [sem(f"e_w_in{n}") for n in range(4)]
        x_in, bx_in, bg_in = ([sem(f"e_{n}{b}") for b in range(2)] for n in ("x_in", "bx_in", "bg_in"))
        y_out = sem("e_y_out")
        w_high, w_low = [sem(f"e_w_high{n}") for n in range(4)], [sem(f"e_w_low{n}") for n in range(4)]
        b_half = sem("e_b_half")
        turned, x_copied, x_high, x_low = sem("e_turned"), sem("e_x_copied"), sem("e_x_high"), sem("e_x_low")
        x_made, x1_done, z_done, z_high, z_low = (sem("e_x_made"), sem("e_x1_done"), sem("e_z_done"),
                                                  sem("e_z_high"), sem("e_z_low"))
        g_made, g_done, u_done, o_done, o_high, o_low = (sem("e_g_made"), sem("e_g_done"), sem("e_u_done"),
                                                         sem("e_o_done"), sem("e_o_high"), sem("e_o_low"))
        tanh_done = sem("e_tanh_done")
        y_made, y_copied = sem("e_y_made"), sem("e_y_copied")
        parts = [slice(0, A), slice(A, A + G // 2), slice(A + G // 2, A + G), slice(A + G, A + G + Y)]

        def w1(w, b, k, c, f):
            return w[:, b, (k * DC + c) * F + f * P:(k * DC + c) * F + (f + 1) * P]

        def wgl(w, b, k, c, f):
            return w[:, b, A + (k * FC + c) * F + f * P:A + (k * FC + c) * F + (f + 1) * P]

        def w3(w, b, c):
            return w[:, b, A + G + c * DIM:A + G + (c + 1) * DIM]

        def tiles(eng, step):
            step(-1, 1, -1)
            step(0, 0, 0)
            step(1, 1, 0)
            step(2, 0, 1)
            with eng.Fori(1, (TILES - 3) // 2) as r:
                step(2 * r + 1, 1, r)
                step(2 * r + 2, 0, r + 1)
            step(TILES - 2, 1, TILES // 2 - 1)
            step(TILES - 1, 0, TILES // 2)
            step(TILES, 1, TILES // 2)

        def on(i):
            return not isinstance(i, int) or 0 <= i < TILES

        with nc.Block() as block:
            @block.sync
            def _(sp):
                def expert(i):
                    return sp.value_load(owner[0:1, bass.ds(i, 1)], min_val=0, max_val=E - 1)

                def rows_and_biases(i, b, e):
                    wait(sp, turned, i - 1)
                    sp.dma_start(xg[:, b], XG[bass.ds(i * MT, MT), :].rearrange("(t p) d -> p t d", p=P)
                                 ).then_inc(x_in[b], 16)
                    wait(sp, z_done, FC * (i - 1))
                    sp.dma_start(bias[:, b, 0:2 * FC], Bias[bass.ds(e, 1), :, 0:2 * FC].rearrange("a p n -> (a p) n")
                                 ).then_inc(bx_in[b], 16)

                def gate_biases(i, b, e):
                    wait(sp, o_done, FC * (i - 1))
                    sp.dma_start(bias[:, b, 2 * FC:], Bias[bass.ds(e, 1), :, 2 * FC:].rearrange("a p n -> (a p) n")
                                 ).then_inc(bg_in[b], 16)

                def weights(i, n, e):
                    wait(sp, w_low[n], i)
                    ws, rows_, width = [((W1, W2), DC, F), ((Wg,), FC, F), ((Wl,), FC, F), ((W3,), FC, DIM)][n]
                    at = parts[n].start
                    for k, w in enumerate(ws):
                        to = wr[:, at + k * rows_ * width:at + (k + 1) * rows_ * width]
                        sp.dma_start(to.rearrange("p (c f) -> p c f", c=rows_),
                                     w[bass.ds(e, 1)].rearrange("a (c p) f -> p (a c) f", p=P)).then_inc(w_in[n], 16)

                def step(i, b, h):
                    if on(i + 1):
                        gate_biases(i + 1, 1 - b, expert(i + 1))
                    if on(i + 2):
                        e = expert(i + 2)
                        rows_and_biases(i + 2, b, e)
                        weights(i + 2, 0, e)
                        weights(i + 2, 1, e)
                    if on(i - 1):
                        sp.wait_ge(y_copied, i)
                        sp.dma_start(YG[bass.ds((i - 1) * MT, MT), :].rearrange("(t p) d -> p t d", p=P), y[:, :, :]
                                     ).then_inc(y_out, 16)
                    if on(i + 2):
                        weights(i + 2, 2, e)
                        weights(i + 2, 3, e)

                e0 = expert(0)
                for n in range(4):
                    weights(0, n, e0)
                sp.wait_ge(sent, 16 * TT * TOP)
                rows_and_biases(0, 0, e0)
                tiles(sp, step)
                sp.wait_ge(y_out, 16 * TILES)

            @block.gpsimd
            def _(pool):
                for i in range(TT):
                    for k in range(TOP):
                        pool.indirect_dma_start(XG, bass.IndirectOffsetOnAxis(ap=place[:, k, i:i + 1], axis=0),
                                                xn[:, i, :], None).then_inc(sent, 16)

                def step(i, b, h):
                    if on(i + 1):
                        first = isinstance(i, int) and i == -1
                        for n in (2, 3) if first else (1, 2, 3):
                            pool.wait_ge(w_high[n], i + 2)
                            pool.tensor_tensor(wl[:, 1 - b, parts[n]], wr[:, parts[n]],
                                               wh[:, 1 - b, parts[n]].bitcast(F32), ALU.subtract).then_inc(w_low[n], 1)

                tiles(pool, step)

            @block.tensor
            def _(pe):
                def first(i, b, h):
                    if not on(i):
                        return
                    pe.wait_ge(x_in[b], 16 * (h + 1))
                    wait(pe, x_copied, i)
                    for t in range(MT // P):
                        for c in range(DC):
                            m = pe.transpose(pt[:, c, t * P:(t + 1) * P], xg[:, b, t, c * P:(c + 1) * P], ident[:, :])
                    m.then_inc(turned, 1)

                def products(i, b):
                    if not on(i):
                        return
                    pe.wait_ge(x_low, i + 1)
                    pe.wait_ge(w_low[0], i + 1)
                    for f in range(FC):
                        wait(pe, o_done, FC * (i - 2) + f + 1)
                        if isinstance(i, int) and i == 1:
                            pe.wait_ge(z_done, f + 1)
                        for k in range(2):
                            for c in range(DC):
                                m = three_passes(pe, pp[:, f, k, :], w1(wh, b, k, c, f), w1(wl, b, k, c, f),
                                                 xh[:, c, :], xl[:, c, :], c == 0, c == DC - 1)
                        m.then_inc(x_made, 1)

                def outputs(i, b):
                    if not on(i):
                        return
                    pe.wait_ge(o_low, 2 * (i + 1))
                    pe.wait_ge(w_low[3], i + 1)
                    wait(pe, y_copied, i)
                    for t in range(MT // P):
                        for c in range(FC):
                            m = three_passes(pe, py[:, t, :], oh[:, c, t * P:(t + 1) * P], ol[:, c, t * P:(t + 1) * P],
                                             w3(wh, b, c), w3(wl, b, c), c == 0, c == FC - 1)
                    m.then_inc(y_made, 1)

                def gate(i, b):
                    if not on(i):
                        return
                    pe.wait_ge(w_low[1], i + 1)
                    pe.wait_ge(w_low[2], i + 1)
                    pe.wait_ge(z_low, 2 * (i + 1))
                    for f in range(FC):
                        if not isinstance(i, int) or i + 1 < TILES:
                            pe.wait_ge(z_done, FC * (i + 1) + f + 1)
                        else:
                            wait(pe, o_done, FC * (i - 1) + f + 1)
                        for k in range(2):
                            for c in range(FC):
                                m = three_passes(pe, pp[:, f, k, :], wgl(wh, b, k, c, f), wgl(wl, b, k, c, f),
                                                 zh[:, b, c, :], zl[:, b, c, :], c == 0, c == FC - 1)
                        m.then_inc(g_made, 1)

                def step(i, b, h):
                    products(i + 1, 1 - b)
                    outputs(i - 1, 1 - b)
                    first(i + 2, b, h + 1)
                    gate(i, b)

                first(0, 0, 0)
                tiles(pe, step)

            @block.scalar
            def _(act):
                def first(i, b):
                    if not on(i):
                        return
                    act.wait_ge(turned, i + 1)
                    wait(act, x_low, i)
                    act.activation(xf[:, :, :], pt[:, :, :], ACT.Copy).then_inc(x_copied, 1)

                def high(i, b, n):
                    if not on(i):
                        return
                    act.wait_ge(w_in[n], (32 if n == 0 else 16) * (i + 1))
                    used, each = [(x_made, FC), (g_made, FC), (g_made, FC), (y_made, 1)][n]
                    wait(act, used, each * (i - 1))
                    act.activation(wh[:, b, parts[n]], wr[:, parts[n]], ACT.Copy).then_inc(w_high[n], 1)

                def step(i, b, h):
                    if on(i + 1):
                        for f in range(FC):
                            act.wait_ge(x_made, FC * (i + 1) + f + 1)
                            if f == 0:
                                act.wait_ge(bx_in[1 - b], 16 * (h + 1 if b == 0 else h + 2))
                            wait(act, z_done, FC * (i + 1) + f - 1)
                            act.activation(x1[:, f % 2, :], pp[:, f, 0, :], ACT.Identity,
                                           bias=bias[:, 1 - b, f:f + 1]).then_inc(x1_done, 1)
                    after_first = not isinstance(i, int) or i >= 0
                    if after_first:
                        high(i + 1, 1 - b, 1)
                    first(i + 2, b)
                    if after_first:
                        high(i + 1, 1 - b, 2)
                    high(i + 2, b, 0)
                    if on(i - 1):
                        act.wait_ge(y_made, i)
                        wait(act, y_out, 16 * (i - 1))
                        act.activation(y[:, :, :], py[:, :, :], ACT.Copy).then_inc(y_copied, 1)
                    if after_first:
                        high(i + 1, 1 - b, 3)
                    if on(i):
                        for f in range(FC):
                            act.wait_ge(g_made, FC * i + f + 1)
                            if f == 0:
                                act.wait_ge(b_half, i + 1)
                            wait(act, u_done, FC * i + f - 1)
                            act.activation(tanh[:, f % 2, :], pp[:, f, 0, :], ACT.Tanh, scale=0.5,
                                           bias=halfg[:, b, f:f + 1]).then_inc(tanh_done, 1)
                            act.activation(g[:, f % 2, :], pp[:, f, 0, :], ACT.Identity,
                                           bias=bias[:, b, 2 * FC + f:2 * FC + f + 1]).then_inc(g_done, 1)

                for n in range(4):
                    high(0, 0, n)
                first(0, 0)
                tiles(act, step)

            @block.vector
            def _(v):
                def first(i, b):
                    if not on(i):
                        return
                    v.wait_ge(x_copied, i + 1)
                    wait(v, x_made, FC * i)
                    v.tensor_copy(xh[:, :, :], xf[:, :, :]).then_inc(x_high, 1)
                    v.wait_ge(x_high, i + 1)
                    v.tensor_tensor(xl[:, :, :], xf[:, :, :], xh[:, :, :].bitcast(F32), ALU.subtract
                                    ).then_inc(x_low, 1)

                def low(i, b):
                    if not on(i):
                        return
                    v.wait_ge(w_high[0], i + 1)
                    v.tensor_tensor(wl[:, b, parts[0]], wr[:, parts[0]], wh[:, b, parts[0]].bitcast(F32), ALU.subtract
                                    ).then_inc(w_low[0], 1)

                def halves(i, b, h):
                    if not on(i):
                        return
                    v.wait_ge(bg_in[b], 16 * (h + 1))
                    wait(v, tanh_done, FC * (i - 1))
                    v.tensor_scalar(halfg[:, b], bias[:, b, 2 * FC:3 * FC], 0.5, None, ALU.mult).then_inc(b_half, 1)

                def step(i, b, h):
                    if on(i + 1):
                        for f in range(FC):
                            v.wait_ge(x1_done, FC * (i + 1) + f + 1)
                            wait(v, z_low, 2 * (i + 1) + f // 2 - 1)
                            v.scalar_tensor_tensor(out=z[:, f, :], in0=pp[:, f, 1, :],
                                                   scalar=bias[:, 1 - b, FC + f:FC + f + 1], in1=x1[:, f % 2, :],
                                                   op0=ALU.add, op1=ALU.mult).then_inc(z_done, 1)
                            if f % 2:
                                pair = f // 2
                                w = slice(f - 1, f + 1)
                                v.wait_ge(z_done, FC * (i + 1) + f + 1)
                                wait(v, g_made, FC * i)
                                v.tensor_copy(zh[:, 1 - b, w, :], z[:, w, :]).then_inc(z_high, 1)
                                v.wait_ge(z_high, 2 * (i + 1) + pair + 1)
                                v.tensor_tensor(zl[:, 1 - b, w, :], z[:, w, :], zh[:, 1 - b, w, :].bitcast(F32),
                                                ALU.subtract).then_inc(z_low, 1)
                    halves(i + 1, 1 - b, h if b == 0 else h + 1)
                    first(i + 2, b)
                    low(i + 2, b)
                    if on(i):
                        for f in range(FC):
                            v.wait_ge(g_done, FC * i + f + 1)
                            wait(v, o_done, FC * i + f - 1)
                            v.scalar_tensor_tensor(out=u[:, f % 2, :], in0=tanh[:, f % 2, :], scalar=1.0,
                                                   in1=g[:, f % 2, :], op0=ALU.add, op1=ALU.mult).then_inc(u_done, 1)
                            v.wait_ge(u_done, FC * i + f + 1)
                            wait(v, o_low, 2 * i + f // 2 - 1)
                            v.scalar_tensor_tensor(out=o[:, f, :], in0=pp[:, f, 1, :],
                                                   scalar=bias[:, b, 3 * FC + f:3 * FC + f + 1], in1=u[:, f % 2, :],
                                                   op0=ALU.add, op1=ALU.mult).then_inc(o_done, 1)
                            if f % 2:
                                pair = f // 2
                                w = slice(f - 1, f + 1)
                                v.wait_ge(o_done, FC * i + f + 1)
                                wait(v, y_made, i)
                                v.tensor_copy(oh[:, w, :], o[:, w, :]).then_inc(o_high, 1)
                                v.wait_ge(o_high, 2 * i + pair + 1)
                                v.tensor_tensor(ol[:, w, :], o[:, w, :], oh[:, w, :].bitcast(F32), ALU.subtract
                                                ).then_inc(o_low, 1)

                low(0, 0)
                v.wait_ge(w_high[1], 1)
                v.tensor_tensor(wl[:, 0, parts[1]], wr[:, parts[1]], wh[:, 0, parts[1]].bitcast(F32), ALU.subtract
                                ).then_inc(w_low[1], 1)
                first(0, 0)
                tiles(v, step)

    with ExitStack() as ctx:
        sem = lambda n: ctx.enter_context(nc.semaphore(n))
        got = ctx.enter_context(nc.sbuf_tensor("f_got", [P, TT, TOP, DIM], F32))
        half = ctx.enter_context(nc.sbuf_tensor("f_half", [P, TOP, TT], F32))
        b3s = ctx.enter_context(nc.sbuf_tensor("f_b3", [E, DIM], F32))
        combT = ctx.enter_context(nc.sbuf_tensor("f_combT", [E, TT, P], F32))
        pc = ctx.enter_context(nc.psum_tensor("f_pc", [P, TT, P], F32))
        pb = ctx.enter_context(nc.psum_tensor("f_pb", [P, TT, DIM], F32))
        b3_in, c_turned, c_copied, b_made, b_added = (sem("f_b3_in"), sem("f_c_turned"), sem("f_c_copied"),
                                                      sem("f_b_made"), sem("f_b_added"))
        fetched = [sem(f"f_fetched{i}") for i in range(TT)]
        halved, mixed, stored = sem("f_halved"), sem("f_mixed"), sem("f_stored")

        with nc.Block() as block:
            @block.gpsimd
            def _(pool):
                for i in range(TT):
                    for k in range(TOP):
                        pool.indirect_dma_start(got[:, i, k, :], None, YG,
                                                bass.IndirectOffsetOnAxis(ap=place[:, k, i:i + 1], axis=0)
                                                ).then_inc(fetched[i], 16)

            @block.tensor
            def _(pe):
                for t in range(2):
                    for i in range(4 * t, 4 * t + 4):
                        m = pe.transpose(pc[0:E, i, :], comb[:, i, :], ident[:, :])
                    m.then_inc(c_turned, 1)
                pe.wait_ge(b3_in, 16)
                for i in range(TT):
                    pe.wait_ge(c_copied, i // 4 + 1)
                    pe.matmul(pb[:, i, :], combT[:, i, :], b3s[:, :], start=True, stop=True).then_inc(b_made, 1)

            @block.scalar
            def _(act):
                for t in range(2):
                    act.wait_ge(c_turned, t + 1)
                    act.activation(combT[:, 4 * t:4 * t + 4, :], pc[0:E, 4 * t:4 * t + 4, :], ACT.Copy
                                   ).then_inc(c_copied, 1)

            @block.vector
            def _(v):
                v.tensor_scalar(half[:, :, :], share[:, :, :], 0.5, None, ALU.mult).then_inc(halved, 1)
                v.wait_ge(halved, 1)
                for i in range(TT):
                    v.wait_ge(b_made, (i | 1) + 1)
                    v.tensor_tensor(res_x[:, i, :], res_x[:, i, :], pb[:, i, :], ALU.add).then_inc(b_added, 1)
                for i in range(TT):
                    v.wait_ge(b_added, i + 1)
                    v.wait_ge(fetched[i], 16 * TOP)
                    for k in range(TOP):
                        if k:
                            v.wait_ge(mixed, TOP * i + k)
                        v.scalar_tensor_tensor(out=res_x[:, i, :], in0=got[:, i, k, :], scalar=half[:, k, i:i + 1],
                                               in1=res_x[:, i, :], op0=ALU.mult, op1=ALU.add).then_inc(mixed, 1)

            @block.sync
            def _(sp):
                sp.dma_start(b3s[:, :], b3).then_inc(b3_in, 16)
                to = out.rearrange("b q d -> (b q) d").rearrange("(i p) d -> p i d", p=P)
                for i in range(TT):
                    sp.wait_ge(mixed, TOP * (i + 1))
                    sp.dma_start(to[:, i, :], res_x[:, i, :]).then_inc(stored, 16)
                sp.wait_ge(stored, 16 * TT)


def layer(nc, x, ctx_in, Wq, WkT, Wv, Wo, ln_g, ln_b, Wqkv, WoT, Wgate, bgate, W1, W2, Wg, Wl, W3, Bias, b3, out):
    scratch = lambda n, s: nc.dram_tensor(n, s, F32, kind="Internal").ap()
    QT = scratch("queries_scratch", (B, 2, P, DC, UH, NQ))
    OT = scratch("outputs_scratch", (B, 2, P, DC, UH, NQ))
    XG = scratch("routed_scratch", (ROWS, DIM))
    YG = scratch("expert_scratch", (ROWS, DIM))
    with ExitStack() as ctx:
        sb = lambda n, s, d: ctx.enter_context(nc.sbuf_tensor(n, s, d))
        sem = lambda n: ctx.enter_context(nc.semaphore(n))
        ident, ones, halfpow = sb("ident", [P, P], F32), sb("ones", [P, P], F32), sb("halfpow", [P, 16], F32)
        res_x = sb("res_x", [P, TT, DIM], F32)
        share = sb("share", [P, TOP, TT], F32)
        place = sb("place", [P, TOP, TT], U32)
        owner = sb("owner", [P, TILES], I32)
        constants(nc, ident, ones, halfpow, res_x, x, sem("zeroed"), sem("made"), sem("x_loaded"))
        spent, spent2 = [], []
        queries(nc, res_x, ident, halfpow, Wq, WkT, QT, spent)
        attend(nc, ident, ones, ctx_in, ln_g, ln_b, QT, OT, spent, spent2)
        project_out(nc, res_x, Wv, Wo, OT, spent2)
        self_attention(nc, res_x, ident, halfpow, Wqkv, WoT, XG)
        comb = sb("comb", [P, TT, E], F32)
        xn = sb("xn", [P, TT, DIM], F32)
        route(nc, res_x, ident, ones, halfpow, Wgate, bgate, xn, share, comb, place, owner)
        experts(nc, res_x, ident, W1, W2, Wg, Wl, W3, Bias, b3, XG, YG, xn, share, comb, place, owner, out)


def kernel(x, ctx_1024, L0_xattn_Wq, L0_xattn_Wkv, L0_xattn_Wo, L0_xattn_ln_g, L0_xattn_ln_b, L0_attn_q_heads,
           L0_attn_k_heads, L0_attn_v_heads, L0_attn_output_proj, L0_ffn_Wgate, L0_ffn_bgate, L0_ffn_W1, L0_ffn_b1,
           L0_ffn_W2, L0_ffn_b2, L0_ffn_Wg, L0_ffn_bg, L0_ffn_Wl, L0_ffn_bl, L0_ffn_W3, L0_ffn_b3):
    import numpy as np
    import concourse.bacc as bacc
    from concourse.bass_utils import run_bass_kernel_spmd

    inner = HEADS * DH
    by_column = lambda a: np.ascontiguousarray(a.reshape(-1, P).T)
    arrays = {
        "x": x, "ctx_in": ctx_1024, "Wq": L0_xattn_Wq,
        "WkT": L0_xattn_Wkv[:, :inner].T, "Wv": L0_xattn_Wkv[:, inner:], "Wo": L0_xattn_Wo,
        "ln_g": by_column(L0_xattn_ln_g), "ln_b": by_column(L0_xattn_ln_b),
        "Wqkv": np.stack([L0_attn_q_heads.T, L0_attn_k_heads.T, L0_attn_v_heads.T]),
        "WoT": L0_attn_output_proj.T, "Wgate": L0_ffn_Wgate, "bgate": L0_ffn_bgate,
        "W1": L0_ffn_W1, "W2": L0_ffn_W2, "Wg": L0_ffn_Wg, "Wl": L0_ffn_Wl, "W3": L0_ffn_W3,
        "Bias": np.concatenate([b.reshape(E, FC, P).transpose(0, 2, 1)
                                for b in (L0_ffn_b1, L0_ffn_b2, L0_ffn_bg, L0_ffn_bl)], axis=2),
        "b3": L0_ffn_b3,
    }
    nc = bacc.Bacc("TRN2", target_bir_lowering=False, num_devices=1)
    feed, args = {}, []
    for name, a in arrays.items():
        a = np.ascontiguousarray(a)
        feed[f"in_{name}"] = a
        args.append(nc.dram_tensor(f"in_{name}", a.shape, mybir.dt.from_np(a.dtype), kind="ExternalInput").ap())
    args.append(nc.dram_tensor("out_x", (B, NQ, DIM), F32, kind="ExternalOutput").ap())
    layer(nc, *args)
    r = run_bass_kernel_spmd(nc, [feed], core_ids=[0])
    return r.results[0]["out_x"]
```

```python
from contextlib import ExitStack

import concourse.bass as bass
from concourse import mybir

F32 = mybir.dt.float32
F32R = mybir.dt.float32r
U32 = mybir.dt.uint32
I32 = mybir.dt.int32
ALU = mybir.AluOpType
ACT = mybir.ActivationFunctionType
AX_X = mybir.AxisListType.X

P = 128
B, NQ, DIM = 16, 64, 256
NK = 1601
HEADS, DH = 16, 64
TOK = B * NQ
TT = TOK // P
DC = DIM // P
PAIRS = HEADS // 2
HALF = TOK // 2
UH = HEADS // 2
UQ = UH * NQ
UNITS = 2 * B
KT = -(-NK // P)
LAST = NK - (KT - 1) * P
EPS = 1e-5
SCALE = DH ** -0.5


def wait(eng, sem, value):
    if isinstance(value, int) and value <= 0:
        return
    eng.wait_ge(sem, value)


def rows(t):
    return LAST if t == KT - 1 else P


class LayerNorm:

    def __init__(self, nc, sb, ps, sem, tag, x, ident, halfpow, split, xn=None):
        self.nc, self.x, self.ident, self.halfpow, self.split = nc, x, ident, halfpow, split
        self.st = sb(f"{tag}_st", [P, TT, 6], F32)
        self.mv = sb(f"{tag}_mv", [P, TT, 2], F32)
        self.ve = sb(f"{tag}_ve", [P, TT], F32)
        self.rstd = sb(f"{tag}_rstd", [P, TT], F32)
        self.xn = sb(f"{tag}_xn", [P, TT, DIM], F32) if xn is None else xn
        self.hT = sb(f"{tag}_hT", [P, DC, TOK], F32)
        if split:
            self.hTh = sb(f"{tag}_hTh", [P, DC, TOK], F32R)
            self.hTl = sb(f"{tag}_hTl", [P, DC, TOK], F32R)
        self.ps = ps
        self.stats = sem(f"{tag}_stats")
        self.aggr = sem(f"{tag}_aggr")
        self.veps = sem(f"{tag}_veps")
        self.root = sem(f"{tag}_root")
        self.norm = sem(f"{tag}_norm")
        self.turned = sem(f"{tag}_turned")
        self.copied = sem(f"{tag}_copied")
        self.high = sem(f"{tag}_high")
        self.low = sem(f"{tag}_low")

    def vector_normalise(self, v, arrived=None):
        for i in range(TT):
            if arrived:
                v.wait_ge(arrived[i // 2], 16)
            v.bn_stats(self.st[:, i, :], self.x[:, i, :]).then_inc(self.stats, 1)
        for i in range(TT):
            v.wait_ge(self.stats, i + 1)
            v.bn_aggr(self.mv[:, i, :], self.st[:, i, :]).then_inc(self.aggr, 1)
        v.wait_ge(self.aggr, TT)
        v.tensor_scalar(self.ve[:, :], self.mv[:, :, 1], EPS, None, ALU.add).then_inc(self.veps, 1)
        v.wait_ge(self.root, 1)
        for i in range(TT):
            v.tensor_scalar(self.xn[:, i, :], self.x[:, i, :], self.mv[:, i, 0:1], self.rstd[:, i:i + 1],
                            ALU.subtract, ALU.mult).then_inc(self.norm, 1)

    def pool_root(self, pool):
        pool.wait_ge(self.veps, 1)
        pool.tensor_tensor(self.rstd[:, :], self.ve[:, :], self.halfpow[:, 0:TT], ALU.pow).then_inc(self.root, 1)

    def tensor_turn(self, pe):
        for th in range(2):
            for c in range(DC):
                for i in range(4):
                    pe.wait_ge(self.norm, 4 * th + i + 1)
                    m = pe.transpose(self.ps[:, 2 * th + c, i * P:(i + 1) * P],
                                     self.xn[:, 4 * th + i, c * P:(c + 1) * P], self.ident[:, :])
                m.then_inc(self.turned, 1)

    def scalar_copy(self, act):
        for th in range(2):
            for c in range(DC):
                act.wait_ge(self.turned, 2 * th + c + 1)
                act.activation(self.hT[:, c, th * HALF:(th + 1) * HALF], self.ps[:, 2 * th + c, :],
                               ACT.Copy).then_inc(self.copied, 1)

    def vector_split(self, v):
        for th in range(2):
            cols = slice(th * HALF, (th + 1) * HALF)
            v.wait_ge(self.copied, 2 * th + 2)
            v.tensor_copy(self.hTh[:, :, cols], self.hT[:, :, cols]).then_inc(self.high, 1)
            v.wait_ge(self.high, th + 1)
            v.tensor_tensor(self.hTl[:, :, cols], self.hT[:, :, cols], self.hTh[:, :, cols].bitcast(F32),
                            ALU.subtract).then_inc(self.low, 1)


def three_passes(pe, out, wh, wl, mh, ml, first, last, **more):
    pe.matmul(out, wl, mh, start=first, stop=False, **more)
    pe.matmul(out, wh, ml, start=False, stop=False, **more)
    return pe.matmul(out, wh, mh, start=False, stop=last, **more)


def constants(nc, ident, ones, halfpow, res_x, x, zeroed, made, x_in):
    with nc.Block() as block:
        @block.gpsimd
        def _(pool):
            pool.memset(ident[:, :], 0.0).then_inc(zeroed, 1)
            pool.memset(ones[:, :], 1.0).then_inc(made, 1)
            pool.memset(halfpow[:, :], -0.5).then_inc(made, 1)
            pool.wait_ge(zeroed, 1)
            pool.affine_select(out=ident[:, :], in_=ident[:, :], compare_op=ALU.not_equal, fill=1.0, base=0,
                               pattern=[[-1, P]], channel_multiplier=1).then_inc(made, 1)
            pool.wait_ge(made, 3)

        @block.sync
        def _(sp):
            tokens = x.rearrange("b q d -> (b q) d").rearrange("(i p) d -> p i d", p=P)
            for j in range(TT // 2):
                sp.dma_start(res_x[:, 2 * j:2 * j + 2, :], tokens[:, 2 * j:2 * j + 2, :]).then_inc(x_in[j], 16)


def collecting(nc, ctx, kept):
    def sem(name):
        kept.append(ctx.enter_context(nc.semaphore(name)))
        return kept[-1]
    return sem


def clear(pool, spent):
    for s in spent:
        pool.sem_clear(s)


class Context:

    def __init__(self, sb):
        self.raw = sb("raw", [P, KT, DIM], F32)
        self.nrm = sb("nrm", [P, KT, DIM], F32)
        self.st = sb("st", [P, KT, 6], F32)
        self.msum, self.mdif, self.vsum = (sb(n, [P, KT], F32) for n in ("msum", "mdif", "vsum"))
        self.ve, self.negmu = sb("ve", [P, KT], F32), sb("negmu", [P, KT], F32)
        self.rstd, self.shift = sb("rstd", [P, KT], F32), sb("shift", [P, KT], F32)

    def load(self, sp, ctx_in, n, t, arrived):
        sp.dma_start(self.raw[0:rows(t), t, :], ctx_in[n, t * P:t * P + rows(t), :]).then_inc(arrived, 16)

    def vector_moments(self, v, c_mom, c_ve, before):
        st, msum, mdif, vsum = self.st, self.msum, self.mdif, self.vsum
        v.tensor_tensor(msum[:, :], st[:, :, 1], st[:, :, 4], ALU.add).then_inc(c_mom, 1)
        v.tensor_tensor(mdif[:, :], st[:, :, 1], st[:, :, 4], ALU.subtract).then_inc(c_mom, 1)
        v.tensor_tensor(vsum[:, :], st[:, :, 2], st[:, :, 5], ALU.add).then_inc(c_mom, 1)
        v.wait_ge(c_mom, 5 * before + 3)
        v.tensor_scalar(self.negmu[:, :], msum[:, :], -0.5, None, ALU.mult).then_inc(c_ve, 1)
        v.tensor_tensor(mdif[:, :], mdif[:, :], mdif[:, :], ALU.mult).then_inc(c_mom, 1)
        v.tensor_scalar(vsum[:, :], vsum[:, :], 1.0 / DIM, EPS, ALU.mult, ALU.add).then_inc(c_mom, 1)
        v.wait_ge(c_mom, 5 * before + 5)
        v.scalar_tensor_tensor(out=self.ve[:, :], in0=mdif[:, :], scalar=0.25, in1=vsum[:, :],
                               op0=ALU.mult, op1=ALU.add).then_inc(c_ve, 1)

    def pool_root(self, pool, halfpow, c_rstd, c_shift, before):
        pool.tensor_tensor(self.rstd[:, :], self.ve[:, :], halfpow[:, 0:KT], ALU.pow).then_inc(c_rstd, 1)
        pool.wait_ge(c_rstd, before + 1)
        pool.tensor_tensor(self.shift[:, :], self.negmu[:, :], self.rstd[:, :], ALU.mult).then_inc(c_shift, 1)


def queries(nc, res_x, x_in, ident, halfpow, Wq, WkT, QT, ctx_in, cx, spent):
    with ExitStack() as ctx:
        sb = lambda n, s, d: ctx.enter_context(nc.sbuf_tensor(n, s, d))
        sem = collecting(nc, ctx, spent)
        bank = ctx.enter_context(nc.psum_tensor("q_banks", [P, 8, HALF], F32))
        ln = LayerNorm(nc, sb, bank[:, 0:4, :], sem, "ln1", res_x, ident, halfpow, True)
        wq = sb("wq", [P, DC, HEADS * DH], F32)
        wqh = sb("wqh", [P, DC, HEADS * DH], F32R)
        wql = sb("wql", [P, DC, HEADS * DH], F32R)
        wk = sb("wk", [P, PAIRS, DIM], F32)
        wkh = sb("wkh", [P, PAIRS, 2, DIM], F32R)
        wkl = sb("wkl", [P, PAIRS, 2, DIM], F32R)
        qf = sb("qf", [P, 2, TOK], F32)
        qh = sb("qh", [P, 2, TOK], F32R)
        ql = sb("ql", [P, 2, TOK], F32R)
        stage = sb("stage", [P, 2, 2, DC, B // 2, 2, NQ], F32)

        wq_in, wk_in = sem("wq_in"), sem("wk_in")
        wq_high, wq_low = sem("wq_high"), sem("wq_low")
        wk_zero, wk_high, wk_low = sem("wk_zero"), sem("wk_high"), sem("wk_low")
        q_made, q_copied, q_high, q_low = sem("q_made"), sem("q_copied"), sem("q_high"), sem("q_low")
        k_made, k_act, k_dve = sem("k_made"), sem("k_act"), sem("k_dve")
        stored = [sem("stored0"), sem("stored1")]
        raw_in, st_zero, st_made, c_mom, c_ve, c_rstd, c_shift = (
            sem("f_raw_in"), sem("f_st_zero"), sem("f_st_made"), sem("f_c_mom"), sem("f_c_ve"), sem("f_c_rstd"),
            sem("f_c_shift"))
        normed = sem("f_normed")
        pieces = [(th, hh, c) for th in range(2) for hh in range(2) for c in range(DC)]

        def low_keys(eng, hh):
            r = slice(hh * DH, (hh + 1) * DH)
            eng.wait_ge(wk_high, hh + 1)
            eng.tensor_tensor(wkl[r, :, hh, :], wk[r, :, :], wkh[r, :, hh, :].bitcast(F32), ALU.subtract
                              ).then_inc(wk_low, 1)

        with nc.Block() as block:
            @block.sync
            def _(sp):
                sp.dma_start(wq[:, :, :], Wq.rearrange("(c p) n -> p c n", p=P)).then_inc(wq_in, 16)
                sp.dma_start(wk[:, :, :], WkT.rearrange("(j p) d -> p j d", p=P)).then_inc(wk_in, 16)
                for t in range(KT):
                    cx.load(sp, ctx_in, 0, t, raw_in)
                for p in range(PAIRS):
                    hf, k = p // (PAIRS // 2), p % (PAIRS // 2)
                    for th in range(2):
                        sp.wait_ge(k_act, 4 * p + 2 * (th + 1))
                        sp.wait_ge(k_dve, 4 * p + 2 * (th + 1))
                        for c in range(DC):
                            dst = QT[th * B // 2:(th + 1) * B // 2, hf, :, c, 2 * k:2 * k + 2, :]
                            sp.dma_start(dst.rearrange("b p h t -> p b (h t)"),
                                         stage[:, p % 2, th, c].rearrange("p b h t -> p b (h t)")
                                         ).then_inc(stored[p % 2], 16)
                for s in stored:
                    sp.wait_ge(s, 16 * 4 * PAIRS // 2)

            @block.gpsimd
            def _(pool):
                pool.memset(wkh[:, :, :, :].bitcast(F32), 0.0).then_inc(wk_zero, 1)
                ln.pool_root(pool)
                pool.wait_ge(wq_high, 1)
                pool.tensor_tensor(wql[:, :, :], wq[:, :, :], wqh[:, :, :].bitcast(F32), ALU.subtract
                                   ).then_inc(wq_low, 1)
                pool.memset(wkl[:, :, :, :].bitcast(F32), 0.0).then_inc(wk_zero, 1)
                pool.wait_ge(wk_zero, 2)
                low_keys(pool, 0)
                pool.memset(cx.st[:, :, :], 0.0).then_inc(st_zero, 1)
                pool.wait_ge(c_ve, 2)
                cx.pool_root(pool, halfpow, c_rstd, c_shift, 0)

            @block.tensor
            def _(pe):
                ln.tensor_turn(pe)

                def project(p):
                    for th in range(2):
                        if p >= 1:
                            pe.wait_ge(q_copied, 2 * (p - 1) + th + 1)
                        else:
                            pe.wait_ge(ln.low, th + 1)
                        for c in range(DC):
                            w = slice(p * P, (p + 1) * P)
                            t = slice(th * HALF, (th + 1) * HALF)
                            m = three_passes(pe, bank[:, 4 + th, :], wqh[:, c, w], wql[:, c, w],
                                             ln.hTh[:, c, t], ln.hTl[:, c, t], c == 0, c == DC - 1)
                        m.then_inc(q_made, 1)

                pe.wait_ge(wq_low, 1)
                project(0)
                for p in range(PAIRS):
                    if p + 1 < PAIRS:
                        project(p + 1)
                    if p == 0:
                        pe.wait_ge(wk_low, 2)
                    pe.wait_ge(q_low, p + 1)
                    for n, (th, hh, c) in enumerate(pieces):
                        g = len(pieces) * p + n
                        if g >= 4:
                            pe.wait_ge(k_act if g % 2 == 0 else k_dve, (g - 4) // 2 + 1)
                        t = slice(th * HALF, (th + 1) * HALF)
                        w = slice(c * P, (c + 1) * P)
                        three_passes(pe, bank[:, g % 4, :], wkh[:, p, hh, w], wkl[:, p, hh, w],
                                     qh[:, p % 2, t], ql[:, p % 2, t], True, True).then_inc(k_made, 1)

            def take(eng, copy, p, parity, mine):
                for n, (th, hh, c) in enumerate(pieces):
                    if n % 2 != parity:
                        continue
                    g = len(pieces) * p + n
                    eng.wait_ge(k_made, g + 1)
                    if p >= 2:
                        eng.wait_ge(stored[p % 2], 64 * (p // 2))
                    copy(stage[:, p % 2, th, c, :, hh, :],
                         bank[:, g % 4, :].rearrange("p (b t) -> p b t", t=NQ)).then_inc(mine, 1)

            @block.scalar
            def _(act):
                act.wait_ge(wq_in, 16)
                act.activation(wqh[:, :, :], wq[:, :, :], ACT.Copy).then_inc(wq_high, 1)
                ln.scalar_copy(act)
                act.wait_ge(wk_in, 16)
                act.wait_ge(wk_zero, 1)
                for hh in range(2):
                    r = slice(hh * DH, (hh + 1) * DH)
                    act.activation(wkh[r, :, hh, :], wk[r, :, :], ACT.Copy).then_inc(wk_high, 1)

                def copy_q(p):
                    for th in range(2):
                        act.wait_ge(q_made, 2 * p + th + 1)
                        if p >= 2:
                            act.wait_ge(q_low, p - 1)
                        act.activation(qf[:, p % 2, th * HALF:(th + 1) * HALF], bank[:, 4 + th, :],
                                       ACT.Copy).then_inc(q_copied, 1)

                copy_q(0)
                for p in range(PAIRS):
                    if p + 1 < PAIRS:
                        copy_q(p + 1)
                    take(act, lambda o, i: act.activation(o, i, ACT.Copy), p, 0, k_act)

            @block.vector
            def _(v):
                ln.vector_normalise(v, x_in)
                ln.vector_split(v)

                def split_q(p):
                    v.wait_ge(q_copied, 2 * p + 2)
                    if p >= 2:
                        v.wait_ge(k_made, len(pieces) * (p - 1))
                    v.tensor_copy(qh[:, p % 2, :], qf[:, p % 2, :]).then_inc(q_high, 1)
                    v.wait_ge(q_high, p + 1)
                    v.tensor_tensor(ql[:, p % 2, :], qf[:, p % 2, :], qh[:, p % 2, :].bitcast(F32),
                                    ALU.subtract).then_inc(q_low, 1)

                v.wait_ge(wk_zero, 2)
                low_keys(v, 1)
                split_q(0)
                for p in range(PAIRS):
                    if p + 1 < PAIRS:
                        split_q(p + 1)
                    take(v, v.tensor_copy, p, 1, k_dve)
                    if p == 2:
                        v.wait_ge(raw_in, 16 * KT)
                        v.wait_ge(st_zero, 1)
                    if 2 <= p < 5:
                        for t in range(5 * (p - 2), min(5 * (p - 1), KT)):
                            v.bn_stats(cx.st[0:rows(t), t, :], cx.raw[0:rows(t), t, :]).then_inc(st_made, 1)
                    if p == 4:
                        v.wait_ge(st_made, KT)
                        cx.vector_moments(v, c_mom, c_ve, 0)
                    if p >= 6:
                        v.wait_ge(c_shift, 1)
                        for t in range(7 * (p - 6), min(7 * (p - 5), KT)):
                            m = rows(t)
                            v.tensor_scalar(cx.nrm[0:m, t, :], cx.raw[0:m, t, :], cx.rstd[0:m, t:t + 1],
                                            cx.shift[0:m, t:t + 1], ALU.mult, ALU.add).then_inc(normed, 1)
                v.wait_ge(normed, KT)



SLOTS = 2 * KT
LAG = KT + 8
RING = 5


def ring(t):
    return RING - 1 if t == KT - 1 else t % (RING - 1)


class Step:

    def __init__(self, r, c):
        self.r, self.c = r, c

    def back(self, n):
        c = self.c - n
        r = self.r + c // SLOTS
        c = c % SLOTS
        if isinstance(r, int) and not 0 <= r < B:
            return None
        return r, c // KT, c % KT

    def unit(self, start):
        c = self.c - start
        if c % KT:
            return None
        r = self.r + c // SLOTS
        if isinstance(r, int) and not 0 <= r < B:
            return None
        return r, c % SLOTS // KT

    def batch(self, at):
        c = self.c - at
        n = self.r + c // SLOTS
        return [n] if c % SLOTS == 0 and (not isinstance(n, int) or 0 <= n < B) else []

    def context(self, at):
        found = []
        for t in range(KT):
            c = self.c - at(t)
            if c % SLOTS == 0:
                n = self.r + c // SLOTS
                if not isinstance(n, int) or 0 <= n < B:
                    found.append((n, t))
        return found


def clock(eng, step):
    for c in range(-2 * SLOTS, 2 * SLOTS):
        step(Step(0, c))
    with eng.Fori(2, B - 2) as r:
        for c in range(SLOTS):
            step(Step(r, c))
    for c in range(4 * SLOTS):
        step(Step(B - 2, c))


def spread(start):
    return lambda t: start + 5 * t // 3


def value_weights(cx):
    return cx.raw[:, 0:DC * HEADS * DH // DIM, :].rearrange("p a b -> p (a b)").rearrange(
        "p (c h d) -> p c h d", c=DC, h=HEADS)


def output_weights(cx):
    return cx.nrm[:, 0:PAIRS, :]


def attend(nc, ident, ones, halfpow, ctx_in, cx, ln_g, ln_b, QT, OT, Wv, Wo, weights_in, earlier, spent):
    with ExitStack() as ctx:
        sb = lambda n, s, d: ctx.enter_context(nc.sbuf_tensor(n, s, d))
        ps = lambda n, s: ctx.enter_context(nc.psum_tensor(n, s, F32))
        sem = collecting(nc, ctx, spent)
        raw, nrm, st, rstd, shift = cx.raw, cx.nrm, cx.st, cx.rstd, cx.shift
        ch = sb("ch", [P, KT, DIM], F32R)
        cl = sb("cl", [P, KT, DIM], F32R)
        tf = sb("tf", [P, 3, DC, P], F32)
        th = sb("th", [P, KT, DC, P], F32R)
        tl = sb("tl", [P, KT, DC, P], F32R)
        gain = sb("gain", [P, DC], F32)
        bias = sb("bias", [P, DC], F32)
        qr = sb("qr", [P, DC, UQ], F32)
        qh = sb("qsh", [P, 2, DC, UQ], F32R)
        ql = sb("qsl", [P, 2, DC, UQ], F32R)
        s = sb("s", [P, 2, KT, UQ], F32)
        ph = sb("ph", [P, RING, UQ], F32R)
        pl = sb("pl", [P, RING, UQ], F32R)
        top = sb("top", [P, UQ], F32)
        col = {"top": sb("top_col_s", [P, 4], F32), "inv": sb("inv_col_s", [P, 4], F32)}
        col_h, col_l = sb("col_h", [P, 4], F32R), sb("col_l", [P, 4], F32R)
        diag_h, diag_l = sb("diag_h", [P, 4, P], F32R), sb("diag_l", [P, 4, P], F32R)
        ones_r = sb("ones_r", [P, P], F32R)
        most = sb("most", [P, 2, UQ], F32)
        total = sb("total", [P, 2, UQ], F32)
        inv = sb("inv", [P, UQ], F32)
        o = sb("o", [P, 2, DC, UQ], F32)
        score = ps("score", [P, 2, UQ])
        acc = ps("acc", [P, 2, DC, UQ])
        turn = ps("turn", [P, DC, P])
        misc = ps("misc", [P, 4, P])

        raw_in = [sem(f"raw_in{t}") for t in range(KT)]
        gb_in, q_in = sem("gb_in"), sem("q_in")
        o_out = [sem("o_out0"), sem("o_out1")]
        c_stats, c_mom, c_ve, c_rstd, c_shift = sem("c_stats"), sem("c_mom"), sem("c_ve"), sem("c_rstd"), sem("c_shift")
        c_norm, c_turn, c_gain = sem("c_norm"), sem("c_turn"), sem("c_gain")
        t_high, t_low, r_high, r_low = sem("t_high"), sem("t_low"), sem("r_high"), sem("r_low")
        q_high, q_low = sem("qs_high"), sem("qs_low")
        scored, copied, maxed = sem("scored"), sem("copied"), sem("maxed")
        top_turned, top_col, top_spread, top_row = sem("top_turned"), sem("top_col"), sem("top_spread"), sem("top_row")
        shifted, expd, p_high, p_low, summed = sem("shifted"), sem("expd"), sem("p_high"), sem("p_low"), sem("summed")
        ones_made = sem("ones_made")
        col_high, col_low, diag_high, diag_low = ({n: sem(f"{n}_{kind}") for n in ("top", "inv")} for kind in (
            "col_high", "col_low", "diag_high", "diag_low"))
        multiplied, sum_col, inverted, inv_spread, inv_row, scaled, biased = (
            sem("multiplied"), sem("sum_col"), sem("inverted"), sem("inv_spread"), sem("inv_row"), sem("scaled"),
            sem("biased"))

        slot = lambda r, u, t: SLOTS * r + KT * u + t
        unit = lambda r, u: 2 * r + u
        tile = lambda n, t: KT * n + t
        at_norm, at_turn, at_split = spread(-12), spread(-11), spread(-10)
        at_raw = lambda t: spread(-11)(t) - SLOTS
        at_stats = lambda t: t - 27
        at_root = -14
        at_rows = spread(LAG - KT + 1)

        def later(found):
            return [f for f in found if not (isinstance(f[0], int) and f[0] == 0)]

        def split_column(v, n, i):
            v.wait_ge({"top": top_col, "inv": inverted}[n], i + 1)
            other_used(v, n, i)
            v.tensor_copy(col_h[:, :], col[n][:, :]).then_inc(col_high[n], 1)
            v.wait_ge(col_high[n], i + 1)
            v.tensor_tensor(col_l[:, :], col[n][:, :], col_h[:, :].bitcast(F32), ALU.subtract).then_inc(col_low[n], 1)
            v.wait_ge(col_low[n], i + 1)
            v.tensor_tensor(diag_l[:, :, :], ident[:, :].unsqueeze(1).broadcast_to([P, 4, P]),
                            col_l[:, :].bitcast(F32).unsqueeze(2).broadcast_to([P, 4, P]), ALU.mult
                            ).then_inc(diag_low[n], 1)

        def high_blocks(pool, n, i):
            pool.wait_ge(col_high[n], i + 1)
            pool.tensor_tensor(diag_h[:, :, :], ident[:, :].unsqueeze(1).broadcast_to([P, 4, P]),
                               col_h[:, :].bitcast(F32).unsqueeze(2).broadcast_to([P, 4, P]), ALU.mult
                               ).then_inc(diag_high[n], 1)

        def other_used(v, n, i):
            if n == "top":
                wait(v, top_spread, i)
                wait(v, inv_spread, i - 1)
            else:
                v.wait_ge(top_spread, min(i + 2, UNITS) if isinstance(i, int) else i + 2)
                wait(v, inv_spread, i)

        def spread_column(pe, n, i, done):
            pe.wait_ge(diag_high[n], i + 1)
            pe.wait_ge(diag_low[n], i + 1)
            pe.matmul(misc[:, :, :], ones_r[:, :], diag_l[:, :, :], start=True, stop=False)
            pe.matmul(misc[:, :, :], ones_r[:, :], diag_h[:, :, :], start=False, stop=True).then_inc(done, 1)

        with nc.Block() as block:
            @block.sync
            def _(sp):
                sp.dma_start(gain[:, :], ln_g).then_inc(gb_in, 16)
                sp.dma_start(bias[:, :], ln_b).then_inc(gb_in, 16)

                def step(k):
                    for n, t in later(k.context(at_raw)):
                        wait(sp, c_norm, tile(n - 2, t) + 1)
                        cx.load(sp, ctx_in, n, t, raw_in[t])
                    if (f := k.unit(-9)):
                        r, u = f
                        wait(sp, q_low, unit(r, u))
                        sp.dma_start(qr[:, :, :], QT[r, u].rearrange("p c h t -> p c (h t)")).then_inc(q_in, 16)
                    if (f := k.unit(KT + LAG + 6)):
                        r, u = f
                        sp.wait_ge(biased, DC * (unit(r, u) + 1))
                        sp.dma_start(OT[r, u].rearrange("p c h t -> p c (h t)"), o[:, u]).then_inc(o_out[u], 16)
                        if isinstance(r, int) and r == B - 1 and u == 0:
                            sp.wait_ge(c_norm, KT * (B - 1))
                            sp.dma_start(value_weights(cx), Wv.rearrange("(c p) (h d) -> p c h d", p=P, d=DH)
                                         ).then_inc(weights_in, 16)
                            sp.wait_ge(r_low, KT * B)
                            sp.dma_start(output_weights(cx), Wo.rearrange("(j p) d -> p j d", p=P)
                                         ).then_inc(weights_in, 16)

                clock(sp, step)
                for u in range(2):
                    sp.wait_ge(o_out[u], 16 * B)
                sp.wait_ge(weights_in, 32)

            @block.gpsimd
            def _(pool):
                clear(pool, earlier)

                def step(k):
                    if (f := k.unit(KT + 2)):
                        high_blocks(pool, "top", unit(*f))
                    if (f := k.unit(KT + LAG + 1)):
                        high_blocks(pool, "inv", unit(*f))
                    for n, _ in later([(n, 0) for n in k.batch(at_root)]):
                        pool.wait_ge(c_ve, 2 * n)
                        wait(pool, c_norm, KT * (n - 1))
                        cx.pool_root(pool, halfpow, c_rstd, c_shift, n - 1)
                    if (f := k.unit(-5)):
                        r, u = f
                        pool.wait_ge(q_high, unit(r, u) + 1)
                        pool.tensor_tensor(ql[:, u], qr[:, :, :], qh[:, u].bitcast(F32), ALU.subtract
                                           ).then_inc(q_low, 1)
                    for n, t in k.context(at_split):
                        pool.wait_ge(t_high, tile(n, t) + 1)
                        pool.tensor_tensor(tl[:, t, :, 0:rows(t)], tf[:, 2 if t == KT - 1 else t % 2, :, 0:rows(t)],
                                           th[:, t, :, 0:rows(t)].bitcast(F32), ALU.subtract).then_inc(t_low, 1)
                    for n, t in k.context(at_rows):
                        pool.wait_ge(r_high, tile(n, t) + 1)
                        pool.tensor_tensor(cl[0:rows(t), t, :], nrm[0:rows(t), t, :],
                                           ch[0:rows(t), t, :].bitcast(F32), ALU.subtract).then_inc(r_low, 1)
                    if (f := k.back(LAG - 2)):
                        r, u, t = f
                        if t == 1:
                            wait(pool, sum_col, unit(r, u) - 1)
                            pool.wait_ge(expd, slot(r, u, t) + 1)
                            pool.tensor_tensor(total[:, u, :], s[:, u, 0, :], s[:, u, 1, :], ALU.add).then_inc(summed, 1)
                        elif t > 1:
                            pool.wait_ge(expd, slot(r, u, t) + 1)
                            pool.wait_ge(summed, (KT - 1) * unit(r, u) + t - 1)
                            pool.tensor_tensor(total[0:rows(t), u, :], total[0:rows(t), u, :], s[0:rows(t), u, t, :],
                                               ALU.add).then_inc(summed, 1)

                clock(pool, step)

            @block.tensor
            def _(pe):
                pe.wait_ge(ones_made, 1)

                def step(k):
                    if (f := k.back(0)):
                        r, u, t = f
                        if t == 0:
                            pe.wait_ge(q_low, unit(r, u) + 1)
                        if u == 0:
                            pe.wait_ge(t_low, tile(r, t) + 1)
                        wait(pe, copied, slot(r, u, t) - 1)
                        for c in range(DC):
                            m = three_passes(pe, score[0:rows(t), slot(0, u, t) % 2, :], th[:, t, c, 0:rows(t)],
                                             tl[:, t, c, 0:rows(t)], qh[:, u, c, :], ql[:, u, c, :],
                                             c == 0, c == DC - 1)
                        m.then_inc(scored, 1)
                    for n, t in k.context(at_turn):
                        wait(pe, c_norm, tile(n - 1, t) + 1)
                        wait(pe, c_gain, DC * tile(n, t))
                        for c in range(DC):
                            m = pe.transpose(turn[:, c, 0:rows(t)], nrm[0:rows(t), t, c * P:(c + 1) * P],
                                             ident[0:rows(t), 0:rows(t)])
                        m.then_inc(c_turn, 1)
                    if (f := k.back(LAG)):
                        r, u, t = f
                        if t == 0:
                            wait(pe, scaled, DC * (unit(r, u) - 1))
                        if u == 0:
                            pe.wait_ge(r_low, tile(r, t) + 1)
                        pe.wait_ge(p_low, slot(r, u, t) + 1)
                        n = rows(t)
                        for c in range(DC):
                            w = slice(c * P, (c + 1) * P)
                            m = three_passes(pe, acc[:, u, c, :], ch[0:n, t, w], cl[0:n, t, w],
                                             ph[0:n, ring(t), :], pl[0:n, ring(t), :], t == 0, t == KT - 1)
                        m.then_inc(multiplied, 1)
                    if (f := k.unit(KT + 1)):
                        r, u = f
                        pe.wait_ge(maxed, (KT - 1) * (unit(r, u) + 1))
                        wait(pe, inv_row, unit(r, u) - 1)
                        for q in range(4):
                            m = pe.transpose(misc[:, q, :], top[:, q * P:(q + 1) * P], ident[:, :])
                        m.then_inc(top_turned, 1)
                    if (f := k.unit(KT + 3)):
                        spread_column(pe, "top", unit(*f), top_spread)
                    if (f := k.unit(KT + LAG)):
                        r, u = f
                        pe.wait_ge(summed, (KT - 1) * (unit(r, u) + 1))
                        ahead = unit(r, u) + 2
                        pe.wait_ge(top_row, min(ahead, UNITS) if isinstance(r, int) else ahead)
                        for q in range(4):
                            m = pe.matmul(misc[:, 0, q:q + 1], total[:, u, q * P:(q + 1) * P], ones[:, 0:1],
                                          start=True, stop=True)
                        m.then_inc(sum_col, 1)
                    if (f := k.unit(KT + LAG + 2)):
                        spread_column(pe, "inv", unit(*f), inv_spread)

                clock(pe, step)

            @block.scalar
            def _(act):
                def step(k):
                    if (f := k.unit(KT + 4)):
                        r, u = f
                        act.wait_ge(top_spread, unit(r, u) + 1)
                        wait(act, shifted, KT * (unit(r, u) - 1))
                        act.activation(most[:, u, :], misc[:, :, :], ACT.Copy).then_inc(top_row, 1)
                    if (f := k.back(LAG - 2)):
                        r, u, t = f
                        n = rows(t)
                        act.wait_ge(expd, slot(r, u, t) + 1)
                        wait(act, multiplied, slot(r, u, t) - (RING - 2))
                        act.activation(ph[0:n, ring(t), :], s[0:n, u, t, :], ACT.Copy).then_inc(p_high, 1)
                    if (f := k.back(LAG - 3)):
                        r, u, t = f
                        n = rows(t)
                        act.wait_ge(shifted, slot(r, u, t) + 1)
                        act.activation(s[0:n, u, t, :], s[0:n, u, t, :], ACT.Exp, scale=SCALE).then_inc(expd, 1)
                    for n, t in later(k.context(at_norm)):
                        act.wait_ge(c_shift, n)
                        wait(act, r_low, tile(n - 1, t) + 1)
                        wait(act, c_turn, tile(n - 1, t) + 1)
                        m = rows(t)
                        act.activation(nrm[0:m, t, :], raw[0:m, t, :], ACT.Identity, bias=shift[0:m, t:t + 1],
                                       scale=rstd[0:m, t:t + 1]).then_inc(c_norm, 1)
                    if (f := k.back(0)):
                        r, u, t = f
                        n = rows(t)
                        act.wait_ge(scored, slot(r, u, t) + 1)
                        wait(act, p_low, slot(r - 1, u, t) + 1)
                        if t:
                            wait(act, summed, (KT - 1) * unit(r - 1, u) + t)
                        else:
                            wait(act, summed, (KT - 1) * unit(r - 1, u) + 1)
                        act.activation(s[0:n, u, t, :], score[0:n, slot(0, u, t) % 2, :], ACT.Copy
                                       ).then_inc(copied, 1)
                    for n, t in k.context(at_turn):
                        act.wait_ge(c_turn, tile(n, t) + 1)
                        if isinstance(n, int) and n == 0:
                            act.wait_ge(gb_in, 32)
                        wait(act, t_low, tile(n, t) - 1)
                        m = rows(t)
                        for c in range(DC):
                            act.activation(tf[:, 2 if t == KT - 1 else t % 2, c, 0:m], turn[:, c, 0:m], ACT.Identity,
                                           bias=bias[:, c:c + 1], scale=gain[:, c:c + 1]).then_inc(c_gain, 1)
                    if (f := k.unit(KT + LAG + 3)):
                        r, u = f
                        act.wait_ge(inv_spread, unit(r, u) + 1)
                        wait(act, scaled, DC * unit(r, u))
                        act.activation(inv[:, :], misc[:, :, :], ACT.Copy).then_inc(inv_row, 1)
                    if (f := k.unit(KT + LAG + 5)):
                        r, u = f
                        for c in range(DC):
                            act.wait_ge(scaled, DC * unit(r, u) + c + 1)
                            act.activation(o[:, u, c, :], o[:, u, c, :], ACT.Identity, bias=bias[:, c:c + 1],
                                           scale=gain[:, c:c + 1]).then_inc(biased, 1)

                clock(act, step)

            @block.vector
            def _(v):
                v.tensor_copy(ones_r[:, :], ones[:, :]).then_inc(ones_made, 1)

                def step(k):
                    if (f := k.unit(KT + 2)):
                        r, u = f
                        v.wait_ge(top_turned, unit(r, u) + 1)
                        v.tensor_reduce(col["top"][:, :], misc[:, :, :], AX_X, ALU.max).then_inc(top_col, 1)
                        split_column(v, "top", unit(r, u))
                    if (f := k.back(LAG - 4)):
                        r, u, t = f
                        n = rows(t)
                        if t == 0:
                            v.wait_ge(top_row, unit(r, u) + 1)
                        v.tensor_tensor(s[0:n, u, t, :], s[0:n, u, t, :], most[0:n, u, :], ALU.subtract
                                        ).then_inc(shifted, 1)
                    if (f := k.back(LAG - 1)):
                        r, u, t = f
                        n = rows(t)
                        v.wait_ge(p_high, slot(r, u, t) + 1)
                        v.tensor_tensor(pl[0:n, ring(t), :], s[0:n, u, t, :], ph[0:n, ring(t), :].bitcast(F32),
                                        ALU.subtract).then_inc(p_low, 1)
                    if (f := k.back(1)):
                        r, u, t = f
                        n = rows(t)
                        if t == 1:
                            wait(v, top_turned, unit(r, u))
                            v.wait_ge(copied, slot(r, u, t) + 1)
                            v.tensor_tensor(top[:, :], s[:, u, 0, :], s[:, u, 1, :], ALU.max).then_inc(maxed, 1)
                        elif t > 1:
                            v.wait_ge(copied, slot(r, u, t) + 1)
                            v.wait_ge(maxed, (KT - 1) * unit(r, u) + t - 1)
                            v.tensor_tensor(top[0:n, :], top[0:n, :], s[0:n, u, t, :], ALU.max).then_inc(maxed, 1)
                    if (f := k.unit(-5)):
                        r, u = f
                        v.wait_ge(q_in, 16 * (unit(r, u) + 1))
                        wait(v, scored, KT * (unit(r, u) - 1))
                        v.tensor_copy(qh[:, u], qr[:, :, :]).then_inc(q_high, 1)
                    for n, t in later(k.context(at_stats)):
                        m = rows(t)
                        v.wait_ge(raw_in[t], 16 * n)
                        wait(v, c_ve, 2 * (n - 1))
                        v.bn_stats(st[0:m, t, :], raw[0:m, t, :]).then_inc(c_stats, 1)
                    for n, _ in later([(n, 0) for n in k.batch(at_root)]):
                        v.wait_ge(c_stats, KT * n)
                        cx.vector_moments(v, c_mom, c_ve, n - 1)
                    for n, t in k.context(at_split):
                        m = rows(t)
                        v.wait_ge(c_gain, DC * (tile(n, t) + 1))
                        wait(v, scored, slot(n - 1, 1, t) + 1)
                        v.tensor_copy(th[:, t, :, 0:m], tf[:, 2 if t == KT - 1 else t % 2, :, 0:m]).then_inc(t_high, 1)
                    for n, t in k.context(at_rows):
                        m = rows(t)
                        wait(v, c_norm, tile(n - 1, t) + 1)
                        wait(v, multiplied, slot(n - 1, 1, t) + 1)
                        v.tensor_copy(ch[0:m, t, :], nrm[0:m, t, :]).then_inc(r_high, 1)
                    if (f := k.unit(KT + LAG + 1)):
                        r, u = f
                        v.wait_ge(sum_col, unit(r, u) + 1)
                        v.reciprocal(col["inv"][:, :], misc[:, 0, 0:4]).then_inc(inverted, 1)
                        split_column(v, "inv", unit(r, u))
                    if (f := k.unit(KT + LAG + 4)):
                        r, u = f
                        v.wait_ge(inv_row, unit(r, u) + 1)
                        v.wait_ge(multiplied, KT * (unit(r, u) + 1))
                        wait(v, o_out[u], 16 * r)
                        for c in range(DC):
                            v.tensor_tensor(o[:, u, c, :], acc[:, u, c, :], inv[:, :], ALU.mult).then_inc(scaled, 1)

                clock(v, step)


def project_out(nc, res_x, cx, OT, earlier):
    with ExitStack() as ctx:
        sb = lambda n, s, d: ctx.enter_context(nc.sbuf_tensor(n, s, d))
        ps = lambda n, s: ctx.enter_context(nc.psum_tensor(n, s, F32))
        sem = lambda n: ctx.enter_context(nc.semaphore(n))
        wv, wo = value_weights(cx), output_weights(cx)
        wvh = sb("wvh", [P, DC, HEADS, P], F32R)
        wvl = sb("wvl", [P, DC, HEADS, P], F32R)
        woh = sb("woh", [P, PAIRS, DIM], F32R)
        wol = sb("wol", [P, PAIRS, DIM], F32R)
        at = sb("at", [P, 2, 2, DC, B // 2, 2 * NQ], F32)
        ath = sb("ath", [P, 2, 2, DC, B // 2, 2 * NQ], F32R)
        atl = sb("atl", [P, 2, 2, DC, B // 2, 2 * NQ], F32R)
        vh = sb("vh", [P, 2, TOK], F32R)
        vl = sb("vl", [P, 2, TOK], F32R)
        pv = ps("pv", [P, 2, HALF])
        po = ps("po", [P, TT, DIM])
        h_zero, l_zero, wv_high, wv_low, wo_high, wo_low = (sem("h_zero"), sem("l_zero"), sem("wv_high"),
                                                            sem("wv_low"), sem("wo_high"), sem("wo_low"))
        at_in = [[sem(f"at_in{a}{b}") for b in range(2)] for a in range(2)]
        at_high, at_low = sem("at_high"), sem("at_low")
        v_made, v_high, v_low, out_made, added = (sem("v_made"), sem("v_high"), sem("v_low"), sem("out_made"),
                                                  sem("added"))
        out_used = sem("out_used")

        def group(g):
            return slice(g * HEADS // 2, (g + 1) * HEADS // 2)

        def side(w, g, hh):
            return w[:, :, group(g).start + hh:group(g).stop:2, hh * DH:(hh + 1) * DH]

        def plain(g, hh):
            return wv[:, :, group(g).start + hh:group(g).stop:2, :]

        with nc.Block() as block:
            @block.sync
            def _(sp):
                for p in range(PAIRS):
                    hf, k = p // (PAIRS // 2), p % (PAIRS // 2)
                    for t in range(2):
                        if p >= 2:
                            sp.wait_ge(at_low, 2 * (p - 2) + t + 1)
                        for c in range(DC):
                            src = OT[t * B // 2:(t + 1) * B // 2, hf, :, c, 2 * k:2 * k + 2, :]
                            sp.dma_start(at[:, p % 2, t, c], src.rearrange("b p h t -> p b (h t)")
                                         ).then_inc(at_in[p % 2][t], 16)

            @block.gpsimd
            def _(pool):
                for g in range(2):
                    pool.memset(wvh[:, :, group(g), :].bitcast(F32), 0.0).then_inc(h_zero, 1)
                clear(pool, earlier)
                pool.wait_ge(wo_high, 1)
                pool.tensor_tensor(wol[:, :, :], wo[:, :, :], woh[:, :, :].bitcast(F32), ALU.subtract
                                   ).then_inc(wo_low, 1)

            @block.tensor
            def _(pe):
                def values(p):
                    if p % (PAIRS // 2) == 0:
                        pe.wait_ge(wv_low, 2 * (p // (PAIRS // 2) + 1))
                    for t in range(2):
                        if p >= 1:
                            pe.wait_ge(v_low, 2 * (p - 1) + t + 1)
                        pe.wait_ge(at_low, 2 * p + t + 1)
                        for hh in range(2):
                            for c in range(DC):
                                m = three_passes(pe, pv[:, t, :], wvh[:, c, 2 * p + hh, :], wvl[:, c, 2 * p + hh, :],
                                                 ath[:, p % 2, t, c, :, hh * NQ:(hh + 1) * NQ],
                                                 atl[:, p % 2, t, c, :, hh * NQ:(hh + 1) * NQ],
                                                 hh == 0 and c == 0, hh == 1 and c == DC - 1)
                        m.then_inc(v_made, 1)

                values(0)
                for p in range(PAIRS):
                    if p + 1 < PAIRS:
                        values(p + 1)
                    if p == 0:
                        pe.wait_ge(wo_low, 1)
                    pe.wait_ge(v_low, 2 * p + 2)
                    for i in range(TT):
                        w = slice(i * P, (i + 1) * P)
                        m = three_passes(pe, po[:, i, :], vh[:, p % 2, w], vl[:, p % 2, w], woh[:, p, :], wol[:, p, :],
                                         p == 0 and i % 2 == 0, p == PAIRS - 1, skip_group_check=True)
                        if p == PAIRS - 1:
                            m.then_inc(out_made, 1)
                        elif i == TT - 1:
                            m.then_inc(out_used, 1)

            @block.scalar
            def _(act):
                def high_at(p, t):
                    act.wait_ge(at_in[p % 2][t], 32 * (p // 2 + 1))
                    if p >= 2:
                        act.wait_ge(v_made, 2 * (p - 2) + t + 1)
                    act.activation(ath[:, p % 2, t], at[:, p % 2, t], ACT.Copy).then_inc(at_high, 1)

                def high_weights(g):
                    act.wait_ge(h_zero, g + 1)
                    for hh in range(2):
                        act.activation(side(wvh, g, hh), plain(g, hh), ACT.Copy).then_inc(wv_high, 1)

                high_weights(0)
                for t in range(2):
                    high_at(0, t)
                high_at(1, 0)
                for p in range(PAIRS):
                    for t in range(2):
                        act.wait_ge(v_made, 2 * p + t + 1)
                        if p >= 2:
                            act.wait_ge(out_used, p - 1)
                        act.activation(vh[:, p % 2, t * HALF:(t + 1) * HALF], pv[:, t, :], ACT.Copy
                                       ).then_inc(v_high, 1)
                        if p == 0 and t == 0:
                            high_at(1, 1)
                        if p == 0 and t == 1:
                            act.activation(woh[:, :, :], wo[:, :, :], ACT.Copy).then_inc(wo_high, 1)
                            high_at(2, 0)
                            high_at(2, 1)
                        if 0 < p < PAIRS - 2:
                            high_at(p + 2, t)
                    if p == 1:
                        high_weights(1)

            @block.vector
            def _(v):
                def low_at(p, t):
                    v.wait_ge(at_high, 2 * p + t + 1)
                    v.tensor_tensor(atl[:, p % 2, t], at[:, p % 2, t], ath[:, p % 2, t].bitcast(F32),
                                    ALU.subtract).then_inc(at_low, 1)

                def low_weights(g):
                    v.wait_ge(l_zero, g + 1)
                    for hh in range(2):
                        v.wait_ge(wv_high, 2 * g + hh + 1)
                        v.tensor_tensor(side(wvl, g, hh), plain(g, hh), side(wvh, g, hh).bitcast(F32), ALU.subtract
                                        ).then_inc(wv_low, 1)

                v.memset(wvl[:, :, group(0), :].bitcast(F32), 0.0).then_inc(l_zero, 1)
                low_weights(0)
                for t in range(2):
                    low_at(0, t)
                low_at(1, 0)
                v.memset(wvl[:, :, group(1), :].bitcast(F32), 0.0).then_inc(l_zero, 1)
                for p in range(PAIRS):
                    for t in range(2):
                        cols = slice(t * HALF, (t + 1) * HALF)
                        v.wait_ge(v_high, 2 * p + t + 1)
                        v.tensor_tensor(vl[:, p % 2, cols], pv[:, t, :], vh[:, p % 2, cols].bitcast(F32),
                                        ALU.subtract).then_inc(v_low, 1)
                        if p == 0 and t == 0:
                            low_at(1, 1)
                        if p == 0 and t == 1:
                            low_at(2, 0)
                            low_at(2, 1)
                        if 0 < p < PAIRS - 2:
                            low_at(p + 2, t)
                    if p == 1:
                        low_weights(1)
                for i in range(TT):
                    v.wait_ge(out_made, (i | 1) + 1)
                    v.tensor_tensor(res_x[:, i, :], res_x[:, i, :], po[:, i, :], ALU.add).then_inc(added, 1)
                v.wait_ge(added, TT)


SH, SD = 16, 16
SPAIRS = SH // 2


def self_attention(nc, res_x, ident, halfpow, Wqkv, WoT, XG):
    with ExitStack() as ctx:
        sb = lambda n, s, d: ctx.enter_context(nc.sbuf_tensor(n, s, d))
        sem = lambda n: ctx.enter_context(nc.semaphore(n))
        bank = ctx.enter_context(nc.psum_tensor("s_banks", [P, 8, HALF], F32))
        ln = LayerNorm(nc, sb, bank[:, 0:4, :], sem, "ln2", res_x, ident, halfpow, False)
        w = sb("w_qkv", [P, 3, DC, DIM], F32)
        wo = sb("w_so", [P, DC, DIM], F32)
        qT = sb("s_qT", [P, DC, TOK], F32)
        kT = sb("s_kT", [P, DC, TOK], F32)
        vb = sb("s_vb", [P, B, SPAIRS, 2 * SD], F32)
        mine = sb("s_mine", [P, 8], F32)
        above = sb("s_above", [P, NQ], F32)
        above2 = sb("s_above2", [P, NQ], F32)
        kb = sb("s_kb", [P, 16, 8, NQ], F32)
        s = sb("s_s", [P, 4, SH, NQ], F32)
        top = sb("s_top", [P, 2, SH], F32)
        tot = sb("s_tot", [P, 2, SH], F32)
        inv = sb("s_inv", [P, 2, SH], F32)
        aT = sb("s_aT", [P, 2, SPAIRS, P], F32)
        oT = sb("s_oT", [P, 2, DC, P], F32)

        nil = sb("s_nil", [P, ROWS // P * DIM // 4], F32)
        w_in, wo_in, nil_set, cleared = sem("s_w_in"), sem("s_wo_in"), sem("s_nil_set"), sem("s_cleared")
        g1, g2, v_zero = sem("s_g1"), sem("s_g2"), sem("s_v_zero")
        qk_made, qk_copied, v_made = sem("s_qk_made"), sem("s_qk_copied"), sem("s_v_made")
        v_laid = sem("s_v_laid")
        k_laid0, k_laid, scored, masked = sem("s_k_laid0"), sem("s_k_laid"), sem("s_scored"), sem("s_masked")
        topped, shifted, expd, summed, inverted, normed = (sem("s_topped"), sem("s_shifted"), sem("s_expd"),
                                                           sem("s_summed"), sem("s_inverted"), sem("s_normed"))
        turned, a_copied, o_made, o_copied, y_made, added = (sem("s_turned"), sem("s_a_copied"), sem("s_o_made"),
                                                             sem("s_o_copied"), sem("s_y_made"), sem("s_added"))

        with nc.Block() as block:
            @block.sync
            def _(sp):
                sp.dma_start(w[:, :, :, :], Wqkv.rearrange("n (c p) d -> p n c d", p=P)).then_inc(w_in, 16)
                sp.dma_start(wo[:, :, :], WoT.rearrange("(c p) d -> p c d", p=P)).then_inc(wo_in, 16)
                sp.wait_ge(nil_set, 1)
                flat = XG.rearrange("(p n) d -> p (n d)", p=P)
                w4 = ROWS // P * DIM // 4
                for n in range(4):
                    sp.dma_start(flat[:, n * w4:(n + 1) * w4], nil[:, :]).then_inc(cleared, 16)
                sp.wait_ge(cleared, 64)

            @block.gpsimd
            def _(pool):
                pool.memset(nil[:, :], 0.0).then_inc(nil_set, 1)
                pool.memset(mine[:, :], 1.0).then_inc(g1, 1)
                pool.memset(above[:, :], 0.0).then_inc(g1, 1)
                pool.memset(above2[:, :], 0.0).then_inc(g1, 1)
                pool.memset(vb[:, :, :, :], 0.0).then_inc(v_zero, 1)
                pool.wait_ge(g1, 3)
                pool.affine_select(out=mine[:, :], in_=mine[:, :], compare_op=ALU.is_ge, fill=0.0, base=0,
                                   pattern=[[-SD, 8]], channel_multiplier=1).then_inc(g2, 1)
                pool.affine_select(out=above[:, :], in_=above[:, :], compare_op=ALU.is_ge, fill=-1e30, base=0,
                                   pattern=[[-1, NQ]], channel_multiplier=1).then_inc(g2, 1)
                pool.affine_select(out=above2[:, :], in_=above2[:, :], compare_op=ALU.is_ge, fill=-1e30, base=-NQ,
                                   pattern=[[-1, NQ]], channel_multiplier=1).then_inc(g2, 1)
                pool.wait_ge(g2, 3)
                pool.affine_select(out=mine[:, :], in_=mine[:, :], compare_op=ALU.is_ge, fill=0.0, base=SD - 1,
                                   pattern=[[SD, 8]], channel_multiplier=-1).then_inc(g2, 1)
                ln.pool_root(pool)
                pool.wait_ge(g2, 4)

                def lay_keys(i):
                    pool.wait_ge(qk_copied, 4 if i < TT // 2 else 8)
                    for n in range(1, 4):
                        g = 4 * i + n
                        b, m = 2 * i + n // 2, n % 2
                        if g >= 16:
                            pool.wait_ge(scored, g - 15)
                        keys = kT[:, m, b * NQ:(b + 1) * NQ].unsqueeze(1).broadcast_to([P, 8, NQ])
                        pool.tensor_tensor(kb[:, g % 16, :, :], keys, mine[:, :].unsqueeze(2).broadcast_to([P, 8, NQ]),
                                           ALU.mult).then_inc(k_laid, 1)

                def normalise(i):
                    pool.wait_ge(inverted, i + 1)
                    pool.tensor_tensor(s[:, i % 4], s[:, i % 4], inv[:, i % 2, :].unsqueeze(2).broadcast_to([P, SH, NQ]),
                                       ALU.mult).then_inc(normed, 1)

                for i in range(3):
                    lay_keys(i)
                for i in range(TT):
                    normalise(i)
                    if i + 3 < TT:
                        lay_keys(i + 3)

            @block.tensor
            def _(pe):
                ln.tensor_turn(pe)
                pe.wait_ge(w_in, 16)
                for n in range(8):
                    t, kind, m = n // 4, n // 2 % 2, n % 2
                    pe.wait_ge(ln.copied, 2 * t + 2)
                    bk = 4 + n % 4
                    if n >= 4:
                        pe.wait_ge(qk_copied, n - 3)
                    for c in range(DC):
                        mm = pe.matmul(bank[:, bk, :], w[:, kind, c, m * P:(m + 1) * P],
                                       ln.hT[:, c, t * HALF:(t + 1) * HALF], start=c == 0, stop=c == DC - 1)
                    mm.then_inc(qk_made, 1)

                def values(b):
                    if b >= 4:
                        pe.wait_ge(v_laid, 2 * (b - 3))
                    else:
                        pe.wait_ge(qk_copied, b + 5)
                    for hh in range(2):
                        for c in range(DC):
                            heads = w[:, 2, c, :].rearrange("p (j e d) -> p j e d", e=2, d=SD)[:, :, hh, :]
                            mm = pe.matmul(bank[hh * NQ:(hh + 1) * NQ, 4 + b % 4, 0:P], ln.hT[:, c, b * NQ:(b + 1) * NQ],
                                           heads, start=c == 0, stop=c == DC - 1)
                    mm.then_inc(v_made, 1)

                def scores(i):
                    for n in range(4):
                        b2, m = n // 2, n % 2
                        if n == 0:
                            pe.wait_ge(k_laid0, i + 1)
                        else:
                            pe.wait_ge(k_laid, 3 * i + n)
                        if i >= 2 and n == 0:
                            pe.wait_ge(masked, 2 * (i - 1))
                        b = 2 * i + b2
                        pe.matmul(bank[b2 * NQ:(b2 + 1) * NQ, 2 * (i % 2) + m, :], qT[:, m, b * NQ:(b + 1) * NQ],
                                  kb[:, (4 * i + n) % 16, :, :], start=True, stop=True).then_inc(scored, 1)

                def turn(i):
                    pe.wait_ge(normed, i + 1)
                    if i >= 1:
                        pe.wait_ge(a_copied, 2 * i)
                    for g in range(2):
                        for n in range(4):
                            pr = 4 * g + n
                            mm = pe.transpose(bank[:, 4 + g, n * P:(n + 1) * P],
                                              s[:, i % 4, 2 * pr:2 * pr + 2, :].rearrange("p h k -> p (h k)"), ident[:, :])
                        mm.then_inc(turned, 1)

                def outputs(i):
                    pe.wait_ge(a_copied, 2 * i + 2)
                    if i >= 1:
                        pe.wait_ge(o_copied, i)
                    for pr in range(SPAIRS):
                        m, r = pr // 4, 32 * (pr % 4)
                        for b2 in range(2):
                            mm = pe.matmul(bank[r:r + 32, 6, m * P + b2 * NQ:m * P + (b2 + 1) * NQ],
                                           vb[:, 2 * i + b2, pr, :], aT[:, i % 2, pr, b2 * NQ:(b2 + 1) * NQ],
                                           start=True, stop=True)
                    mm.then_inc(o_made, 1)

                def project(i):
                    pe.wait_ge(o_copied, i + 1)
                    if i >= 1:
                        pe.wait_ge(added, i)
                    for c in range(DC):
                        mm = pe.matmul(bank[:, 7, 0:DIM], oT[:, i % 2, c, :], wo[:, c, :], start=c == 0,
                                       stop=c == DC - 1)
                    mm.then_inc(y_made, 1)

                for i in range(3):
                    for b in (range(4), range(4, 10), range(10, B))[i]:
                        values(b)
                    scores(i)
                pe.wait_ge(v_laid, 2 * B)
                pe.wait_ge(wo_in, 16)
                for i in range(TT):
                    turn(i)
                    if i >= 1:
                        project(i - 1)
                    if i + 3 < TT:
                        scores(i + 3)
                    outputs(i)
                project(TT - 1)

            @block.scalar
            def _(act):
                ln.scalar_copy(act)
                for n in range(8):
                    t, kind, m = n // 4, n // 2 % 2, n % 2
                    act.wait_ge(qk_made, n + 1)
                    act.activation((kT if kind else qT)[:, m, t * HALF:(t + 1) * HALF], bank[:, 4 + n % 4, :],
                                   ACT.Copy).then_inc(qk_copied, 1)
                act.wait_ge(v_zero, 1)
                for b in range(B):
                    act.wait_ge(v_made, b + 1)
                    for hh in range(2):
                        r = slice(hh * NQ, (hh + 1) * NQ)
                        src = bank[r, 4 + b % 4, 0:P].rearrange("p (j d) -> p j d", d=SD)
                        act.activation(vb[r, b, :, hh * SD:(hh + 1) * SD], src, ACT.Copy).then_inc(v_laid, 1)

                def exp(i):
                    act.wait_ge(shifted, i + 1)
                    act.activation(s[:, i % 4], s[:, i % 4], ACT.Exp, scale=SD ** -0.5).then_inc(expd, 1)

                exp(0)
                exp(1)
                for i in range(TT):
                    for g in range(2):
                        act.wait_ge(turned, 2 * i + g + 1)
                        if i >= 2:
                            act.wait_ge(o_made, i - 1)
                        act.activation(aT[:, i % 2, 4 * g:4 * g + 4, :], bank[:, 4 + g, :], ACT.Copy
                                       ).then_inc(a_copied, 1)
                    act.wait_ge(o_made, i + 1)
                    if i >= 2:
                        act.wait_ge(y_made, i - 1)
                    act.activation(oT[:, i % 2], bank[:, 6, 0:DC * P], ACT.Copy).then_inc(o_copied, 1)
                    if i + 2 < TT:
                        exp(i + 2)

            @block.vector
            def _(v):
                ln.vector_normalise(v)
                v.wait_ge(g2, 4)
                v.tensor_copy(above[NQ:P, :], above2[NQ:P, :]).then_inc(g1, 1)
                v.wait_ge(g1, 4)

                def lay_keys(i):
                    v.wait_ge(qk_copied, 4 if i < TT // 2 else 8)
                    g, b = 4 * i, 2 * i
                    if g >= 16:
                        v.wait_ge(scored, g - 15)
                    keys = kT[:, 0, b * NQ:(b + 1) * NQ].unsqueeze(1).broadcast_to([P, 8, NQ])
                    v.tensor_tensor(kb[:, g % 16, :, :], keys, mine[:, :].unsqueeze(2).broadcast_to([P, 8, NQ]),
                                    ALU.mult).then_inc(k_laid0, 1)

                def shift(i):
                    for m in range(2):
                        v.wait_ge(scored, 4 * i + 3 + m)
                        if i >= 4:
                            v.wait_ge(turned, 2 * (i - 3))
                        v.tensor_tensor(s[:, i % 4, 8 * m:8 * m + 8, :], bank[:, 2 * (i % 2) + m, :],
                                        above[:, :].unsqueeze(1).broadcast_to([P, 8, NQ]), ALU.add).then_inc(masked, 1)
                    v.wait_ge(masked, 2 * i + 2)
                    if i >= 2:
                        v.wait_ge(shifted, i - 1)
                    v.tensor_reduce(top[:, i % 2], s[:, i % 4], AX_X, ALU.max).then_inc(topped, 1)
                    v.wait_ge(topped, i + 1)
                    v.tensor_tensor(s[:, i % 4], s[:, i % 4], top[:, i % 2].unsqueeze(2).broadcast_to([P, SH, NQ]),
                                    ALU.subtract).then_inc(shifted, 1)

                def invert(i):
                    v.wait_ge(expd, i + 1)
                    if i >= 2:
                        v.wait_ge(inverted, i - 1)
                        v.wait_ge(normed, i - 1)
                    v.tensor_reduce(tot[:, i % 2], s[:, i % 4], AX_X, ALU.add).then_inc(summed, 1)
                    v.wait_ge(summed, i + 1)
                    v.reciprocal(inv[:, i % 2], tot[:, i % 2]).then_inc(inverted, 1)

                for i in range(4):
                    lay_keys(i)
                shift(0)
                shift(1)
                for i in range(-1, TT):
                    if 0 <= i < TT - 4:
                        lay_keys(i + 4)
                    if i + 1 < TT:
                        invert(i + 1)
                    if i >= 1:
                        v.wait_ge(y_made, i)
                        v.tensor_tensor(res_x[:, i - 1, :], res_x[:, i - 1, :], bank[:, 7, 0:DIM], ALU.add
                                        ).then_inc(added, 1)
                    if i + 3 < TT:
                        shift(i + 3)
                v.wait_ge(y_made, TT)
                v.tensor_tensor(res_x[:, TT - 1, :], res_x[:, TT - 1, :], bank[:, 7, 0:DIM], ALU.add
                                ).then_inc(added, 1)
                v.wait_ge(added, TT)


E, F = 8, 512
FC = F // P
TOP = 2
MT = 256
TILES = (TOP * TOK + E * (MT - 1)) // MT
ROWS = TILES * MT
BIASES = 4 * FC


def route(nc, res_x, ident, ones, halfpow, Wgate, bgate, xn, share, comb, place, placef, spots, owner):
    with ExitStack() as ctx:
        sb = lambda n, s, d: ctx.enter_context(nc.sbuf_tensor(n, s, d))
        ps = lambda n, s: ctx.enter_context(nc.psum_tensor(n, s, F32))
        sem = lambda n: ctx.enter_context(nc.semaphore(n))
        bank = ps("r_banks", [P, 4, HALF])
        ln = LayerNorm(nc, sb, bank, sem, "ln3", res_x, ident, halfpow, False, xn)
        wg = sb("r_wg", [P, DC, E], F32)
        bg = sb("r_bg", [E, 1], F32)
        logitsT = sb("r_logitsT", [E, TOK], F32)
        before = sb("r_before", [P, P], F32)
        iota_e = sb("r_iota_e", [P, E], F32)
        iota_t = sb("r_iota_t", [P, TILES], F32)
        logits = sb("r_logits", [P, TT, E], F32)
        best = sb("r_best", [P, TT, 8], F32)
        which = sb("r_which", [P, TT, 8], U32)
        whichf = sb("r_whichf", [P, TT, TOP], F32)
        gap = sb("r_gap", [P, TT], F32)
        egap = sb("r_egap", [P, TT], F32)
        den = sb("r_den", [P, TT], F32)
        hot = sb("r_hot", [P, TOP, TT, E], F32)
        both = sb("r_both", [P, TT, E], F32)
        mixed = sb("r_mixed", [P, TOP, TT, E], F32)
        sofar = sb("r_sofar", [P, TT + 1, E], F32)
        rank = sb("r_rank", [P, TT + 1, E], F32)
        over = sb("r_over", [P, 4, E], F32)
        ends = sb("r_ends", [P, 4, E], F32)
        base = sb("r_base", [P, E], F32)
        spot = sb("r_spot", [P, TT, E], F32)
        picked = sb("r_picked", [P, TOP, TT, E], F32)
        past = sb("r_past", [P, TILES, E], F32)
        ownerf = sb("r_ownerf", [P, TILES], F32)
        pg = ps("r_pg", [P, TT, E])
        pr = ps("r_pr", [P, TT + 1, E])

        w_in, g1, g2 = sem("r_w_in"), sem("r_g1"), sem("r_g2")
        gatedT, gT_copied = sem("r_gatedT"), sem("r_gT_copied")
        gated, g_copied, d = sem("r_gated"), sem("r_g_copied"), sem("r_d")
        ranked, r_copied, edone = sem("r_ranked"), sem("r_r_copied"), sem("r_edone")
        steps = ["max", "index", "indexf", "gap", "den", "share0", "share1", "hot", "both", "sofar", "mixed", "comb",
                 "over", "tiles1", "tiles", "end1", "end2", "ends", "base", "spot", "picked", "placef", "place",
                 "past", "ownerf", "ownermin", "owner"]
        counts = {"max": TT, "index": TT, "hot": TOP, "sofar": TT, "mixed": TOP, "picked": TOP, "over": 4,
                  "end1": 2, "end2": 2, "ends": 2}
        at, n = {}, 0
        for name in steps:
            n += counts.get(name, 1)
            at[name] = n

        with nc.Block() as block:
            @block.sync
            def _(sp):
                sp.dma_start(wg[:, :, :], Wgate.rearrange("(c p) e -> p c e", p=P)).then_inc(w_in, 16)
                sp.dma_start(bg[:, :], bgate.rearrange("(e a) -> e a", a=1)).then_inc(w_in, 16)

            @block.gpsimd
            def _(pool):
                pool.memset(before[:, :], 1.0).then_inc(g1, 1)
                pool.memset(sofar[:, 0, :], 0.0).then_inc(g2, 1)
                pool.iota(iota_e[:, :], [[1, E]], base=0, channel_multiplier=0,
                          allow_small_or_imprecise_dtypes=True).then_inc(g2, 1)
                pool.iota(spots[:, :], [[1, MT]], base=0, channel_multiplier=0,
                          allow_small_or_imprecise_dtypes=True).then_inc(g2, 1)
                pool.iota(iota_t[:, :], [[1, TILES]], base=0, channel_multiplier=0,
                          allow_small_or_imprecise_dtypes=True).then_inc(g2, 1)
                pool.wait_ge(g1, 1)
                pool.affine_select(out=before[:, :], in_=before[:, :], compare_op=ALU.is_gt, fill=0.0, base=0,
                                   pattern=[[1, P]], channel_multiplier=-1).then_inc(g2, 1)
                ln.pool_root(pool)

            @block.tensor
            def _(pe):
                ln.tensor_turn(pe)
                pe.wait_ge(w_in, 32)
                for t in range(2):
                    pe.wait_ge(ln.copied, 2 * t + 2)
                    for c in range(DC):
                        m = pe.matmul(bank[0:E, 2 * t, :], wg[:, c, :], ln.hT[:, c, t * HALF:(t + 1) * HALF],
                                      start=c == 0, stop=c == DC - 1)
                    m.then_inc(gatedT, 1)
                for i in range(TT):
                    pe.wait_ge(gT_copied, i // 4 + 1)
                    m = pe.transpose(pg[:, i, :], logitsT[:, i * P:(i + 1) * P], ident[0:E, 0:E])
                m.then_inc(gated, 1)
                pe.wait_ge(d, at["sofar"])
                pe.wait_ge(g2, 5)
                pe.matmul(pr[:, 0:TT, :], ones[:, :], sofar[:, 0:TT, :], start=True, stop=False)
                pe.matmul(pr[:, 0:TT, :], before[:, :], both[:, :, :], start=False, stop=True)
                pe.matmul(pr[:, TT, :], ones[:, :], sofar[:, TT, :], start=True, stop=True).then_inc(ranked, 1)
            @block.scalar
            def _(act):
                ln.scalar_copy(act)
                act.wait_ge(w_in, 32)
                for t in range(2):
                    act.wait_ge(gatedT, t + 1)
                    act.activation(logitsT[:, t * HALF:(t + 1) * HALF], bank[0:E, 2 * t, :], ACT.Identity,
                                   bias=bg[:, 0:1]).then_inc(gT_copied, 1)
                act.wait_ge(gated, 1)
                act.activation(logits[:, :, :], pg[:, :, :], ACT.Copy).then_inc(g_copied, 1)
                act.wait_ge(d, at["gap"])
                act.activation(egap[:, :], gap[:, :], ACT.Exp).then_inc(edone, 1)
                act.wait_ge(ranked, 1)
                act.activation(rank[:, :, :], pr[:, :, :], ACT.Copy).then_inc(r_copied, 1)

            @block.vector
            def _(v):
                done = [0]

                def after(name):
                    v.wait_ge(d, at[name])

                def inc(op):
                    done[0] += 1
                    op.then_inc(d, 1)

                ln.vector_normalise(v)
                v.wait_ge(g_copied, 1)
                for i in range(TT):
                    inc(v.max(best[:, i, :], logits[:, i, :]))
                for i in range(TT):
                    v.wait_ge(d, i + 1)
                    inc(v.max_index(which[:, i, :], best[:, i, :], logits[:, i, :]))
                after("index")
                inc(v.tensor_copy(whichf[:, :, :], which[:, :, 0:TOP]))
                inc(v.tensor_tensor(gap[:, :], best[:, :, 1], best[:, :, 0], ALU.subtract))
                v.wait_ge(edone, 1)
                inc(v.tensor_scalar(den[:, :], egap[:, :], 1.0, None, ALU.add))
                after("den")
                inc(v.reciprocal(share[:, 0, :], den[:, :]))
                after("share0")
                inc(v.tensor_tensor(share[:, 1, :], egap[:, :], share[:, 0, :], ALU.mult))
                v.wait_ge(g2, 5)
                for k in range(TOP):
                    inc(v.tensor_tensor(hot[:, k], whichf[:, :, k].unsqueeze(2).broadcast_to([P, TT, E]),
                                        iota_e[:, :].unsqueeze(1).broadcast_to([P, TT, E]), ALU.is_equal))
                after("hot")
                inc(v.tensor_tensor(both[:, :, :], hot[:, 0], hot[:, 1], ALU.add))
                for i in range(TT):
                    v.wait_ge(d, at["both"] + i)
                    inc(v.tensor_tensor(sofar[:, i + 1, :], sofar[:, i, :], both[:, i, :], ALU.add))
                for k in range(TOP):
                    inc(v.tensor_tensor(mixed[:, k], hot[:, k], share[:, k, :].unsqueeze(2).broadcast_to([P, TT, E]),
                                        ALU.mult))
                after("mixed")
                inc(v.tensor_tensor(comb[:, :, :], mixed[:, 0], mixed[:, 1], ALU.add))
                v.wait_ge(r_copied, 1)
                for n in range(4):
                    inc(v.tensor_scalar(over[:, n, :], rank[:, TT, :], float(n * MT), None, ALU.is_gt))
                after("over")
                inc(v.tensor_tensor(over[:, 0:2, :], over[:, 0:2, :], over[:, 2:4, :], ALU.add))
                after("tiles1")
                inc(v.tensor_tensor(ends[:, 0, :], over[:, 0, :], over[:, 1, :], ALU.add))
                for n, name in enumerate(("tiles", "end1", "end2")):
                    after(name)
                    z = 1 << n
                    inc(v.tensor_tensor(ends[:, n + 1, z:], ends[:, n, z:], ends[:, n, 0:E - z], ALU.add))
                    inc(v.tensor_copy(ends[:, n + 1, 0:z], ends[:, n, 0:z]))
                after("ends")
                inc(v.tensor_tensor(base[:, :], ends[:, 3, :], ends[:, 0, :], ALU.subtract))
                after("base")
                inc(v.scalar_tensor_tensor(out=spot[:, :, :], in0=base[:, :].unsqueeze(1).broadcast_to([P, TT, E]),
                                           scalar=float(MT), in1=rank[:, 0:TT, :], op0=ALU.mult, op1=ALU.add))
                after("spot")
                for k in range(TOP):
                    inc(v.tensor_tensor(picked[:, k], hot[:, k], spot[:, :, :], ALU.mult))
                after("picked")
                inc(v.tensor_reduce(placef[:, :, :], picked[:, :, :, :], AX_X, ALU.add))
                after("placef")
                inc(v.tensor_copy(place[:, :, :], placef[:, :, :]))
                inc(v.tensor_tensor(past[:, :, :], ends[:, 3, :].unsqueeze(1).broadcast_to([P, TILES, E]),
                                    iota_t[:, :].unsqueeze(2).broadcast_to([P, TILES, E]), ALU.is_le))
                after("past")
                inc(v.tensor_reduce(ownerf[:, :], past[:, :, :], AX_X, ALU.add))
                after("ownerf")
                inc(v.tensor_scalar(ownerf[:, :], ownerf[:, :], float(E - 1), None, ALU.min))
                after("ownermin")
                inc(v.tensor_copy(owner[:, :], ownerf[:, :]))
                assert done[0] == at["owner"]
                after("owner")


def experts(nc, res_x, ident, W1, W2, Wg, Wl, W3, Bias, b3, XG, YG, xn, share, comb, place, placef, spots,
            owner, out):
    with ExitStack() as ctx:
        sb = lambda n, s, d: ctx.enter_context(nc.sbuf_tensor(n, s, d))
        ps = lambda n, s: ctx.enter_context(nc.psum_tensor(n, s, F32))
        sem = lambda n: ctx.enter_context(nc.semaphore(n))
        A = 2 * DC * F
        G = 2 * FC * F
        Y = FC * DIM
        wr = sb("wr", [P, A + G + Y], F32)
        wh = sb("wh", [P, 2, A + G + Y], F32R)
        wl = sb("wl", [P, 2, A + G + Y], F32R)
        bias = sb("e_bias", [P, 2, BIASES], F32)
        halfg = sb("e_halfg", [P, 2, FC], F32)
        xg = sb("e_xg", [P, 2, MT // P, DIM], F32)
        xf = sb("e_xf", [P, DC, MT], F32)
        xh = sb("e_xh", [P, DC, MT], F32R)
        xl = sb("e_xl", [P, DC, MT], F32R)
        x1 = sb("e_x1", [P, 2, MT], F32)
        z = sb("e_z", [P, FC, MT], F32)
        assert MT == DIM and FC <= TT
        o = xn[:, 0:FC, :]
        zh = sb("e_zh", [P, 2, FC, MT], F32R)
        zl = sb("e_zl", [P, 2, FC, MT], F32R)
        tanh = sb("e_tanh", [P, 2, MT], F32)
        g = sb("e_g", [P, 2, MT], F32)
        u = sb("e_u", [P, 2, MT], F32)
        oh = sb("e_oh", [P, FC, MT], F32R)
        ol = sb("e_ol", [P, FC, MT], F32R)
        y = sb("e_y", [P, MT // P, DIM], F32)
        pp = ps("pp", [P, FC, 2, MT])
        pt = ps("pt", [P, DC, MT])
        py = ps("py", [P, MT // P, DIM])

        sent, one_of, hot_made, hot_used, x_half = (sem("e_sent"), sem("e_one_of"), sem("e_hot_made"),
                                                    sem("e_hot_used"), sem("e_x_half"))
        w_in = [sem(f"e_w_in{n}") for n in range(4)]
        x_in, bx_in, bg_in = ([sem(f"e_{n}{b}") for b in range(2)] for n in ("x_in", "bx_in", "bg_in"))
        y_out = sem("e_y_out")
        w_high, w_low = [sem(f"e_w_high{n}") for n in range(4)], [sem(f"e_w_low{n}") for n in range(4)]
        b_half = sem("e_b_half")
        turned, x_copied, x_high, x_low = sem("e_turned"), sem("e_x_copied"), sem("e_x_high"), sem("e_x_low")
        x_made, x1_done, z_done, z_high, z_low = (sem("e_x_made"), sem("e_x1_done"), sem("e_z_done"),
                                                  sem("e_z_high"), sem("e_z_low"))
        g_made, g_done, u_done, o_done, o_high, o_low = (sem("e_g_made"), sem("e_g_done"), sem("e_u_done"),
                                                         sem("e_o_done"), sem("e_o_high"), sem("e_o_low"))
        tanh_done = sem("e_tanh_done")
        y_made, y_copied = sem("e_y_made"), sem("e_y_copied")
        parts = [slice(0, A), slice(A, A + G // 2), slice(A + G // 2, A + G), slice(A + G, A + G + Y)]

        def w1(w, b, k, c, f):
            return w[:, b, (k * DC + c) * F + f * P:(k * DC + c) * F + (f + 1) * P]

        def wgl(w, b, k, c, f):
            return w[:, b, A + (k * FC + c) * F + f * P:A + (k * FC + c) * F + (f + 1) * P]

        def w3(w, b, c):
            return w[:, b, A + G + c * DIM:A + G + (c + 1) * DIM]

        def tiles(eng, step):
            step(-1, 1, -1)
            step(0, 0, 0)
            step(1, 1, 0)
            step(2, 0, 1)
            with eng.Fori(1, (TILES - 3) // 2) as r:
                step(2 * r + 1, 1, r)
                step(2 * r + 2, 0, r + 1)
            step(TILES - 2, 1, TILES // 2 - 1)
            step(TILES - 1, 0, TILES // 2)
            step(TILES, 1, TILES // 2)

        def on(i):
            return not isinstance(i, int) or 0 <= i < TILES

        with nc.Block() as block:
            @block.sync
            def _(sp):
                def expert(i):
                    return sp.value_load(owner[0:1, bass.ds(i, 1)], min_val=0, max_val=E - 1)

                def tile_rows(i, b):
                    if isinstance(i, int) and i == 1:
                        sp.wait_ge(sent, 16 * TT * TOP)
                    wait(sp, turned, i - 1)
                    sp.dma_start(xg[:, b], XG[bass.ds(i * MT, MT), :].rearrange("(t p) d -> p t d", p=P)
                                 ).then_inc(x_in[b], 16)

                def first_biases(i, b, e):
                    wait(sp, z_done, FC * (i - 1))
                    sp.dma_start(bias[:, b, 0:2 * FC], Bias[bass.ds(e, 1), :, 0:2 * FC].rearrange("a p n -> (a p) n")
                                 ).then_inc(bx_in[b], 16)

                def gate_biases(i, b, e):
                    wait(sp, o_done, FC * (i - 1))
                    sp.dma_start(bias[:, b, 2 * FC:], Bias[bass.ds(e, 1), :, 2 * FC:].rearrange("a p n -> (a p) n")
                                 ).then_inc(bg_in[b], 16)

                def weights(i, n, e):
                    wait(sp, w_low[n], i)
                    ws, rows_, width = [((W1, W2), DC, F), ((Wg,), FC, F), ((Wl,), FC, F), ((W3,), FC, DIM)][n]
                    at = parts[n].start
                    for k, w in enumerate(ws):
                        to = wr[:, at + k * rows_ * width:at + (k + 1) * rows_ * width]
                        sp.dma_start(to.rearrange("p (c f) -> p c f", c=rows_),
                                     w[bass.ds(e, 1)].rearrange("a (c p) f -> p (a c) f", p=P)).then_inc(w_in[n], 16)

                def step(i, b, h):
                    if on(i + 1):
                        gate_biases(i + 1, 1 - b, expert(i + 1))
                    if on(i + 2):
                        e = expert(i + 2)
                        tile_rows(i + 2, b)
                        first_biases(i + 2, b, e)
                        weights(i + 2, 0, e)
                        weights(i + 2, 1, e)
                    if on(i - 1):
                        sp.wait_ge(y_copied, i)
                        sp.dma_start(YG[bass.ds((i - 1) * MT, MT), :].rearrange("(t p) d -> p t d", p=P), y[:, :, :]
                                     ).then_inc(y_out, 16)
                    if on(i + 2):
                        weights(i + 2, 2, e)
                        weights(i + 2, 3, e)

                e0 = expert(0)
                for n in range(4):
                    weights(0, n, e0)
                first_biases(0, 0, e0)
                tiles(sp, step)
                sp.wait_ge(y_out, 16 * TILES)

            @block.gpsimd
            def _(pool):
                for i in range(TT):
                    for k in range(TOP):
                        pool.indirect_dma_start(XG, bass.IndirectOffsetOnAxis(ap=place[:, k, i:i + 1], axis=0),
                                                xn[:, i, :], None).then_inc(sent, 16)

                def step(i, b, h):
                    if on(i + 1):
                        for n in (2, 3) if isinstance(i, int) and i == -1 else (1, 2, 3):
                            pool.wait_ge(w_high[n], i + 2)
                            pool.tensor_tensor(wl[:, 1 - b, parts[n]], wr[:, parts[n]],
                                               wh[:, 1 - b, parts[n]].bitcast(F32), ALU.subtract).then_inc(w_low[n], 1)

                tiles(pool, step)

            @block.tensor
            def _(pe):
                def first(i, b, h):
                    if not on(i):
                        return
                    pe.wait_ge(x_in[b], 16 * (h if b == 0 else h + 1))
                    wait(pe, x_copied, i)
                    for t in range(MT // P):
                        for c in range(DC):
                            m = pe.transpose(pt[:, c, t * P:(t + 1) * P], xg[:, b, t, c * P:(c + 1) * P], ident[:, :])
                    m.then_inc(turned, 1)

                def products(i, b):
                    if not on(i):
                        return
                    pe.wait_ge(x_low, i + 1)
                    pe.wait_ge(w_low[0], i + 1)
                    for f in range(FC):
                        wait(pe, o_done, FC * (i - 2) + f + 1)
                        if isinstance(i, int) and i == 1:
                            pe.wait_ge(z_done, f + 1)
                        for k in range(2):
                            for c in range(DC):
                                m = three_passes(pe, pp[:, f, k, :], w1(wh, b, k, c, f), w1(wl, b, k, c, f),
                                                 xh[:, c, :], xl[:, c, :], c == 0, c == DC - 1)
                        m.then_inc(x_made, 1)

                def outputs(i, b):
                    if not on(i):
                        return
                    pe.wait_ge(o_low, 2 * (i + 1))
                    pe.wait_ge(w_low[3], i + 1)
                    wait(pe, y_copied, i)
                    for t in range(MT // P):
                        for c in range(FC):
                            m = three_passes(pe, py[:, t, :], oh[:, c, t * P:(t + 1) * P], ol[:, c, t * P:(t + 1) * P],
                                             w3(wh, b, c), w3(wl, b, c), c == 0, c == FC - 1)
                    m.then_inc(y_made, 1)

                def gate(i, b):
                    if not on(i):
                        return
                    pe.wait_ge(w_low[1], i + 1)
                    pe.wait_ge(w_low[2], i + 1)
                    pe.wait_ge(z_low, 2 * (i + 1))
                    for f in range(FC):
                        if not isinstance(i, int) or i + 1 < TILES:
                            pe.wait_ge(z_done, FC * (i + 1) + f + 1)
                        else:
                            wait(pe, o_done, FC * (i - 1) + f + 1)
                        for k in range(2):
                            for c in range(FC):
                                m = three_passes(pe, pp[:, f, k, :], wgl(wh, b, k, c, f), wgl(wl, b, k, c, f),
                                                 zh[:, b, c, :], zl[:, b, c, :], c == 0, c == FC - 1)
                        m.then_inc(g_made, 1)

                def step(i, b, h):
                    products(i + 1, 1 - b)
                    outputs(i - 1, 1 - b)
                    first(i + 2, b, h + 1)
                    gate(i, b)

                for i in range(TT):
                    pe.wait_ge(hot_made, i + 1)
                    for c in range(DC):
                        m = pe.matmul((pt, py)[c][:, 0, :], xn[:, i, c * P:(c + 1) * P], u[:, i % 2, :],
                                      start=i == 0, stop=i == TT - 1)
                    m.then_inc(hot_used if i < TT - 1 else turned, 1)
                tiles(pe, step)

            @block.scalar
            def _(act):
                def first(i, b):
                    if not on(i):
                        return
                    act.wait_ge(turned, i + 1)
                    wait(act, x_low, i)
                    act.activation(xf[:, :, :], pt[:, :, :], ACT.Copy).then_inc(x_copied, 1)

                def high(i, b, n):
                    if not on(i):
                        return
                    act.wait_ge(w_in[n], (32 if n == 0 else 16) * (i + 1))
                    used, each = [(x_made, FC), (g_made, FC), (g_made, FC), (y_made, 1)][n]
                    wait(act, used, each * (i - 1))
                    act.activation(wh[:, b, parts[n]], wr[:, parts[n]], ACT.Copy).then_inc(w_high[n], 1)

                def step(i, b, h):
                    if on(i + 1):
                        for f in range(FC):
                            act.wait_ge(x_made, FC * (i + 1) + f + 1)
                            if f == 0:
                                act.wait_ge(bx_in[1 - b], 16 * (h + 1 if b == 0 else h + 2))
                            wait(act, z_done, FC * (i + 1) + f - 1)
                            act.activation(x1[:, f % 2, :], pp[:, f, 0, :], ACT.Identity,
                                           bias=bias[:, 1 - b, f:f + 1]).then_inc(x1_done, 1)
                    after_first = not isinstance(i, int) or i >= 0
                    if after_first:
                        high(i + 1, 1 - b, 1)
                    first(i + 2, b)
                    if after_first:
                        high(i + 1, 1 - b, 2)
                    high(i + 2, b, 0)
                    if on(i - 1):
                        act.wait_ge(y_made, i)
                        wait(act, y_out, 16 * (i - 1))
                        act.activation(y[:, :, :], py[:, :, :], ACT.Copy).then_inc(y_copied, 1)
                    if after_first:
                        high(i + 1, 1 - b, 3)
                    if on(i):
                        for f in range(FC):
                            act.wait_ge(g_made, FC * i + f + 1)
                            if f == 0:
                                act.wait_ge(b_half, i + 1)
                            wait(act, u_done, FC * i + f - 1)
                            act.activation(tanh[:, f % 2, :], pp[:, f, 0, :], ACT.Tanh, scale=0.5,
                                           bias=halfg[:, b, f:f + 1]).then_inc(tanh_done, 1)
                            act.activation(g[:, f % 2, :], pp[:, f, 0, :], ACT.Identity,
                                           bias=bias[:, b, 2 * FC + f:2 * FC + f + 1]).then_inc(g_done, 1)

                high(0, 0, 0)
                act.wait_ge(turned, 1)
                act.activation(xf[:, 0, :], pt[:, 0, :], ACT.Copy).then_inc(x_half, 1)
                act.activation(xf[:, 1, :], py[:, 0, :], ACT.Copy).then_inc(x_copied, 1)
                for n in range(1, 4):
                    high(0, 0, n)
                tiles(act, step)

            @block.vector
            def _(v):
                def first(i, b):
                    if not on(i):
                        return
                    v.wait_ge(x_copied, i + 1)
                    wait(v, x_made, FC * i)
                    v.tensor_copy(xh[:, :, :], xf[:, :, :]).then_inc(x_high, 1)
                    v.wait_ge(x_high, i + 1)
                    v.tensor_tensor(xl[:, :, :], xf[:, :, :], xh[:, :, :].bitcast(F32), ALU.subtract
                                    ).then_inc(x_low, 1)

                def low(i, b):
                    if not on(i):
                        return
                    v.wait_ge(w_high[0], i + 1)
                    v.tensor_tensor(wl[:, b, parts[0]], wr[:, parts[0]], wh[:, b, parts[0]].bitcast(F32), ALU.subtract
                                    ).then_inc(w_low[0], 1)

                def halves(i, b, h):
                    if not on(i):
                        return
                    v.wait_ge(bg_in[b], 16 * (h + 1))
                    wait(v, tanh_done, FC * (i - 1))
                    v.tensor_scalar(halfg[:, b], bias[:, b, 2 * FC:3 * FC], 0.5, None, ALU.mult).then_inc(b_half, 1)

                def step(i, b, h):
                    if on(i + 1):
                        for f in range(FC):
                            v.wait_ge(x1_done, FC * (i + 1) + f + 1)
                            wait(v, z_low, 2 * (i + 1) + f // 2 - 1)
                            v.scalar_tensor_tensor(out=z[:, f, :], in0=pp[:, f, 1, :],
                                                   scalar=bias[:, 1 - b, FC + f:FC + f + 1], in1=x1[:, f % 2, :],
                                                   op0=ALU.add, op1=ALU.mult).then_inc(z_done, 1)
                            if f % 2:
                                pair = f // 2
                                w = slice(f - 1, f + 1)
                                v.wait_ge(z_done, FC * (i + 1) + f + 1)
                                wait(v, g_made, FC * i)
                                v.tensor_copy(zh[:, 1 - b, w, :], z[:, w, :]).then_inc(z_high, 1)
                                v.wait_ge(z_high, 2 * (i + 1) + pair + 1)
                                v.tensor_tensor(zl[:, 1 - b, w, :], z[:, w, :], zh[:, 1 - b, w, :].bitcast(F32),
                                                ALU.subtract).then_inc(z_low, 1)
                    halves(i + 1, 1 - b, h if b == 0 else h + 1)
                    first(i + 2, b)
                    low(i + 2, b)
                    if isinstance(i, int) and i == 0:
                        v.wait_ge(sent, 16 * TT * TOP)
                    if on(i):
                        for f in range(FC):
                            v.wait_ge(g_done, FC * i + f + 1)
                            wait(v, o_done, FC * i + f - 1)
                            v.scalar_tensor_tensor(out=u[:, f % 2, :], in0=tanh[:, f % 2, :], scalar=1.0,
                                                   in1=g[:, f % 2, :], op0=ALU.add, op1=ALU.mult).then_inc(u_done, 1)
                            v.wait_ge(u_done, FC * i + f + 1)
                            wait(v, o_low, 2 * i + f // 2 - 1)
                            v.scalar_tensor_tensor(out=o[:, f, :], in0=pp[:, f, 1, :],
                                                   scalar=bias[:, b, 3 * FC + f:3 * FC + f + 1], in1=u[:, f % 2, :],
                                                   op0=ALU.add, op1=ALU.mult).then_inc(o_done, 1)
                            if f % 2:
                                pair = f // 2
                                w = slice(f - 1, f + 1)
                                v.wait_ge(o_done, FC * i + f + 1)
                                wait(v, y_made, i)
                                v.tensor_copy(oh[:, w, :], o[:, w, :]).then_inc(o_high, 1)
                                v.wait_ge(o_high, 2 * i + pair + 1)
                                v.tensor_tensor(ol[:, w, :], o[:, w, :], oh[:, w, :].bitcast(F32), ALU.subtract
                                                ).then_inc(o_low, 1)

                for i in range(TT):
                    if i >= 2:
                        v.wait_ge(hot_used, i - 1)
                    v.tensor_scalar(u[:, i % 2, :], spots[:, :], placef[:, 0, i:i + 1], None, ALU.is_equal
                                    ).then_inc(one_of, 1)
                    v.wait_ge(one_of, i + 1)
                    v.scalar_tensor_tensor(out=u[:, i % 2, :], in0=spots[:, :], scalar=placef[:, 1, i:i + 1],
                                           in1=u[:, i % 2, :], op0=ALU.is_equal, op1=ALU.add).then_inc(hot_made, 1)
                low(0, 0)
                v.wait_ge(x_half, 1)
                first(0, 0)
                v.wait_ge(w_high[1], 1)
                v.tensor_tensor(wl[:, 0, parts[1]], wr[:, parts[1]], wh[:, 0, parts[1]].bitcast(F32), ALU.subtract
                                ).then_inc(w_low[1], 1)
                tiles(v, step)

    with ExitStack() as ctx:
        sem = lambda n: ctx.enter_context(nc.semaphore(n))
        got = ctx.enter_context(nc.sbuf_tensor("f_got", [P, TT, TOP, DIM], F32))
        half = ctx.enter_context(nc.sbuf_tensor("f_half", [P, TOP, TT], F32))
        b3s = ctx.enter_context(nc.sbuf_tensor("f_b3", [E, DIM], F32))
        combT = ctx.enter_context(nc.sbuf_tensor("f_combT", [E, TT, P], F32))
        pc = ctx.enter_context(nc.psum_tensor("f_pc", [P, TT, P], F32))
        pb = ctx.enter_context(nc.psum_tensor("f_pb", [P, TT, DIM], F32))
        b3_in, c_turned, c_copied, b_made, b_added = (sem("f_b3_in"), sem("f_c_turned"), sem("f_c_copied"),
                                                      sem("f_b_made"), sem("f_b_added"))
        fetched = [sem(f"f_fetched{i}") for i in range(TT)]
        halved, mixed, stored = sem("f_halved"), sem("f_mixed"), sem("f_stored")

        with nc.Block() as block:
            @block.gpsimd
            def _(pool):
                for i in range(TT):
                    for k in range(TOP):
                        pool.indirect_dma_start(got[:, i, k, :], None, YG,
                                                bass.IndirectOffsetOnAxis(ap=place[:, k, i:i + 1], axis=0)
                                                ).then_inc(fetched[i], 16)

            @block.tensor
            def _(pe):
                for t in range(2):
                    for i in range(4 * t, 4 * t + 4):
                        m = pe.transpose(pc[0:E, i, :], comb[:, i, :], ident[:, :])
                    m.then_inc(c_turned, 1)
                pe.wait_ge(b3_in, 16)
                for i in range(TT):
                    pe.wait_ge(c_copied, i // 4 + 1)
                    pe.matmul(pb[:, i, :], combT[:, i, :], b3s[:, :], start=True, stop=True).then_inc(b_made, 1)

            @block.scalar
            def _(act):
                for t in range(2):
                    act.wait_ge(c_turned, t + 1)
                    act.activation(combT[:, 4 * t:4 * t + 4, :], pc[0:E, 4 * t:4 * t + 4, :], ACT.Copy
                                   ).then_inc(c_copied, 1)

            @block.vector
            def _(v):
                v.tensor_scalar(half[:, :, :], share[:, :, :], 0.5, None, ALU.mult).then_inc(halved, 1)
                v.wait_ge(halved, 1)
                for i in range(TT):
                    v.wait_ge(b_made, (i | 1) + 1)
                    v.tensor_tensor(res_x[:, i, :], res_x[:, i, :], pb[:, i, :], ALU.add).then_inc(b_added, 1)
                for i in range(TT):
                    v.wait_ge(b_added, i + 1)
                    v.wait_ge(fetched[i], 16 * TOP)
                    for k in range(TOP):
                        if k:
                            v.wait_ge(mixed, TOP * i + k)
                        v.scalar_tensor_tensor(out=res_x[:, i, :], in0=got[:, i, k, :], scalar=half[:, k, i:i + 1],
                                               in1=res_x[:, i, :], op0=ALU.mult, op1=ALU.add).then_inc(mixed, 1)

            @block.sync
            def _(sp):
                sp.dma_start(b3s[:, :], b3).then_inc(b3_in, 16)
                to = out.rearrange("b q d -> (b q) d").rearrange("(i p) d -> p i d", p=P)
                for i in range(TT):
                    sp.wait_ge(mixed, TOP * (i + 1))
                    sp.dma_start(to[:, i, :], res_x[:, i, :]).then_inc(stored, 16)
                sp.wait_ge(stored, 16 * TT)


def layer(nc, x, ctx_in, Wq, WkT, Wv, Wo, ln_g, ln_b, Wqkv, WoT, Wgate, bgate, W1, W2, Wg, Wl, W3, Bias, b3, out):
    scratch = lambda n, s: nc.dram_tensor(n, s, F32, kind="Internal").ap()
    QT = scratch("queries_scratch", (B, 2, P, DC, UH, NQ))
    OT = scratch("outputs_scratch", (B, 2, P, DC, UH, NQ))
    XG = scratch("routed_scratch", (ROWS, DIM))
    YG = scratch("expert_scratch", (ROWS, DIM))
    with ExitStack() as ctx:
        sb = lambda n, s, d: ctx.enter_context(nc.sbuf_tensor(n, s, d))
        sem = lambda n: ctx.enter_context(nc.semaphore(n))
        ident, ones, halfpow = sb("ident", [P, P], F32), sb("ones", [P, P], F32), sb("halfpow", [P, 16], F32)
        res_x = sb("res_x", [P, TT, DIM], F32)
        share = sb("share", [P, TOP, TT], F32)
        place = sb("place", [P, TOP, TT], U32)
        owner = sb("owner", [P, TILES], I32)
        x_in = [sem(f"x_in{j}") for j in range(TT // 2)]
        constants(nc, ident, ones, halfpow, res_x, x, sem("zeroed"), sem("made"), x_in)
        spent, spent2 = [], []
        with ExitStack() as rows_ctx:
            cx = Context(lambda n, s, d: rows_ctx.enter_context(nc.sbuf_tensor(n, s, d)))
            queries(nc, res_x, x_in, ident, halfpow, Wq, WkT, QT, ctx_in, cx, spent)
            attend(nc, ident, ones, halfpow, ctx_in, cx, ln_g, ln_b, QT, OT, Wv, Wo, sem("weights_in"), spent, spent2)
            project_out(nc, res_x, cx, OT, spent2)
        self_attention(nc, res_x, ident, halfpow, Wqkv, WoT, XG)
        comb = sb("comb", [P, TT, E], F32)
        placef, spots = sb("placef", [P, TOP, TT], F32), sb("spots", [P, MT], F32)
        xn = sb("xn", [P, TT, DIM], F32)
        route(nc, res_x, ident, ones, halfpow, Wgate, bgate, xn, share, comb, place, placef, spots, owner)
        experts(nc, res_x, ident, W1, W2, Wg, Wl, W3, Bias, b3, XG, YG, xn, share, comb, place, placef, spots,
                owner, out)


def kernel(x, ctx_1024, L0_xattn_Wq, L0_xattn_Wkv, L0_xattn_Wo, L0_xattn_ln_g, L0_xattn_ln_b, L0_attn_q_heads,
           L0_attn_k_heads, L0_attn_v_heads, L0_attn_output_proj, L0_ffn_Wgate, L0_ffn_bgate, L0_ffn_W1, L0_ffn_b1,
           L0_ffn_W2, L0_ffn_b2, L0_ffn_Wg, L0_ffn_bg, L0_ffn_Wl, L0_ffn_bl, L0_ffn_W3, L0_ffn_b3):
    import numpy as np
    import concourse.bacc as bacc
    from concourse.bass_utils import run_bass_kernel_spmd

    inner = HEADS * DH
    by_column = lambda a: np.ascontiguousarray(a.reshape(-1, P).T)
    arrays = {
        "x": x, "ctx_in": ctx_1024, "Wq": L0_xattn_Wq,
        "WkT": L0_xattn_Wkv[:, :inner].T, "Wv": L0_xattn_Wkv[:, inner:], "Wo": L0_xattn_Wo,
        "ln_g": by_column(L0_xattn_ln_g), "ln_b": by_column(L0_xattn_ln_b),
        "Wqkv": np.stack([L0_attn_q_heads.T, L0_attn_k_heads.T, L0_attn_v_heads.T]),
        "WoT": L0_attn_output_proj.T, "Wgate": L0_ffn_Wgate, "bgate": L0_ffn_bgate,
        "W1": L0_ffn_W1, "W2": L0_ffn_W2, "Wg": L0_ffn_Wg, "Wl": L0_ffn_Wl, "W3": L0_ffn_W3,
        "Bias": np.concatenate([b.reshape(E, FC, P).transpose(0, 2, 1)
                                for b in (L0_ffn_b1, L0_ffn_b2, L0_ffn_bg, L0_ffn_bl)], axis=2),
        "b3": L0_ffn_b3,
    }
    nc = bacc.Bacc("TRN2", target_bir_lowering=False, num_devices=1)
    feed, args = {}, []
    for name, a in arrays.items():
        a = np.ascontiguousarray(a)
        feed[f"in_{name}"] = a
        args.append(nc.dram_tensor(f"in_{name}", a.shape, mybir.dt.from_np(a.dtype), kind="ExternalInput").ap())
    args.append(nc.dram_tensor("out_x", (B, NQ, DIM), F32, kind="ExternalOutput").ap())
    layer(nc, *args)
    r = run_bass_kernel_spmd(nc, [feed], core_ids=[0])
    return r.results[0]["out_x"]
```
